# Optimizing a Trainium2 kernel written in Bass

```python
import numpy as np
import jax
import jax.numpy as jnp

def _softmax(x, axis=-1):
    return jax.nn.softmax(x, axis=axis)

def _gelu(x):
    return jax.nn.gelu(x, approximate=True)

def _silu(x):
    return jax.nn.silu(x)

def _sigmoid(x):
    return jax.nn.sigmoid(x)

def _layernorm(x, axis=-1, eps=1e-05):
    m = jnp.mean(x, axis=axis, keepdims=True)
    v = jnp.var(x, axis=axis, keepdims=True)
    return (x - m) / jnp.sqrt(v + eps)

def _scatter_add(tgt, idx, src, axis=0):
    return tgt.at[idx].add(src)

def _segment_sum(src, seg, n):
    return jax.ops.segment_sum(src, seg, n)
kernel_name = 'mk_macaron_d2_jaxref_r8_169124'

def setup_inputs(seed: int=0):
    np.random.seed(seed)
    _w = jnp.asarray

    def _L0_attn_setup():
        import jax, jax.numpy as jnp
        import numpy as np
        D_ATTN = 256
        D_STATE = 64
        SHIFT_FRAC = 0.5
        LN_EPS = 1e-05

        def _reference_tuple_inner(x, W_key, W_value, W_output, W_shift, gate, time_decay, time_first, ln_gamma, ln_beta):
            B, T, D = x.shape
            shift_len = max(1, int(T * SHIFT_FRAC))
            x_cat = jnp.roll(x, -shift_len, axis=1)
            g = jax.nn.sigmoid(gate)
            x_shift = jnp.einsum('btd,ed->bte', x_cat, W_shift) * g + x * (1.0 - g)
            mu = jnp.mean(x_shift, axis=-1, keepdims=True)
            var = jnp.var(x_shift, axis=-1, keepdims=True)
            x_norm = (x_shift - mu) * jax.lax.rsqrt(var + LN_EPS) * ln_gamma + ln_beta
            k = jnp.einsum('btd,sd->bts', x_norm, W_key)
            v = jnp.einsum('btd,sd->bts', x_norm, W_value)
            w = jnp.exp(time_decay)
            u = jnp.exp(time_first)
            wkv = jnp.exp(-u * jax.nn.sigmoid(k)) * v

            def step(state, wkv_t):
                state = state * w + wkv_t
                return (state, state)
            init = jnp.zeros((B, k.shape[-1]), x.dtype)
            last_state, states = jax.lax.scan(step, init, jnp.swapaxes(wkv, 0, 1))
            states = jnp.swapaxes(states, 0, 1)
            output = jnp.einsum('bts,ds->btd', states, W_output)
            return (output, jax.lax.stop_gradient(last_state))
        key = jax.random.key(seed)
        ks = jax.random.split(key, 8)
        B, T = (8, 256)
        s_attn = 1.0 / np.sqrt(D_ATTN)
        s_state = 1.0 / np.sqrt(D_STATE)
        x = jax.random.normal(ks[0], (B, T, D_ATTN), jnp.float32)
        W_key = jax.random.normal(ks[1], (D_STATE, D_ATTN), jnp.float32) * s_attn
        W_value = jax.random.normal(ks[2], (D_STATE, D_ATTN), jnp.float32) * s_attn
        W_output = jax.random.normal(ks[3], (D_ATTN, D_STATE), jnp.float32) * s_state
        W_shift = jax.random.normal(ks[4], (D_ATTN, D_ATTN), jnp.float32) * s_attn
        gate = jnp.ones((D_ATTN,), jnp.float32)
        time_decay = -jax.random.uniform(ks[5], (D_STATE,), jnp.float32, 0.05, 1.0)
        time_first = jax.random.normal(ks[6], (D_STATE,), jnp.float32) * 0.1
        ln_gamma = jnp.ones((D_ATTN,), jnp.float32)
        ln_beta = jnp.zeros((D_ATTN,), jnp.float32)
        return dict(x=x, W_key=W_key, W_value=W_value, W_output=W_output, W_shift=W_shift, gate=gate, time_decay=time_decay, time_first=time_first, ln_gamma=ln_gamma, ln_beta=ln_beta)
    _L0_attn_in = _L0_attn_setup()

    def _L0_ffn_setup():
        import jax, jax.numpy as jnp
        import numpy as np
        key = jax.random.key(seed)
        k1, k2, k3, k4, k5 = jax.random.split(key, 5)
        B, L, H, N = (2, 256, 256, 1024)
        x = jax.random.normal(k1, (B, L, H), dtype=jnp.float32)
        W0 = jax.random.normal(k2, (N, H), dtype=jnp.float32) * (1.0 / np.sqrt(H))
        bias0 = jax.random.normal(k3, (N,), dtype=jnp.float32) * 0.02
        W1 = jax.random.normal(k4, (H, N), dtype=jnp.float32) * (1.0 / np.sqrt(N))
        bias1 = jax.random.normal(k5, (H,), dtype=jnp.float32) * 0.02
        return {'x': x, 'W0': W0, 'bias0': bias0, 'W1': W1, 'bias1': bias1}
    _L0_ffn_in = _L0_ffn_setup()

    def _L1_attn_setup():
        import jax, jax.numpy as jnp
        import numpy as np
        import math
        E = 256
        H = 16
        D = E // H

        def _alibi_slopes(n):

            def pow2_slopes(n):
                start = 2 ** (-2 ** (-(math.log2(n) - 3)))
                return [start * start ** i for i in range(n)]
            if math.log2(n).is_integer():
                return pow2_slopes(n)
            c = 2 ** math.floor(math.log2(n))
            return pow2_slopes(c) + _alibi_slopes(2 * c)[::2][:n - c]

        def _alibi_bias(seq_len):
            slopes = jnp.asarray(_alibi_slopes(H), dtype=jnp.float32)
            pos = jnp.arange(seq_len)
            rel = jnp.abs(pos[None, :] - pos[:, None]).astype(jnp.float32)
            return -slopes[:, None, None] * rel[None, :, :]
        key = jax.random.key(seed)
        ks = jax.random.split(key, 5)
        B, S = (2, 256)
        scale = 1.0 / math.sqrt(E)
        x = jax.random.normal(ks[0], (B, S, E), dtype=jnp.float32)
        Wq = jax.random.normal(ks[1], (E, E), dtype=jnp.float32) * scale
        Wk = jax.random.normal(ks[2], (E, E), dtype=jnp.float32) * scale
        Wv = jax.random.normal(ks[3], (E, E), dtype=jnp.float32) * scale
        Wo = jax.random.normal(ks[4], (E, E), dtype=jnp.float32) * scale
        z = jnp.zeros((E,), dtype=jnp.float32)
        return {'x': x, 'Wq': Wq, 'bq': z, 'Wk': Wk, 'bk': z, 'Wv': Wv, 'bv': z, 'Wo': Wo, 'bo': z}
    _L1_attn_in = _L1_attn_setup()

    def _L1_ffn_setup():
        import jax, jax.numpy as jnp
        import numpy as np
        B, T, C = (2, 128, 256)
        E, TOPK = (8, 2)
        F_MOE = 176
        F_SHARED = 704
        key = jax.random.key(seed)
        ks = jax.random.split(key, 9)
        s = 0.02
        return {'x': jax.random.normal(ks[0], (B, T, C), dtype=jnp.float32), 'gate_w': jax.random.normal(ks[1], (E, C), dtype=jnp.float32) * s, 'expert_fc1': jax.random.normal(ks[2], (E, F_MOE, C), dtype=jnp.float32) * s, 'expert_fc2': jax.random.normal(ks[3], (E, F_MOE, C), dtype=jnp.float32) * s, 'expert_proj': jax.random.normal(ks[4], (E, C, F_MOE), dtype=jnp.float32) * s, 'shared_fc1': jax.random.normal(ks[5], (F_SHARED, C), dtype=jnp.float32) * s, 'shared_fc2': jax.random.normal(ks[6], (F_SHARED, C), dtype=jnp.float32) * s, 'shared_proj': jax.random.normal(ks[7], (C, F_SHARED), dtype=jnp.float32) * s, 'shared_gate_w': jax.random.normal(ks[8], (1, C), dtype=jnp.float32) * s}
    _L1_ffn_in = _L1_ffn_setup()
    _d = {'L0_attn_x': _L0_attn_in['x'], 'L0_attn_W_key': _L0_attn_in['W_key'], 'L0_attn_W_value': _L0_attn_in['W_value'], 'L0_attn_W_output': _L0_attn_in['W_output'], 'L0_attn_W_shift': _L0_attn_in['W_shift'], 'L0_attn_gate': _L0_attn_in['gate'], 'L0_attn_time_decay': _L0_attn_in['time_decay'], 'L0_attn_time_first': _L0_attn_in['time_first'], 'L0_attn_ln_gamma': _L0_attn_in['ln_gamma'], 'L0_attn_ln_beta': _L0_attn_in['ln_beta'], 'L0_ffn_W0': _L0_ffn_in['W0'], 'L0_ffn_bias0': _L0_ffn_in['bias0'], 'L0_ffn_W1': _L0_ffn_in['W1'], 'L0_ffn_bias1': _L0_ffn_in['bias1'], 'L1_attn_Wq': _L1_attn_in['Wq'], 'L1_attn_bq': _L1_attn_in['bq'], 'L1_attn_Wk': _L1_attn_in['Wk'], 'L1_attn_bk': _L1_attn_in['bk'], 'L1_attn_Wv': _L1_attn_in['Wv'], 'L1_attn_bv': _L1_attn_in['bv'], 'L1_attn_Wo': _L1_attn_in['Wo'], 'L1_attn_bo': _L1_attn_in['bo'], 'L1_ffn_gate_w': _L1_ffn_in['gate_w'], 'L1_ffn_expert_fc1': _L1_ffn_in['expert_fc1'], 'L1_ffn_expert_fc2': _L1_ffn_in['expert_fc2'], 'L1_ffn_expert_proj': _L1_ffn_in['expert_proj'], 'L1_ffn_shared_fc1': _L1_ffn_in['shared_fc1'], 'L1_ffn_shared_fc2': _L1_ffn_in['shared_fc2'], 'L1_ffn_shared_proj': _L1_ffn_in['shared_proj'], 'L1_ffn_shared_gate_w': _L1_ffn_in['shared_gate_w']}
    _x0 = _d['L0_attn_x']
    _d['L0_attn_x'] = jax.random.normal(jax.random.fold_in(jax.random.key(seed), 1), (2, 1024, 256), dtype=_x0.dtype)
    del _x0
    return _d

def reference(L0_attn_x, L0_attn_W_key, L0_attn_W_value, L0_attn_W_output, L0_attn_W_shift, L0_attn_gate, L0_attn_time_decay, L0_attn_time_first, L0_attn_ln_gamma, L0_attn_ln_beta, L0_ffn_W0, L0_ffn_bias0, L0_ffn_W1, L0_ffn_bias1, L1_attn_Wq, L1_attn_bq, L1_attn_Wk, L1_attn_bk, L1_attn_Wv, L1_attn_bv, L1_attn_Wo, L1_attn_bo, L1_ffn_gate_w, L1_ffn_expert_fc1, L1_ffn_expert_fc2, L1_ffn_expert_proj, L1_ffn_shared_fc1, L1_ffn_shared_fc2, L1_ffn_shared_proj, L1_ffn_shared_gate_w):

    def _L0_attn_ref(x, W_key, W_value, W_output, W_shift, gate, time_decay, time_first, ln_gamma, ln_beta):
        import jax, jax.numpy as jnp
        import numpy as np
        D_ATTN = 256
        D_STATE = 64
        SHIFT_FRAC = 0.5
        LN_EPS = 1e-05

        def _reference_tuple_inner(x, W_key, W_value, W_output, W_shift, gate, time_decay, time_first, ln_gamma, ln_beta):
            B, T, D = x.shape
            shift_len = max(1, int(T * SHIFT_FRAC))
            x_cat = jnp.roll(x, -shift_len, axis=1)
            g = jax.nn.sigmoid(gate)
            x_shift = jnp.einsum('btd,ed->bte', x_cat, W_shift) * g + x * (1.0 - g)
            mu = jnp.mean(x_shift, axis=-1, keepdims=True)
            var = jnp.var(x_shift, axis=-1, keepdims=True)
            x_norm = (x_shift - mu) * jax.lax.rsqrt(var + LN_EPS) * ln_gamma + ln_beta
            k = jnp.einsum('btd,sd->bts', x_norm, W_key)
            v = jnp.einsum('btd,sd->bts', x_norm, W_value)
            w = jnp.exp(time_decay)
            u = jnp.exp(time_first)
            wkv = jnp.exp(-u * jax.nn.sigmoid(k)) * v

            def step(state, wkv_t):
                state = state * w + wkv_t
                return (state, state)
            init = jnp.zeros((B, k.shape[-1]), x.dtype)
            last_state, states = jax.lax.scan(step, init, jnp.swapaxes(wkv, 0, 1))
            states = jnp.swapaxes(states, 0, 1)
            output = jnp.einsum('bts,ds->btd', states, W_output)
            return (output, jax.lax.stop_gradient(last_state))
        return _reference_tuple_inner(x, W_key, W_value, W_output, W_shift, gate, time_decay, time_first, ln_gamma, ln_beta)[0]

    def _L0_ffn_ref(x, W0, bias0, W1, bias1):
        import jax, jax.numpy as jnp
        import numpy as np
        B, L, H = x.shape
        X = x.reshape(-1, H).astype(jnp.float16)
        D = jnp.dot(X.astype(jnp.float32), W0.T) + bias0
        D = jax.nn.gelu(D, approximate=False).astype(jnp.float16)
        E = jnp.dot(D.astype(jnp.float32), W1.T) + bias1
        return E.astype(jnp.float16).reshape(B, L, H)

    def _L1_attn_ref(x, Wq, bq, Wk, bk, Wv, bv, Wo, bo):
        import jax, jax.numpy as jnp
        import numpy as np
        import math
        E = 256
        H = 16
        D = E // H

        def _alibi_slopes(n):

            def pow2_slopes(n):
                start = 2 ** (-2 ** (-(math.log2(n) - 3)))
                return [start * start ** i for i in range(n)]
            if math.log2(n).is_integer():
                return pow2_slopes(n)
            c = 2 ** math.floor(math.log2(n))
            return pow2_slopes(c) + _alibi_slopes(2 * c)[::2][:n - c]

        def _alibi_bias(seq_len):
            slopes = jnp.asarray(_alibi_slopes(H), dtype=jnp.float32)
            pos = jnp.arange(seq_len)
            rel = jnp.abs(pos[None, :] - pos[:, None]).astype(jnp.float32)
            return -slopes[:, None, None] * rel[None, :, :]
        B, S, _ = x.shape

        def proj(W, b):
            return (x @ W.T + b).reshape(B, S, H, D).transpose(0, 2, 1, 3)
        q = proj(Wq, bq)
        k = proj(Wk, bk)
        v = proj(Wv, bv)
        scores = jnp.einsum('bhqd,bhkd->bhqk', q, k) / math.sqrt(D)
        causal = jnp.triu(jnp.ones((S, S), dtype=bool), k=1)
        scores = jnp.where(causal[None, None], -jnp.inf, scores)
        scores = scores + _alibi_bias(S)[None]
        probs = jax.nn.softmax(scores, axis=-1)
        out = jnp.einsum('bhqk,bhkd->bhqd', probs, v)
        out = out.transpose(0, 2, 1, 3).reshape(B, S, E)
        return out @ Wo.T + bo

    def _L1_ffn_ref(x, gate_w, expert_fc1, expert_fc2, expert_proj, shared_fc1, shared_fc2, shared_proj, shared_gate_w):
        import jax, jax.numpy as jnp
        import numpy as np
        B, T, C = (2, 128, 256)
        E, TOPK = (8, 2)
        F_MOE = 176
        F_SHARED = 704
        b, t, c = x.shape
        xf = x.reshape(-1, c)
        n = xf.shape[0]
        router = xf @ gate_w.T
        probs = jax.nn.softmax(router.astype(jnp.float32), axis=1).astype(x.dtype)
        top_p, top_i = jax.lax.top_k(probs, TOPK)
        combine = jnp.zeros((n, E), dtype=x.dtype).at[jnp.arange(n)[:, None], top_i].set(top_p)
        h1 = jnp.einsum('nc,efc->enf', xf, expert_fc1)
        h2 = jnp.einsum('nc,efc->enf', xf, expert_fc2)
        h = jax.nn.silu(h1) * h2
        out_e = jnp.einsum('enf,ecf->enc', h, expert_proj)
        y = jnp.einsum('ne,enc->nc', combine, out_e)
        s1 = xf @ shared_fc1.T
        s2 = xf @ shared_fc2.T
        shared = jax.nn.silu(s1) * s2 @ shared_proj.T
        y = y + jax.nn.sigmoid(xf @ shared_gate_w.T) * shared
        return y.reshape(b, t, c)
    x = L0_attn_x
    x = x + 0.5 * _L0_ffn_ref(_layernorm(x, axis=-1), L0_ffn_W0, L0_ffn_bias0, L0_ffn_W1, L0_ffn_bias1)
    x = x + _L0_attn_ref(_layernorm(x, axis=-1), L0_attn_W_key, L0_attn_W_value, L0_attn_W_output, L0_attn_W_shift, L0_attn_gate, L0_attn_time_decay, L0_attn_time_first, L0_attn_ln_gamma, L0_attn_ln_beta)
    x = x + 0.5 * _L0_ffn_ref(_layernorm(x, axis=-1), L0_ffn_W0, L0_ffn_bias0, L0_ffn_W1, L0_ffn_bias1)
    x = x + 0.5 * _L1_ffn_ref(_layernorm(x, axis=-1), L1_ffn_gate_w, L1_ffn_expert_fc1, L1_ffn_expert_fc2, L1_ffn_expert_proj, L1_ffn_shared_fc1, L1_ffn_shared_fc2, L1_ffn_shared_proj, L1_ffn_shared_gate_w)
    x = x + _L1_attn_ref(_layernorm(x, axis=-1), L1_attn_Wq, L1_attn_bq, L1_attn_Wk, L1_attn_bk, L1_attn_Wv, L1_attn_bv, L1_attn_Wo, L1_attn_bo)
    x = x + 0.5 * _L1_ffn_ref(_layernorm(x, axis=-1), L1_ffn_gate_w, L1_ffn_expert_fc1, L1_ffn_expert_fc2, L1_ffn_expert_proj, L1_ffn_shared_fc1, L1_ffn_shared_fc2, L1_ffn_shared_proj, L1_ffn_shared_gate_w)
    return x

_drawn_inputs = setup_inputs


def setup_inputs(seed=0):
    import zlib

    import numpy as np

    out = dict(_drawn_inputs(seed))
    spreads = {'L0_attn_gate': (1.0, 0.2),
     'L0_attn_ln_gamma': (1.0, 0.2),
     'L0_attn_ln_beta': (0.0, 0.1),
     'L1_attn_bq': (0.0, 0.699),
     'L1_attn_bk': (0.0, 0.8),
     'L1_attn_bv': (0.0, 0.1),
     'L1_attn_bo': (0.0, 0.1)}
    factors = {'L0_ffn_bias0': 4.775,
     'L1_ffn_gate_w': 8.0,
     'L1_ffn_expert_fc1': 8.0,
     'L1_ffn_expert_fc2': 8.0,
     'L1_ffn_expert_proj': 8.0,
     'L1_ffn_shared_fc1': 7.138,
     'L1_ffn_shared_fc2': 7.075,
     'L1_ffn_shared_proj': 7.106,
     'L1_ffn_shared_gate_w': 8.0}
    for name, (base, spread) in spreads.items():
        noise = np.random.default_rng([zlib.crc32(name.encode()), seed]).standard_normal(out[name].shape)
        drawn = base * np.exp(spread * noise) if base else spread * noise
        out[name] = jnp.asarray(drawn.astype(out[name].dtype))
    for name, factor in factors.items():
        out[name] = (out[name] * factor).astype(out[name].dtype)
    return out
```

```python
from contextlib import ExitStack
import math

import numpy as np

import concourse.bass as bass
from concourse import mybir

F32, F16 = mybir.dt.float32, mybir.dt.float16
ALU, ACT, AX = mybir.AluOpType, mybir.ActivationFunctionType, mybir.AxisListType

P = 128
B, T, D = 2, 1024, 256
KD = D // P
GT = 4
GW = GT * P
NG = B * T // GW
FF = 1024
FC = FF // P
NST = 64
NE, FE, FS = 8, 176, 704
FM = NE * FE + FS
MC = -(-FM // P)
ML = FM - (MC - 1) * P
NR = NE + 1
H = 16
DH = D // H
TT = T // P
QH = 4
NQ = B * H // QH
VW = DH + 1
KR = 4 + 3 * DH
QC = T // 512
SS = 16.0
MASK = -60000.0
EPS = 1e-5

WS = 2.0 ** 8
US = 2.0 ** 4
CS = 2.0 ** 8
SEL = US / (WS * CS)

O_W0 = 0
O_W1 = O_W0 + KD * FF
O_SH = O_W1 + FC * D
O_WK = O_SH + KD * D
O_WV = O_WK + KD * NST
O_WO = O_WV + KD * NST
O_RT = O_WO + D
O_F1 = O_RT + 32
O_F2 = O_F1 + KD * FM
O_PR = O_F2 + KD * FM
O_AQ = O_PR + MC * D
O_AK = O_AQ + KD * D
O_AV = O_AK + KD * D
O_AO = O_AV + KD * D
WCOLS = O_AO + KD * D
WCH = 1000
RING = 4
SHARED = 48 * 1024
NCHUNK = WCOLS // WCH
NWG = NCHUNK // RING
assert WCOLS % WCH == 0 and NCHUNK % RING == 0

S_B0, S_LW, S_U, S_BQ, S_BK = 0, FC, FC + 1, FC + 2, FC + 4
SCOLS = FC + 6
R_B1, R_G, R_GAM, R_BET, R_BV, R_BO = range(6)


def block_kernel(nc, x_in, w_in, small_in, rows_in, ident_in, sel_in, order_in, masks_in, alibi_in, out):
    ctx = ExitStack()
    with ctx:
        def sb(name, shape, dt):
            return ctx.enter_context(nc.sbuf_tensor(name, shape, dt))

        def sem(name):
            return ctx.enter_context(nc.semaphore(name))

        shared = sb("shared", [P, SHARED // 4], F32)

        def part_of_shared():
            at = [0]

            def part(name, shape, dt):
                size = math.prod(shape[1:]) * (4 if dt is F32 else 2)
                v = shared[0:shape[0], at[0] // 4:(at[0] + size) // 4]
                at[0] += size
                assert at[0] <= SHARED, (name, at[0])
                v = v if dt is F32 else v.bitcast(dt)
                if len(shape) == 3:
                    v = v.rearrange("p (a b) -> p a b", b=shape[2])
                elif len(shape) == 4:
                    v = v.rearrange("p (a b c) -> p a b c", b=shape[2], c=shape[3])
                return v
            return part

        wkv_part, moe_part, att_part = part_of_shared(), part_of_shared(), part_of_shared()

        x = sb("x", [P, NG * GT, D], F32)
        xTh = sb("xTh", [P, KD, NG * GW], F16)
        xTl = sb("xTl", [P, KD, NG * GW], F16)
        n32 = sb("n32", [P, GT, D], F32)
        nh = sb("nh", [P, GT, D], F16)
        nl = sb("nl", [P, GT, D], F16)
        stat = sb("stat", [P, GT, 6], F32)
        mv = sb("mv", [P, GT, 2], F32)
        ve = sb("ve", [P, GT], F32)
        rstd = sb("rstd", [P, GT], F32)
        mhalf = sb("mhalf", [P, GT], F32)
        wh = sb("wh", [P, WCOLS], F16)
        wl = sb("wl", [P, WCOLS], F16)
        stage_raw = sb("stage", [P, NG * GT * D], F32)
        stage = stage_raw[:, 0:RING * WCH].rearrange("p (r c) -> p r c", r=RING)
        small = sb("small", [P, SCOLS], F32)
        rows = sb("rows", [P, 6, D], F32)
        ident = sb("ident", [P, P], F16)
        ident32 = sb("ident32", [P, P], F32)
        sel = sb("sel", [2 * NR, MC * P], F16)
        order = sb("order", [P, NE], F32)
        hT = sb("hT", [P, FC, GW], F16)
        t16 = sb("t16", [P, 2, 2 * D], F16)
        sg = moe_part("sg", [P, 2, GW], F32)
        pr = moe_part("pr", [P, 2, GW], F32)
        u32 = moe_part("u32", [P, 2, GW], F32)
        uh = moe_part("uh", [P, 2, GW], F16)
        ul = moe_part("ul", [P, 2, GW], F16)
        lg = sb("lg", [P, GT, NR], F32)
        dl = sb("dl", [P, GT, NR], F32)
        er = sb("er", [P, GT, NR], F32)
        prob = sb("prob", [P, GT, NE], F32)
        pm = sb("pm", [P, GT, NE], F32)
        m8 = sb("m8", [P, GT, NE], F32)
        s1 = sb("s1", [P, GT, NE], F32)
        s2 = sb("s2", [P, GT, NE], F32)
        mx = sb("mx", [P, GT], F32)
        comb = sb("comb", [P, GT, NR], F32)
        ch = sb("ch", [P, GT, 2 * NR], F16)
        cT = sb("cT", [2 * NR, GW], F16)
        omg = wkv_part("omg", [P, D], F32)
        gsc = wkv_part("gsc", [P, D], F32)
        eg = wkv_part("eg", [P, D], F32)
        R = wkv_part("R", [P, 2, GT, D], F32)
        z = wkv_part("z", [P, GT, D], F32)
        zn = wkv_part("zn", [P, GT, D], F32)
        zh = wkv_part("zh", [P, GT, D], F16)
        zl = wkv_part("zl", [P, GT, D], F16)
        zTh = wkv_part("zTh", [P, KD, GW], F16)
        zTl = wkv_part("zTl", [P, KD, GW], F16)
        ka = wkv_part("ka", [NST, GW], F32)
        ev = wkv_part("ev", [NST, GW], F32)
        zve = sb("zve", [P, GT], F32)
        zrstd = sb("zrstd", [P, GT], F32)
        kb = wkv_part("kb", [NST, GW], F32)
        wkv = wkv_part("wkv", [NST, GW], F32)
        decay = sb("decay", [NST, 1], F32)
        decayw = wkv_part("decayw", [NST, GW], F32)
        nu = sb("nu", [NST, 1], F32)
        st32 = wkv_part("st32", [NST, 2, GW], F32)
        sth = wkv_part("sth", [NST, 2, GW], F16)
        stl = wkv_part("stl", [NST, 2, GW], F16)

        qop = att_part("qop", [P, 2, QH, T], F16)
        kop = att_part("kop", [P, 2, QH, T], F16)
        prob_t = att_part("prob_t", [P, 2, QH * 512], F32).rearrange("p a (j c) -> p a j c", j=QH)
        rest = prob_t.rearrange("p a j c -> p (a j c)")
        p32 = rest[:, 0:2 * GW].rearrange("p (a c) -> p a c", a=2)
        psplit = rest[:, 2 * GW:4 * GW].bitcast(F16).rearrange("p (a h c) -> p a h c", a=2, h=2)
        vst = hT[:].rearrange("p a b -> p (a b)").bitcast(F32)[:, 0:GT * H * VW].rearrange(
            "p (t h c) -> p t h c", t=GT, h=H)
        vq = hT[:].rearrange("p a b -> p (a b)").bitcast(F32)[:, 0:2 * TT * QH * VW].rearrange(
            "p (a r) -> p a r", a=2)
        att = stage_raw[:].rearrange("p (t d) -> p t d", d=QH * DH)
        o32 = t16[:].rearrange("p a b -> p (a b)").bitcast(F32)
        mxs = sb("mxs", [P, QH * TT], F32)
        mneg = sb("mneg", [P, QH * TT], F16)
        mT = sb("mT", [QH * TT, 2, P], F16)
        masks = sb("masks", [P, 2, P], F16)
        rec = sb("rec", [P, GT, QH], F32)
        bq4 = sb("bq4", [P, KD], F32)

        low_banks = [ctx.enter_context(nc.psum_tensor(f"bank{i}", [P, 512], F32)) for i in range(2)]
        mid = ctx.enter_context(nc.psum_tensor("mid", [P, 4, 512], F32))
        bank = [low_banks[0][:], low_banks[1][:]] + [mid[:, i, :] for i in range(4)]
        ybank = ctx.enter_context(nc.psum_tensor("ybank", [P, 2, 512], F32))
        tp = bank[0].bitcast(F16).rearrange("p (k c) -> p k c", k=KD)
        order4 = order[:].unsqueeze(1).to_broadcast([P, GT, NE])
        tp2 = bank[1].bitcast(F16).rearrange("p (k c) -> p k c", k=KD)

        x_in_done = sem("x_in_done")
        const_done = sem("const_done")
        w_in_done = [sem(f"w_in_done{i}") for i in range(RING)]
        w_high = sem("w_high")
        w_low = sem("w_low")
        set_done = sem("set_done")
        pool_set = sem("pool_set")
        x_done = sem("x_done")
        stat_done = sem("stat_done")
        aggr_done = sem("aggr_done")
        wait_carrier = sem("wait_carrier")
        ve_done = sem("ve_done")
        rstd_done = sem("rstd_done")
        n32_done = sem("n32_done")
        nh_done = sem("nh_done")
        nl_done = sem("nl_done")
        th_ready = sem("th_ready")
        tl_ready = sem("tl_ready")
        xTh_done = sem("xTh_done")
        xTl_done = sem("xTl_done")
        h_ready = sem("h_ready")
        gelu_done = sem("gelu_done")
        y_ready = sem("y_ready")
        t16_done = sem("t16_done")
        h1_ready = sem("h1_ready")
        C_ready = sem("C_ready")
        silu_done = sem("silu_done")
        pr_done = sem("pr_done")
        u32_done = sem("u32_done")
        uh_done = sem("uh_done")
        ul_done = sem("ul_done")
        rt_ready = sem("rt_ready")
        rt_step = sem("rt_step")
        dl_done = sem("dl_done")
        er_done = sem("er_done")
        rt_sel = sem("rt_sel")
        comb_done = sem("comb_done")
        zg_done = sem("zg_done")
        wk2_step = sem("wk2_step")
        act_set = sem("act_set")
        ch_done = sem("ch_done")
        ct_ready = sem("ct_ready")
        cT_done = sem("cT_done")
        wk_set = sem("wk_set")
        R_done = sem("R_done")
        sh_ready = sem("sh_ready")
        z_read = sem("z_read")
        zn_done = sem("zn_done")
        wk_step = sem("wk_step")
        zve_done = sem("zve_done")
        zrstd_done = sem("zrstd_done")
        z_done = sem("z_done")
        zh_done = sem("zh_done")
        zl_done = sem("zl_done")
        zth_ready = sem("zth_ready")
        ztl_ready = sem("ztl_ready")
        zTh_done = sem("zTh_done")
        zTl_done = sem("zTl_done")
        kv_ready = sem("kv_ready")
        ek_done = sem("ek_done")
        sig_done = sem("sig_done")
        ev_done = sem("ev_done")
        st_done = sem("st_done")
        sth_done = sem("sth_done")
        stl_done = sem("stl_done")
        out_done = sem("out_done")
        bq_done = sem("bq_done")
        qk_ready = sem("qk_ready")
        p32_done = sem("p32_done")
        ph_done = sem("ph_done")
        pl_done = sem("pl_done")
        v_ready = sem("v_ready")
        v_done = sem("v_done")
        scratch_done = [sem(f"scratch_done{i}") for i in range(2)]
        vscratch_done = sem("vscratch_done")
        ones_in = sem("ones_in")
        op_in = [sem(f"op_in{i}") for i in range(2)]
        m_in = [sem(f"m_in{i}") for i in range(2)]
        s_ready = sem("s_ready")
        mx_done = sem("mx_done")
        mneg_done = sem("mneg_done")
        mt_ready = sem("mt_ready")
        mT_done = sem("mT_done")
        st_ready = sem("st_ready")
        exp_done = sem("exp_done")
        pv_done = sem("pv_done")
        o32_done = sem("o32_done")
        ot_ready = sem("ot_ready")
        rec_done = sem("rec_done")
        att_done = sem("att_done")
        ah_done = sem("ah_done")
        al_done = sem("al_done")
        ath_ready = sem("ath_ready")
        atl_ready = sem("atl_ready")
        aTh_done = sem("aTh_done")
        aTl_done = sem("aTl_done")
        ob_done = sem("ob_done")
        qs_dram = nc.dram_tensor("scratch_q", [2, B * D, T], F16).ap()
        ks_dram = nc.dram_tensor("scratch_k", [2, B * D, T], F16).ap()
        vs_dram = nc.dram_tensor("scratch_v", [NQ, T, QH * VW], F32).ap()

        RT_STEPS = 16

        def tokens(g, t=0, n=GW):
            return bass.ds(g * GW + t * P, n)

        def tiles(g, t=0, n=GT):
            return bass.ds(g * GT + t, n)

        def W(parts, col, n, rows_=P):
            return parts[0:rows_, col:col + n]

        def row(i, n):
            return rows[:, i:i + 1, :].to_broadcast([P, n, D])

        def pe_transpose_high(pe, n):
            pe.wait_ge(nh_done, n + 1)
            for t in range(GT):
                for k in range(KD):
                    last = nc.tensor.transpose(tp[:, k, t * P:(t + 1) * P], nh[:, t, k * P:(k + 1) * P], ident[:])
            last.then_inc(th_ready, 1)

        def pe_transpose_low(pe, n, ns):
            pe.wait_ge(nl_done, ns + 1)
            pe.wait_ge(xTh_done, n + 1)
            for t in range(GT):
                for k in range(KD):
                    last = nc.tensor.transpose(tp[:, k, t * P:(t + 1) * P], nl[:, t, k * P:(k + 1) * P], ident[:])
            last.then_inc(tl_ready, 1)

        def pe_router(pe, ns, g):
            pe.wait_ge(xTl_done, ns + 1)
            for t in range(GT):
                for i, (xs, ws) in enumerate(((xTh, wh), (xTh, wl), (xTl, wh))):
                    for k in range(KD):
                        last = nc.tensor.matmul(bank[0][:, t * NR:(t + 1) * NR], xs[:, k, tokens(g, t, P)],
                                                W(ws, O_RT + k * NR, NR), start=(i == 0 and k == 0),
                                                stop=(i == 2 and k == KD - 1))
            last.then_inc(rt_ready, 1)

        def pe_transpose_routes(pe, m):
            pe.wait_ge(ch_done, m + 1)
            for t in range(GT):
                last = nc.tensor.transpose(tp[0:2 * NR, 0, t * P:(t + 1) * P], ch[:, t, :], ident[:])
            last.then_inc(ct_ready, 1)

        def pe_ffn(pe, n, f, g, steps):
            pe.wait_ge(xTh_done, n + 1)

            def hidden(c):
                for k in range(KD):
                    for i, ws in enumerate((wh, wl)):
                        last = nc.tensor.matmul(bank[2 + c % 4], W(ws, O_W0 + k * FF + c * P, P),
                                                xTh[:, k, tokens(g)], start=(k == 0 and i == 0),
                                                stop=(k == KD - 1 and i == 1))
                last.then_inc(h_ready, 1)

            def project(c):
                pe.wait_ge(gelu_done, FC * f + c + 1)
                if c == 0:
                    pe.wait_ge(x_done, n + 1)
                    pe.wait_ge(w_low, 5)
                for t in range(GT):
                    for i, ws in enumerate((wh, wl)):
                        last = nc.tensor.matmul(ybank[:, t // 2, (t % 2) * D:(t % 2 + 1) * D],
                                                hT[:, c, t * P:(t + 1) * P], W(ws, O_W1 + c * D, D),
                                                start=(c == 0 and i == 0 and t % 2 == 0),
                                                stop=(c == FC - 1 and i == 1), skip_group_check=True)
                if c == FC - 1:
                    last.then_inc(y_ready, 1)

            for c in range(FC):
                hidden(c)
                if c >= 2:
                    project(c - 2)
                for step in steps.get(c, ()):
                    step(pe)
            project(FC - 2)
            project(FC - 1)

        def pe_moe(pe, n, ns, m, g, steps):
            def hidden(c):
                rows_ = P if c < MC - 1 else ML
                for off, bk in ((O_F1, bank[2 + c % 2]), (O_F2, bank[4 + c % 2])):
                    for k in range(KD):
                        for i, (ws, xs) in enumerate(((wh, xTh), (wh, xTl), (wl, xTh))):
                            last = nc.tensor.matmul(bk[0:rows_, :], W(ws, off + k * FM + c * P, rows_),
                                                    xs[:, k, tokens(g)], start=(k == 0 and i == 0),
                                                    stop=(k == KD - 1 and i == 2))
                    if off == O_F1:
                        last.then_inc(h1_ready, 1)
                if c >= 1:
                    pe.wait_ge(u32_done, MC * m + c)
                nc.tensor.matmul(bank[1][0:rows_, :], sel[:, c * P:c * P + rows_], cT[:],
                                 start=True, stop=True).then_inc(C_ready, 1)

            def project(c):
                rows_ = P if c < MC - 1 else ML
                pe.wait_ge(ul_done, MC * m + c + 1)
                if c == 0:
                    pe.wait_ge(x_done, n + 1)
                for t in range(GT):
                    for i, (us, ws) in enumerate(((uh, wh), (uh, wl), (ul, wh))):
                        last = nc.tensor.matmul(ybank[:, t // 2, (t % 2) * D:(t % 2 + 1) * D],
                                                us[0:rows_, c % 2, t * P:(t + 1) * P],
                                                W(ws, O_PR + c * D, D, rows_),
                                                start=(c == 0 and i == 0 and t % 2 == 0),
                                                stop=(c == MC - 1 and i == 2), skip_group_check=True)
                if c == MC - 1:
                    last.then_inc(y_ready, 1)

            pe.wait_ge(xTh_done, n + 1)
            pe.wait_ge(xTl_done, ns + 1)
            pe.wait_ge(cT_done, m + 1)
            for c in range(MC):
                hidden(c)
                if c >= 1:
                    project(c - 1)
                for step in steps.get(c, ()):
                    step(pe)
            project(MC - 1)

        def pe_wkv(pe, n, ns, q, b):
            pe.wait_ge(xTh_done, n + 2)
            pe.wait_ge(xTl_done, ns + 2)
            for j in range(2):
                if j == 0:
                    pe.wait_ge(x_done, n + 1)
                else:
                    pe.wait_ge(z_read, q + 1)
                for t in range(GT):
                    for i, (xs, ws) in enumerate(((xTh, wh), (xTh, wl), (xTl, wh))):
                        for k in range(KD):
                            last = nc.tensor.matmul(ybank[:, t // 2, (t % 2) * D:(t % 2 + 1) * D],
                                                    xs[:, k, bass.ds((2 * b + 1 - j) * GW + t * P, P)],
                                                    W(ws, O_SH + k * D, D),
                                                    start=(i == 0 and k == 0), stop=(i == 2 and k == KD - 1))
                last.then_inc(sh_ready, 1)
            for j in range(2):
                pe.wait_ge(zh_done, q + j + 1)
                for t in range(GT):
                    for k in range(KD):
                        last = nc.tensor.transpose(tp2[:, k, t * P:(t + 1) * P], zh[:, t, k * P:(k + 1) * P], ident[:])
                last.then_inc(zth_ready, 1)
                pe.wait_ge(zl_done, q + j + 1)
                pe.wait_ge(zTh_done, q + j + 1)
                for t in range(GT):
                    for k in range(KD):
                        last = nc.tensor.transpose(tp2[:, k, t * P:(t + 1) * P], zl[:, t, k * P:(k + 1) * P], ident[:])
                last.then_inc(ztl_ready, 1)
                pe.wait_ge(zTl_done, q + j + 1)
                for off, bk in ((O_WK, bank[2 + j]), (O_WV, bank[4 + j])):
                    for k in range(KD):
                        for i, (ws, zs) in enumerate(((wh, zTh), (wh, zTl), (wl, zTh))):
                            last = nc.tensor.matmul(bk[0:NST, :], W(ws, off + k * NST, NST), zs[:, k, :],
                                                    start=(k == 0 and i == 0), stop=(k == KD - 1 and i == 2))
                last.then_inc(kv_ready, 1)
            for j in range(2):
                pe.wait_ge(stl_done, q + j + 1)
                if j == 1:
                    pe.wait_ge(x_done, n + 2)
                for t in range(GT):
                    for i, (ss, ws) in enumerate(((sth, wh), (sth, wl), (stl, wh))):
                        last = nc.tensor.matmul(ybank[:, t // 2, (t % 2) * D:(t % 2 + 1) * D],
                                                ss[:, j, t * P:(t + 1) * P], W(ws, O_WO, D, NST),
                                                start=(i == 0), stop=(i == 2))
                last.then_inc(y_ready, 1)

        def act_round(act, n):
            act.wait_ge(n32_done, n + 1)
            if not isinstance(n, int) or n:
                act.wait_ge(th_ready, n)
            nc.scalar.copy(nh[:], n32[:]).then_inc(nh_done, 1)

        def act_high_out(act, n, g):
            act.wait_ge(th_ready, n + 1)
            nc.scalar.copy(xTh[:, :, tokens(g)], tp).then_inc(xTh_done, 1)

        def act_exp_routes(act, m):
            act.wait_ge(dl_done, m + 1)
            nc.scalar.activation(er[:], dl[:], ACT.Exp).then_inc(er_done, 1)

        def act_routes_out(act, m):
            act.wait_ge(ct_ready, m + 1)
            nc.scalar.copy(cT[:], tp[0:2 * NR, 0, :]).then_inc(cT_done, 1)

        def act_weights(act, r):
            for j in range(RING):
                act.wait_ge(w_in_done[j], 16 * (r + 1))
                nc.scalar.activation(wh[:, bass.ds((RING * r + j) * WCH, WCH)], stage[:, j, :], ACT.Copy,
                                     scale=WS).then_inc(w_high, 1)

        def act_ffn(act, f, steps):
            for c in range(FC):
                act.wait_ge(h_ready, FC * f + c + 1)
                nc.scalar.activation(hT[:, c, :], bank[2 + c % 4], ACT.Gelu, bias=small[:, S_B0 + c:S_B0 + c + 1],
                                     scale=1 / WS).then_inc(gelu_done, 1)
                for step in steps.get(c, ()):
                    step(act)

        def act_moe(act, m, steps):
            for c in range(MC):
                rows_ = P if c < MC - 1 else ML
                act.wait_ge(h1_ready, MC * m + c + 1)
                nc.scalar.activation(sg[0:rows_, c % 2, :], bank[2 + c % 2][0:rows_, :], ACT.Silu,
                                     scale=1 / WS).then_inc(silu_done, 1)
                act.wait_ge(u32_done, MC * m + c + 1)
                nc.scalar.copy(uh[0:rows_, c % 2, :], u32[0:rows_, c % 2, :]).then_inc(uh_done, 1)
                for step in steps.get(c, ()):
                    step(act)

        def act_wkv(act, q):
            for j in range(2):
                act.wait_ge(zn_done, q + j + 1)
                if j == 1:
                    act.wait_ge(zth_ready, q + 1)
                nc.scalar.copy(zh[:], zn[:]).then_inc(zh_done, 1)
                act.wait_ge(zth_ready, q + j + 1)
                if j == 1:
                    act.wait_ge(kv_ready, q + 1)
                nc.scalar.copy(zTh[:], tp2).then_inc(zTh_done, 1)
            for j in range(2):
                act.wait_ge(kv_ready, q + j + 1)
                nc.scalar.activation(ka[:], bank[2 + j][0:NST, :], ACT.Exp, scale=-1 / WS).then_inc(ek_done, 1)
                act.wait_ge(sig_done, q + j + 1)
                nc.scalar.activation(ev[:], kb[:], ACT.Exp, scale=nu[:]).then_inc(ev_done, 1)
                act.wait_ge(st_done, q + j + 1)
                nc.scalar.copy(sth[:, j, :], st32[:, j, :]).then_inc(sth_done, 1)

        def dve_normalise(dve, n, g, first=False):
            dve_moments(dve, n, g, first)
            dve_scale(dve, n, g)

        def dve_moments(dve, n, g, first=False):
            dve.wait_ge(x_done, 1 if first else n - 2)
            for t in range(GT):
                last = nc.vector.bn_stats(stat[:, t, :], x[:, tiles(g, t, 1), :])
            last.then_inc(stat_done, 1)
            dve.wait_ge(stat_done, n + 1)
            dve.sem_inc(wait_carrier, 1)
            for t in range(GT):
                last = nc.vector.bn_aggr(mv[:, t, :], stat[:, t, :])
            last.then_inc(aggr_done, 1)
            dve.wait_ge(aggr_done, n + 1)
            nc.vector.tensor_scalar(ve[:], mv[:, :, 1], EPS, None, ALU.add).then_inc(ve_done, 1)

        def dve_scale(dve, n, g):
            dve.wait_ge(rstd_done, n + 1)
            if not isinstance(n, int) or n:
                dve.wait_ge(nh_done, n)
            for t in range(GT):
                last = nc.vector.tensor_scalar(n32[:, t, :], x[:, tiles(g, t, 1), :], mv[:, t, 0:1], rstd[:, t:t + 1],
                                               ALU.subtract, ALU.mult)
            last.then_inc(n32_done, 1)

        def dve_low(dve, n, ns):
            dve.wait_ge(nh_done, n + 1)
            if not isinstance(ns, int) or ns:
                dve.wait_ge(tl_ready, ns)
            nc.vector.tensor_tensor(nl[:], n32[:], nh[:], ALU.subtract).then_inc(nl_done, 1)

        def dve_low_out(dve, ns, g):
            dve.wait_ge(tl_ready, ns + 1)
            nc.vector.tensor_copy(xTl[:, :, tokens(g)], tp).then_inc(xTl_done, 1)

        def dve_skip(dve, n, j):
            dve.wait_ge(n32_done, n + 1)
            nc.vector.tensor_tensor(R[:, j, :, :], n32[:], omg[:].unsqueeze(1).to_broadcast([P, GT, D]),
                                    ALU.mult).then_inc(R_done, 1)

        def dve_routes(dve, m):
            at = [0]

            def step(ins):
                at[0] += 1
                ins.then_inc(rt_step, 1)
                dve.wait_ge(rt_step, RT_STEPS * m + at[0])

            def wide(v, n=NE):
                return v.unsqueeze(2).to_broadcast([P, GT, n])

            dve.wait_ge(rt_ready, m + 1)
            step(nc.vector.tensor_scalar(lg[:], bank[0][:, 0:GT * NR].rearrange("p (t r) -> p t r", r=NR), 1 / WS,
                                         None, ALU.mult))
            step(nc.vector.tensor_reduce(mx[:], lg[:, :, 0:NE], AX.X, ALU.max))
            step(nc.vector.tensor_scalar(dl[:, :, NE:NR], lg[:, :, NE:NR], -1.0, None, ALU.mult))
            nc.vector.tensor_tensor(dl[:, :, 0:NE], lg[:, :, 0:NE], wide(mx[:]), ALU.subtract).then_inc(dl_done, 1)
            dve.wait_ge(er_done, m + 1)
            step(nc.vector.tensor_reduce(mx[:], er[:, :, 0:NE], AX.X, ALU.add))
            step(nc.vector.reciprocal(mx[:], mx[:]))
            step(nc.vector.tensor_tensor(prob[:], er[:, :, 0:NE], wide(mx[:]), ALU.mult))
            step(nc.vector.tensor_reduce(mx[:], prob[:], AX.X, ALU.max))
            step(nc.vector.tensor_tensor(s1[:], prob[:], wide(mx[:]), ALU.is_equal))
            step(nc.vector.tensor_tensor(pm[:], s1[:], order4, ALU.mult))
            step(nc.vector.tensor_reduce(mx[:], pm[:], AX.X, ALU.max))
            step(nc.vector.tensor_tensor(s1[:], pm[:], wide(mx[:]), ALU.is_equal))
            step(nc.vector.scalar_tensor_tensor(pm[:], s1[:], -2.0, prob[:], ALU.mult, ALU.add))
            step(nc.vector.tensor_reduce(mx[:], pm[:], AX.X, ALU.max))
            step(nc.vector.tensor_tensor(s2[:], pm[:], wide(mx[:]), ALU.is_equal))
            step(nc.vector.tensor_tensor(s2[:], s2[:], order4, ALU.mult))
            step(nc.vector.tensor_reduce(mx[:], s2[:], AX.X, ALU.max))
            assert at[0] == RT_STEPS
            nc.vector.tensor_tensor(s2[:], s2[:], wide(mx[:]), ALU.is_equal).then_inc(rt_sel, 1)
            dve.wait_ge(rt_sel, 4 * m + 1)
            nc.vector.tensor_tensor(s1[:], s1[:], s2[:], ALU.add).then_inc(rt_sel, 1)
            nc.vector.tensor_scalar(comb[:, :, NE:NR], er[:, :, NE:NR], 1.0, None, ALU.add).then_inc(rt_sel, 1)
            dve.wait_ge(rt_sel, 4 * m + 3)
            nc.vector.scalar_tensor_tensor(comb[:, :, 0:NE], s1[:], CS, prob[:], ALU.mult, ALU.mult)
            nc.vector.reciprocal(er[:, :, NE:NR], comb[:, :, NE:NR]).then_inc(rt_sel, 1)
            dve.wait_ge(rt_sel, 4 * m + 4)
            nc.vector.tensor_scalar(comb[:, :, NE:NR], er[:, :, NE:NR], CS, None, ALU.mult).then_inc(comb_done, 1)
            dve.wait_ge(comb_done, 2 * m + 1)
            if not isinstance(m, int) or m:
                dve.wait_ge(ct_ready, m)
            nc.vector.tensor_copy(ch[:, :, 0:NR], comb[:]).then_inc(comb_done, 1)
            dve.wait_ge(comb_done, 2 * m + 2)
            nc.vector.tensor_tensor(ch[:, :, NR:2 * NR], comb[:], ch[:, :, 0:NR], ALU.subtract).then_inc(ch_done, 1)

        def dve_weights(dve, r):
            for j in range(RING):
                dve.wait_ge(w_high, RING * r + j + 1)
                c = bass.ds((RING * r + j) * WCH, WCH)
                nc.vector.scalar_tensor_tensor(wl[:, c], stage[:, j, :], WS, wh[:, c], ALU.mult,
                                               ALU.subtract).then_inc(w_low, 1)

        def dve_ffn_sum(dve, n, f, g):
            dve.wait_ge(y_ready, n + 1)
            for h in range(2):
                nc.vector.scalar_tensor_tensor(t16[:, h, :].rearrange("p (t d) -> p t d", t=2),
                                               ybank[:, h, :].rearrange("p (t d) -> p t d", t=2), 1 / WS,
                                               row(R_B1, 2), ALU.mult, ALU.add).then_inc(t16_done, 1)
            for h in range(2):
                dve.wait_ge(t16_done, 2 * f + h + 1)
                xs = x[:, tiles(g, 2 * h, 2), :]
                last = nc.vector.scalar_tensor_tensor(xs, t16[:, h, :].rearrange("p (t d) -> p t d", t=2), 0.5, xs,
                                                      ALU.mult, ALU.add)
            last.then_inc(x_done, 1)

        def dve_sum(dve, n, g, factor):
            dve.wait_ge(y_ready, n + 1)
            for h in range(2):
                xs = x[:, tiles(g, 2 * h, 2), :]
                last = nc.vector.scalar_tensor_tensor(xs, ybank[:, h, :].rearrange("p (t d) -> p t d", t=2), factor, xs,
                                                      ALU.mult, ALU.add)
            last.then_inc(x_done, 1)

        def dve_moe(dve, m, steps):
            for c in range(MC):
                rows_ = P if c < MC - 1 else ML
                dve.wait_ge(silu_done, MC * m + c + 1)
                dve.wait_ge(C_ready, MC * m + c + 1)
                nc.vector.tensor_tensor(pr[0:rows_, c % 2, :], bank[4 + c % 2][0:rows_, :], sg[0:rows_, c % 2, :],
                                        ALU.mult).then_inc(pr_done, 1)
                dve.wait_ge(pr_done, MC * m + c + 1)
                nc.vector.tensor_tensor(u32[0:rows_, c % 2, :], bank[1][0:rows_, :], pr[0:rows_, c % 2, :],
                                        ALU.mult).then_inc(u32_done, 1)
                for step in steps.get(c, ()):
                    step(dve)

        def dve_wkv(dve, n, q, b):
            for j in range(2):
                dve.wait_ge(sh_ready, q + j + 1)
                for h in range(2):
                    last = nc.vector.tensor_tensor(z[:, 2 * h:2 * h + 2, :],
                                                   ybank[:, h, :].rearrange("p (t d) -> p t d", t=2),
                                                   gsc[:].unsqueeze(1).to_broadcast([P, 2, D]), ALU.mult)
                last.then_inc(z_read, 1)
                dve.wait_ge(z_read, q + j + 1)
                nc.vector.tensor_tensor(z[:], z[:], R[:, j, :, :], ALU.add).then_inc(wk_step, 1)
                dve.wait_ge(wk_step, 3 * (q + j) + 1)
                for t in range(GT):
                    last = nc.vector.bn_stats(stat[:, t, :], z[:, t, :])
                last.then_inc(wk_step, 1)
                dve.wait_ge(wk_step, 3 * (q + j) + 2)
                dve.sem_inc(wait_carrier, 1)
                for t in range(GT):
                    last = nc.vector.bn_aggr(mv[:, t, :], stat[:, t, :])
                last.then_inc(wk_step, 1)
                dve.wait_ge(wk_step, 3 * (q + j) + 3)
                nc.vector.tensor_scalar(zve[:], mv[:, :, 1], EPS, None, ALU.add).then_inc(zve_done, 1)
                for t in range(GT):
                    last = nc.vector.scalar_tensor_tensor(z[:, t, :], z[:, t, :], mv[:, t, 0:1], rows[:, R_GAM, :],
                                                          ALU.subtract, ALU.mult)
                last.then_inc(zg_done, 1)
                dve.wait_ge(zg_done, q + j + 1)
                dve.wait_ge(zrstd_done, q + j + 1)
                if j == 1:
                    dve.wait_ge(zh_done, q + 1)
                for t in range(GT):
                    last = nc.vector.scalar_tensor_tensor(zn[:, t, :], z[:, t, :], zrstd[:, t:t + 1], rows[:, R_BET, :],
                                                          ALU.mult, ALU.add)
                last.then_inc(zn_done, 1)
                dve.wait_ge(zh_done, q + j + 1)
                if j == 1:
                    dve.wait_ge(ztl_ready, q + 1)
                nc.vector.tensor_tensor(zl[:], zn[:], zh[:], ALU.subtract).then_inc(zl_done, 1)
                dve.wait_ge(ztl_ready, q + j + 1)
                if j == 1:
                    dve.wait_ge(kv_ready, q + 1)
                nc.vector.tensor_copy(zTl[:], tp2).then_inc(zTl_done, 1)
            for j in range(2):
                dve.wait_ge(ek_done, q + j + 1)
                nc.vector.tensor_scalar(kb[:], ka[:], 1.0, None, ALU.add).then_inc(wk2_step, 1)
                dve.wait_ge(wk2_step, 2 * (q + j) + 1)
                nc.vector.reciprocal(kb[:], kb[:]).then_inc(sig_done, 1)
                dve.wait_ge(ev_done, q + j + 1)
                nc.vector.scalar_tensor_tensor(wkv[:], bank[4 + j][0:NST, :], 1 / WS, ev[:], ALU.mult,
                                               ALU.mult).then_inc(wk2_step, 1)
                dve.wait_ge(wk2_step, 2 * (q + j) + 2)
                nc.vector.tensor_tensor_scan(st32[:, j, :], decayw[:], wkv[:],
                                             0.0 if j == 0 else st32[:, 0, GW - 1:GW], ALU.mult,
                                             ALU.add).then_inc(st_done, 1)
                dve.wait_ge(sth_done, q + j + 1)
                nc.vector.tensor_tensor(stl[:, j, :], st32[:, j, :], sth[:, j, :], ALU.subtract).then_inc(stl_done, 1)
            for j in range(2):
                dve_sum(dve, n + j, 2 * b + j, 1 / WS)

        def pool_root(pool, n, src, dst, src_done, dst_done):
            pool.wait_ge(src_done, n + 1)
            nc.gpsimd.tensor_tensor(dst[:], src[:], mhalf[:], ALU.pow).then_inc(dst_done, 1)

        def pool_moe(pool, m, steps):
            for c in range(MC):
                rows_ = P if c < MC - 1 else ML
                pool.wait_ge(uh_done, MC * m + c + 1)
                nc.gpsimd.tensor_tensor(ul[0:rows_, c % 2, :], u32[0:rows_, c % 2, :], uh[0:rows_, c % 2, :],
                                        ALU.subtract).then_inc(ul_done, 1)
                for step in steps.get(c, ()):
                    step(pool)


        STEPS = [(qc, kt) for qc in range(QC) for kt in range(4 * (qc + 1))]
        NS = len(STEPS)
        MU = QH * TT
        M_AT = [round(MU * min(1.0, s / (NS - 2))) for s in range(NS + 1)]
        IN_DMAS = 9

        def span(s):
            qc, kt = STEPS[s]
            return max(0, kt * P - qc * 512)

        def pe_qkv(pe, n, ns, a, g):
            pe.wait_ge(xTh_done, n + 1)
            pe.wait_ge(xTl_done, ns + 1)
            for i, off in enumerate((O_AQ, O_AK)):
                for m in range(KD):
                    o = 2 * i + m
                    if o >= 2:
                        pe.wait_ge(p32_done, 4 * a + o - 1)
                    for k in range(KD):
                        for j, (ws, xs) in enumerate(((wh, xTh), (wh, xTl), (wl, xTh))):
                            last = nc.tensor.matmul(bank[2 + o % 2], W(ws, off + k * D + m * P, P),
                                                    xs[:, k, tokens(g)], start=(k == 0 and j == 0),
                                                    stop=(k == KD - 1 and j == 2))
                    last.then_inc(qk_ready, 1)
            pe.wait_ge(p32_done, 4 * a + 4)
            pe.wait_ge(v_done, a + 1)
            for t in range(GT):
                for j, (xs, ws) in enumerate(((xTh, wh), (xTh, wl), (xTl, wh))):
                    for k in range(KD):
                        last = nc.tensor.matmul(ybank[:, t // 2, (t % 2) * D:(t % 2 + 1) * D], xs[:, k, tokens(g, t, P)],
                                                W(ws, O_AV + k * D, D), start=(j == 0 and k == 0),
                                                stop=(j == 2 and k == KD - 1))
            last.then_inc(v_ready, 1)

        def act_qkv(act, a):
            for o in range(4):
                act.wait_ge(qk_ready, 4 * a + o + 1)
                act.wait_ge(pl_done, 4 * a + o + 1)
                q = o < 2
                m = o % 2
                nc.scalar.activation(p32[:, o % 2, :], bank[2 + o % 2], ACT.Identity,
                                     bias=bq4[:, m:m + 1] if q else small[:, S_BK + m:S_BK + m + 1],
                                     scale=SS / math.sqrt(DH) / WS if q else 1 / WS).then_inc(p32_done, 1)
                act.wait_ge(p32_done, 4 * a + o + 1)
                act.wait_ge(scratch_done[o % 2], 32 * (2 * a + o // 2 + 1))
                nc.scalar.copy(psplit[:, o % 2, 0, :], p32[:, o % 2, :]).then_inc(ph_done, 1)

        def dve_qkv(dve, a):
            for o in range(4):
                dve.wait_ge(ph_done, 4 * a + o + 1)
                nc.vector.tensor_tensor(psplit[:, o % 2, 1, :], p32[:, o % 2, :], psplit[:, o % 2, 0, :],
                                        ALU.subtract).then_inc(pl_done, 1)
            dve.wait_ge(v_ready, a + 1)
            dve.wait_ge(vscratch_done, 64 * (a + 1))
            for t in range(GT):
                last = nc.vector.scalar_tensor_tensor(
                    vst[:, t, :, 0:DH], ybank[:, t // 2, (t % 2) * D:(t % 2 + 1) * D].rearrange("p (h c) -> p h c", h=H),
                    1 / WS, rows[:, R_BV, :].rearrange("p (h c) -> p h c", h=H), ALU.mult, ALU.add)
            last.then_inc(v_done, 1)

        def sp_qkv(sp, a, b, j):
            for o in range(4):
                dst = qs_dram if o < 2 else ks_dram
                for part, done in ((0, ph_done), (1, pl_done)):
                    sp.wait_ge(done, 4 * a + o + 1 + 2 * part)
                    sp.dma_start(dst[part, bass.ds(b * D + (o % 2) * P, P), j * GW:(j + 1) * GW],
                                 psplit[:, o % 2, part, :]).then_inc(scratch_done[o % 2], 16)
            sp.wait_ge(v_done, a + 2)
            for quad in range(H // QH):
                dst = vs_dram[bass.ds(b * (H // QH) + quad, 1), j * GW:(j + 1) * GW, :]
                sp.dma_start(dst.rearrange("u (t p) c -> p (u t) c", p=P),
                             vst[:, :, quad * QH:(quad + 1) * QH, :].rearrange("p t h c -> p t (h c)")
                             ).then_inc(vscratch_done, 16)

        def sp_operands(sp, u, par):
            for c, (op, src, parts) in enumerate(((qop, qs_dram, (0, 1, 0)), (kop, ks_dram, (0, 0, 1)))):
                sp.dma_start(op[0:4, par, :, :], alibi_in[c, 0:4, bass.ds(u * QH, QH), :]).then_inc(op_in[par], 16)
                for i, part in enumerate(parts):
                    sp.dma_start(op[4 + i * DH:4 + (i + 1) * DH, par, :, :],
                                 src[part, bass.ds(u * QH * DH, QH * DH), :].rearrange("(j d) n -> d j n", d=DH)
                                 ).then_inc(op_in[par], 16)
            sp.dma_start(vq[:, par, :].rearrange("p (t c) -> p t c", t=TT),
                         vs_dram[bass.ds(u, 1), :, :].rearrange("u (t p) c -> p (u t) c", p=P)).then_inc(op_in[par], 16)

        def pe_max_block(pe, u, par, v):
            j, qt = v // TT, v % TT
            pe.wait_ge(mx_done, MU * u + v + 1)
            dst = mid[:, 2 * (v % 2):2 * (v % 2) + 2, :]
            n = (qt + 1) * P
            for k0 in range(0, n, 512):
                w = min(512, n - k0)
                nc.tensor.matmul(dst[:, k0 // 512, 0:w], qop[0:KR, par, j, qt * P:(qt + 1) * P],
                                 kop[0:KR, par, j, k0:k0 + w], start=True, stop=False, skip_group_check=True)
            nc.tensor.matmul(dst[:, qt // 4, (qt % 4) * P:(qt % 4 + 1) * P], ident[:], masks[:, 0, :],
                             start=False, stop=True, skip_group_check=True).then_inc(s_ready, 1)

        def dve_max_block(dve, u, v):
            qt = v % TT
            dve.wait_ge(s_ready, MU * u + v + 1)
            flat = mid[:, 2 * (v % 2):2 * (v % 2) + 2, :].rearrange("p a b -> p (a b)")
            nc.vector.tensor_reduce(mxs[:, v:v + 1], flat[:, 0:(qt + 1) * P], AX.X, ALU.max).then_inc(mx_done, 1)

        def dve_max_end(dve, u):
            dve.wait_ge(mx_done, MU * (u + 1) + 2)
            if not isinstance(u, int) or u:
                dve.wait_ge(mt_ready, u)
            nc.vector.tensor_scalar(mneg[:], mxs[:], -1.0, None, ALU.mult).then_inc(mneg_done, 1)

        def pe_max_end(pe, u):
            pe.wait_ge(mneg_done, u + 1)
            if not isinstance(u, int) or u:
                pe.wait_ge(att_done, 2 * u - 1)
            nc.tensor.transpose(ybank[0:MU, 1, 0:P // 2].bitcast(F16), mneg[:], ident[:]).then_inc(mt_ready, 1)

        def act_max_end(act, u, par):
            act.wait_ge(mt_ready, u + 1)
            nc.scalar.copy(mT[:, par, :], ybank[0:MU, 1, 0:P // 2].bitcast(F16)).then_inc(mT_done, 1)

        def sp_max_row(sp, u, par):
            sp.wait_ge(mT_done, u + 1)
            sp.dma_start(qop[KR:KR + 1, par, :, :].rearrange("p j n -> p (j n)"), mT[:, par, :]).then_inc(m_in[par], 16)

        def pe_scores(pe, u, par, s):
            qc, kt = STEPS[s]
            c0 = span(s)
            for j in range(QH):
                e = QH * s + j
                pe.wait_ge(exp_done, QH * NS * u + e + 1)
                diag = kt >= 4 * qc
                last = nc.tensor.matmul(bank[e % 2][:, c0:512], kop[0:KR + 1, par, j, kt * P:(kt + 1) * P],
                                        qop[0:KR + 1, par, j, qc * 512 + c0:(qc + 1) * 512], start=True, stop=not diag,
                                        skip_group_check=True)
                if diag:
                    last = nc.tensor.matmul(bank[e % 2][:, c0:c0 + P], ident[:], masks[:, 1, :], start=False, stop=True,
                                            skip_group_check=True)
                last.then_inc(st_ready, 1)

        def act_exp(act, u, s):
            c0 = span(s)
            act.wait_ge(pv_done, NS * u + s + 1)
            for j in range(QH):
                e = QH * s + j
                act.wait_ge(st_ready, QH * NS * u + e + 1)
                nc.scalar.activation(prob_t[:, s % 2, j, c0:512], bank[e % 2][:, c0:512], ACT.Exp,
                                     scale=1 / SS).then_inc(exp_done, 1)

        def pe_values(pe, u, par, s):
            qc, kt = STEPS[s]
            c0 = span(s)
            pe.wait_ge(exp_done, QH * NS * u + QH * (s + 1) + 2)
            for j in range(QH):
                last = nc.tensor.matmul(ybank[32 * j:32 * j + VW, 0, c0:512],
                                        vq[:, par, (kt * QH + j) * VW:(kt * QH + j + 1) * VW],
                                        prob_t[:, s % 2, j, c0:512], start=(kt == 0), stop=(kt == 4 * qc + 3),
                                        skip_group_check=True)
            last.then_inc(pv_done, 1)

        def act_out(act, u, qc, s):
            act.wait_ge(pv_done, NS * u + s + 3)
            nc.scalar.copy(o32, ybank[:, 0, :]).then_inc(o32_done, 1)

        def pe_out(pe, u, qc):
            pe.wait_ge(o32_done, 2 * u + qc + 1)
            if qc == 0 and isinstance(u, int) and u:
                pe.wait_ge(att_done, 2 * u)
            for t in range(GT):
                last = nc.tensor.transpose(ybank[:, 1, t * P:(t + 1) * P], o32[:, t * P:(t + 1) * P], ident32[:])
            last.then_inc(ot_ready, 1)

        def dve_out(dve, u, qc):
            dve.wait_ge(ot_ready, 2 * u + qc + 1)
            ot = ybank[:, 1, :].rearrange("p (t j c) -> p t j c", t=GT, j=QH)
            nc.vector.reciprocal(rec[:], ot[:, :, :, DH]).then_inc(rec_done, 1)
            dve.wait_ge(rec_done, 2 * u + qc + 1)
            dst = att[:, bass.ds(u * TT + qc * GT, GT), :].rearrange("p t (j c) -> p t j c", j=QH)
            nc.vector.tensor_tensor(dst, ot[:, :, :, 0:DH], rec[:].unsqueeze(3).to_broadcast([P, GT, QH, DH]),
                                    ALU.mult).then_inc(att_done, 1)

        def chunk_end(s):
            return STEPS[s - 1][0] if s >= 1 and (s == NS or STEPS[s][0] != STEPS[s - 1][0]) else None

        def pe_unit(pe, u, par, i, nxt=True):
            pe.wait_ge(m_in[par], 16 * (i + 1))
            for s in range(NS):
                pe_scores(pe, u, par, s)
                if nxt:
                    if s == 0:
                        pe.wait_ge(op_in[1 - par], 16 * IN_DMAS * (i + par + 1))
                    for v in range(M_AT[s], M_AT[s + 1]):
                        pe_max_block(pe, u + 1, 1 - par, v)
                if s >= 2 and chunk_end(s - 1) is not None:
                    pe_out(pe, u, chunk_end(s - 1))
                if s >= 1:
                    pe_values(pe, u, par, s - 1)
            if nxt:
                pe_max_end(pe, u + 1)
            pe_values(pe, u, par, NS - 1)
            if nxt:
                pe.wait_ge(mT_done, u + 2)
            else:
                pe.wait_ge(att_done, 2 * u + 1)
            pe_out(pe, u, QC - 1)

        def act_unit(act, u, par, nxt=True):
            for s in range(NS):
                act_exp(act, u, s)
                if chunk_end(s) is not None:
                    act_out(act, u, chunk_end(s), s - 1)
            if nxt:
                act_max_end(act, u + 1, 1 - par)
            act_out(act, u, QC - 1, NS - 1)

        def dve_unit(dve, u, nxt=True):
            for s in range(NS):
                if nxt:
                    for v in range(M_AT[s], M_AT[s + 1]):
                        dve_max_block(dve, u + 1, v)
                if s >= 2 and chunk_end(s - 1) is not None:
                    dve_out(dve, u, chunk_end(s - 1))
            if nxt:
                dve_max_end(dve, u + 1)
            dve_out(dve, u, QC - 1)

        def pe_att_project(pe, n, a, g):
            pe.wait_ge(ah_done, a + 1)
            for t in range(GT):
                for k in range(KD):
                    last = nc.tensor.transpose(tp[:, k, t * P:(t + 1) * P], nh[:, t, k * P:(k + 1) * P], ident[:])
            last.then_inc(ath_ready, 1)
            pe.wait_ge(al_done, a + 2)
            pe.wait_ge(aTh_done, a + 1)
            for t in range(GT):
                for k in range(KD):
                    last = nc.tensor.transpose(tp[:, k, t * P:(t + 1) * P], nl[:, t, k * P:(k + 1) * P], ident[:])
            last.then_inc(atl_ready, 1)
            pe.wait_ge(aTl_done, a + 1)
            pe.wait_ge(x_done, n + 1)
            for t in range(GT):
                for j, (xs, ws) in enumerate(((xTh, wh), (xTh, wl), (xTl, wh))):
                    for k in range(KD):
                        last = nc.tensor.matmul(ybank[:, t // 2, (t % 2) * D:(t % 2 + 1) * D], xs[:, k, tokens(g, t, P)],
                                                W(ws, O_AO + k * D, D), start=(j == 0 and k == 0),
                                                stop=(j == 2 and k == KD - 1))
            last.then_inc(y_ready, 1)

        def att_rows(b, j):
            return att[:, bass.ds(b * (H // QH) * TT, H // QH * TT), :].rearrange(
                "p (q t) c -> p t q c", t=TT)[:, j * GT:(j + 1) * GT, :, :]

        def quads(v):
            return v[:].rearrange("p t (q c) -> p t q c", c=QH * DH)

        def act_att_project(act, a, b, j):
            act.wait_ge(al_done, a + 1)
            act.wait_ge(att_done, 2 * NQ)
            for t in range(GT):
                last = nc.scalar.copy(quads(nh)[:, t], att_rows(b, j)[:, t])
            last.then_inc(ah_done, 1)
            act.wait_ge(ath_ready, a + 1)
            nc.scalar.copy(xTh[:, :, tokens(2 * b + j)], tp).then_inc(aTh_done, 1)

        def dve_att_project(dve, n, a, b, j):
            dve.wait_ge(ah_done, a + 1)
            nc.vector.tensor_tensor(quads(nl), att_rows(b, j), quads(nh), ALU.subtract).then_inc(al_done, 1)
            dve.wait_ge(atl_ready, a + 1)
            nc.vector.tensor_copy(xTl[:, :, tokens(2 * b + j)], tp).then_inc(aTl_done, 1)
            dve.wait_ge(y_ready, n + 1)
            for h in range(2):
                last = nc.vector.scalar_tensor_tensor(n32[:, 2 * h:2 * h + 2, :],
                                                      ybank[:, h, :].rearrange("p (t d) -> p t d", t=2), 1 / WS,
                                                      row(R_BO, 2), ALU.mult, ALU.add)
            last.then_inc(ob_done, 1)
            dve.wait_ge(ob_done, a + 1)
            xs = x[:, tiles(2 * b + j), :]
            nc.vector.tensor_tensor(xs, xs, n32[:], ALU.add).then_inc(x_done, 1)

        SPLIT = {4: 0, 8: 4, 12: 5, 16: 9, 20: 13}

        def moe_prepare(parts, at):
            return {at + c: [step] for c, step in parts.items()}

        def merged(*lists):
            out = {}
            for steps in lists:
                for c, todo in steps.items():
                    out.setdefault(c, []).extend(todo)
            return out

        def pe_next(n, ns):
            return {3: lambda e: pe_transpose_high(e, n), 5: lambda e: pe_transpose_low(e, n, ns)}

        def act_next(n, g):
            return {1: lambda e: act_round(e, n), 3: lambda e: act_high_out(e, n, g)}

        def dve_next(n, ns, g):
            return {0: lambda e: dve_moments(e, n, g), 1: lambda e: dve_scale(e, n, g),
                    2: lambda e: dve_low(e, n, ns), 5: lambda e: dve_low_out(e, ns, g)}

        def pool_next(n):
            return {0: lambda e: pool_root(e, n, ve, rstd, ve_done, rstd_done)}

        LAST_AT = [1 + 5 * k for k in range(NG - 1)]

        block = ctx.enter_context(nc.Block())

        @block.sync
        def _(sp):
            sp.dma_start(small[:], small_in).then_inc(const_done, 16)
            sp.dma_start(rows[:], rows_in).then_inc(const_done, 16)
            sp.dma_start(ident[:], ident_in).then_inc(const_done, 16)
            for j in range(RING):
                sp.dma_start(stage[:, j, :], w_in[:, j * WCH:(j + 1) * WCH]).then_inc(w_in_done[j], 16)
            sp.dma_start(sel[:], sel_in).then_inc(const_done, 16)
            sp.dma_start(order[:], order_in).then_inc(const_done, 16)
            sp.dma_start(masks[:], masks_in).then_inc(const_done, 16)
            with sp.Fori(1, NWG) as r:
                for j in range(RING):
                    sp.wait_ge(w_low, RING * r + j - (RING - 1))
                    sp.dma_start(stage[:, j, :], w_in[:, bass.ds((RING * r + j) * WCH, WCH)]).then_inc(w_in_done[j], 16)
            sp.wait_ge(x_done, 17)
            for par in range(2):
                sp.dma_start(kop[KR:KR + 1, par, :, :], alibi_in[1, 4:5, 0:QH, :]).then_inc(ones_in, 16)
                sp.sem_inc(scratch_done[par], 32)
            sp.sem_inc(vscratch_done, 64)
            with sp.Fori(0, B) as b:
                for j in range(2):
                    sp_qkv(sp, 2 * b + j, b, j)
            for par in range(2):
                sp.wait_ge(scratch_done[par], 32 * (2 * NG + 1))
            sp.wait_ge(vscratch_done, 64 * (NG + 1))
            sp_operands(sp, 0, 0)
            sp_operands(sp, 1, 1)
            sp_max_row(sp, 0, 0)
            with sp.Fori(0, NQ // 2 - 1) as i:
                for par in range(2):
                    sp_max_row(sp, 2 * i + par + 1, 1 - par)
                    sp.wait_ge(pv_done, NS * (2 * i + par + 1) + 2)
                    sp_operands(sp, 2 * i + par + 2, par)
            sp_max_row(sp, NQ - 1, 1)
            for g in range(NG):
                sp.wait_ge(x_done, 22 + g)
                sp.dma_start(out[g * GW:(g + 1) * GW, :].rearrange("(t p) d -> p t d", p=P),
                             x[:, g * GT:(g + 1) * GT, :]).then_inc(out_done, 16)
            sp.wait_ge(out_done, 16 * NG)

        @block.gpsimd
        def _(pool):
            nc.gpsimd.memset(mhalf[:], -0.5).then_inc(pool_set, 1)
            pool.wait_ge(pool_set, 1)
            with pool.Fori(0, 5) as n:
                pool_root(pool, n, ve, rstd, ve_done, rstd_done)
            with pool.Fori(0, B) as b:
                pool_root(pool, 5 + 2 * b, ve, rstd, ve_done, rstd_done)
                for j in range(2):
                    pool_root(pool, 2 * b + j, zve, zrstd, zve_done, zrstd_done)
                pool_root(pool, 6 + 2 * b, ve, rstd, ve_done, rstd_done)
            with pool.Fori(9, 13) as n:
                pool_root(pool, n, ve, rstd, ve_done, rstd_done)
            with pool.Fori(0, NG - 1) as g:
                pool_moe(pool, g, moe_prepare(pool_next(13 + g), 1))
            pool_moe(pool, NG - 1, merged(*[moe_prepare(pool_next(16 + k), at) for k, at in enumerate(LAST_AT)]))
            for n in (19, 20):
                pool_root(pool, n, ve, rstd, ve_done, rstd_done)
            with pool.Fori(0, NG - 1) as g:
                pool_moe(pool, NG + g, moe_prepare(pool_next(21 + g), 1))
            pool_moe(pool, 2 * NG - 1, {})

        @block.tensor
        def _(pe):
            pe.wait_ge(const_done, 6 * 16)
            pe.sem_inc(pv_done, 2)
            pe_transpose_high(pe, 0)
            pe.wait_ge(w_low, 3)
            with pe.Fori(0, NG - 1) as g:
                pe_ffn(pe, g, g, g, {4: [lambda e: pe_transpose_high(e, g + 1)]})
            pe_ffn(pe, 3, 3, 3, {4: [lambda e: pe_transpose_high(e, 4)], 6: [lambda e: pe_transpose_low(e, 4, 0)]})
            with pe.Fori(0, B) as b:
                pe.wait_ge(xTl_done, 2 * b + 1)
                pe_transpose_high(pe, 5 + 2 * b)
                pe_transpose_low(pe, 5 + 2 * b, 1 + 2 * b)
                pe_wkv(pe, 4 + 2 * b, 2 * b, 2 * b, b)
                pe_transpose_high(pe, 6 + 2 * b)
                pe_transpose_low(pe, 6 + 2 * b, 2 + 2 * b)
            pe.wait_ge(xTl_done, SPLIT[8] + 1)
            with pe.Fori(0, NG - 1) as g:
                pe_ffn(pe, 8 + g, 4 + g, g, {4: [lambda e: pe_transpose_high(e, 9 + g)]})
            pe_ffn(pe, 11, 7, 3, {4: [lambda e: pe_transpose_high(e, 12)],
                                  6: [lambda e: pe_transpose_low(e, 12, SPLIT[12])]})
            def pe_moe_layer(n0, m0, last):
                s0 = SPLIT[n0]
                pe_router(pe, s0, 0)
                pe_transpose_routes(pe, m0)
                with pe.Fori(0, NG - 1) as g:
                    pe_moe(pe, n0 + g, s0 + g, m0 + g, g, merged(
                        moe_prepare(pe_next(n0 + g + 1, s0 + g + 1), 1),
                        {8: [lambda e: pe_router(e, s0 + g + 1, g + 1)],
                         14: [lambda e: pe_transpose_routes(e, m0 + g + 1)]}))
                pe_moe(pe, n0 + NG - 1, s0 + NG - 1, m0 + NG - 1, NG - 1, last)

            pe_moe_layer(12, 0, merged(*[moe_prepare(pe_next(16 + k, SPLIT[16] + k), at)
                                         for k, at in enumerate(LAST_AT)]))
            pe.wait_ge(xTl_done, SPLIT[16] + 3)
            pe_transpose_high(pe, 19)
            pe_transpose_low(pe, 19, SPLIT[16] + 3)
            pe.wait_ge(x_done, 17)
            with pe.Fori(0, NG) as g:
                pe_qkv(pe, 16 + g, SPLIT[16] + g, g, g)
            pe.wait_ge(v_done, NG + 1)
            pe.wait_ge(op_in[0], 16 * IN_DMAS)
            for v in range(MU):
                pe_max_block(pe, 0, 0, v)
            pe_max_end(pe, 0)
            pe.wait_ge(mT_done, 1)
            pe.wait_ge(ones_in, 32)
            with pe.Fori(0, NQ // 2 - 1) as i:
                pe_unit(pe, 2 * i, 0, i)
                pe_unit(pe, 2 * i + 1, 1, i)
            pe_unit(pe, NQ - 2, 0, NQ // 2 - 1)
            pe_unit(pe, NQ - 1, 1, NQ // 2 - 1, nxt=False)
            with pe.Fori(0, NG) as g:
                pe_att_project(pe, 16 + g, g, g)
            pe_transpose_high(pe, 20)
            pe_transpose_low(pe, 20, SPLIT[20])
            pe_moe_layer(20, NG, {})

        @block.scalar
        def _(act):
            for g in range(NG):
                act.dma_start(x[:, g * GT:(g + 1) * GT, :],
                              x_in[g * GW:(g + 1) * GW, :].rearrange("(t p) d -> p t d", p=P)).then_inc(x_in_done, 16)
            act.sem_inc(exp_done, 2)
            act_weights(act, 0)
            act.wait_ge(const_done, 6 * 16)
            nc.scalar.activation(eg[:], rows[:, R_G, :], ACT.Exp, scale=-1.0).then_inc(act_set, 1)
            nc.scalar.activation(decay[:], small[0:NST, S_LW:S_LW + 1], ACT.Exp).then_inc(act_set, 1)
            nc.scalar.activation(nu[:], small[0:NST, S_U:S_U + 1], ACT.Exp).then_inc(act_set, 1)
            nc.scalar.activation(bq4[:], small[:, S_BQ:S_BQ + KD], ACT.Copy, scale=SS / math.sqrt(DH)).then_inc(act_set, 1)
            nc.scalar.copy(ident32[:], ident[:]).then_inc(act_set, 1)
            act_round(act, 0)
            act_high_out(act, 0, 0)
            act_weights(act, 1)
            with act.Fori(0, NG - 1) as g:
                act_round(act, g + 1)
                act_ffn(act, g, {4: [lambda e: act_high_out(e, g + 1, g + 1)]})
                act_weights(act, g + 2)
            act_round(act, 4)
            act_ffn(act, 3, {4: [lambda e: act_high_out(e, 4, 0)]})
            act.wait_ge(set_done, 4)
            with act.Fori(0, B) as b:
                act_round(act, 5 + 2 * b)
                act_high_out(act, 5 + 2 * b, 2 * b + 1)
                act_wkv(act, 2 * b)
                act_round(act, 6 + 2 * b)
                act_high_out(act, 6 + 2 * b, (2 * b + 2) % NG)
            with act.Fori(0, NG - 1) as g:
                act_round(act, g + 9)
                act_ffn(act, g + 4, {4: [lambda e: act_high_out(e, g + 9, g + 1)]})
            act_round(act, 12)
            act_ffn(act, 7, {4: [lambda e: act_high_out(e, 12, 0)]})

            def act_moe_layer(n0, m0, last):
                act_exp_routes(act, m0)
                act_routes_out(act, m0)
                with act.Fori(0, NG - 1) as g:
                    act_moe(act, m0 + g, merged(
                        moe_prepare(act_next(n0 + g + 1, g + 1), 1),
                        {8: [lambda e: act_exp_routes(e, m0 + g + 1)],
                         MC - 1: [lambda e: act_routes_out(e, m0 + g + 1)]}))
                act_moe(act, m0 + NG - 1, last)

            act_moe_layer(12, 0, merged(*[moe_prepare(act_next(16 + k, k), at) for k, at in enumerate(LAST_AT)]))
            act_round(act, 19)
            act_high_out(act, 19, 3)
            with act.Fori(0, NG) as a:
                act_qkv(act, a)
            act_max_end(act, 0, 0)
            with act.Fori(0, NQ // 2 - 1) as i:
                act_unit(act, 2 * i, 0)
                act_unit(act, 2 * i + 1, 1)
            act_unit(act, NQ - 2, 0)
            act_unit(act, NQ - 1, 1, nxt=False)
            with act.Fori(0, B) as b:
                for j in range(2):
                    act_att_project(act, 2 * b + j, b, j)
            act_round(act, 20)
            act_high_out(act, 20, 0)
            act_moe_layer(20, NG, {})

        @block.vector
        def _(dve):
            nc.vector.memset(decayw[:], 1.0).then_inc(set_done, 1)
            dve.wait_ge(x_in_done, 16 * NG)
            dve.sem_inc(x_done, 1)
            dve.sem_inc(mx_done, 2)
            dve.sem_inc(pl_done, 2)
            dve.sem_inc(v_done, 1)
            dve.sem_inc(al_done, 1)
            dve_normalise(dve, 0, 0, first=True)
            dve_weights(dve, 0)
            dve.wait_ge(act_set, 5)
            nc.vector.tensor_scalar(gsc[:], eg[:], 1.0, None, ALU.add).then_inc(set_done, 1)
            dve.wait_ge(set_done, 2)
            nc.vector.tensor_scalar(decayw[:], decayw[:], decay[:], None, ALU.mult).then_inc(set_done, 1)
            nc.vector.tensor_scalar(nu[:], nu[:], -1.0, None, ALU.mult).then_inc(set_done, 1)
            nc.vector.reciprocal(gsc[:], gsc[:]).then_inc(set_done, 1)
            dve.wait_ge(set_done, 5)
            nc.vector.tensor_scalar(omg[:], gsc[:], -1.0, 1.0, ALU.mult, ALU.add).then_inc(set_done, 1)
            dve.wait_ge(set_done, 6)
            nc.vector.tensor_scalar(gsc[:], gsc[:], 1 / WS, None, ALU.mult).then_inc(set_done, 1)
            dve.wait_ge(set_done, 7)
            dve_weights(dve, 1)
            with dve.Fori(0, NG - 1) as g:
                dve_normalise(dve, g + 1, g + 1, first=True)
                dve_ffn_sum(dve, g, g, g)
                dve_weights(dve, g + 2)
            dve_normalise(dve, 4, 0)
            dve_low(dve, 4, 0)
            dve_skip(dve, 4, 0)
            dve_low_out(dve, 0, 0)
            dve_ffn_sum(dve, 3, 3, 3)
            with dve.Fori(0, B) as b:
                dve_normalise(dve, 5 + 2 * b, 2 * b + 1)
                dve_low(dve, 5 + 2 * b, 1 + 2 * b)
                dve_skip(dve, 5 + 2 * b, 1)
                dve_low_out(dve, 1 + 2 * b, 2 * b + 1)
                dve_wkv(dve, 4 + 2 * b, 2 * b, b)
                dve_normalise(dve, 6 + 2 * b, (2 * b + 2) % NG)
                dve_low(dve, 6 + 2 * b, 2 + 2 * b)
                dve_skip(dve, 6 + 2 * b, 0)
                dve_low_out(dve, 2 + 2 * b, (2 * b + 2) % NG)
            with dve.Fori(0, NG - 1) as g:
                dve_normalise(dve, g + 9, g + 1)
                dve_ffn_sum(dve, 8 + g, 4 + g, g)
            dve_normalise(dve, 12, 0)
            dve_low(dve, 12, SPLIT[12])
            dve_low_out(dve, SPLIT[12], 0)
            dve_ffn_sum(dve, 11, 7, 3)

            def dve_moe_layer(n0, m0, last):
                s0 = SPLIT[n0]
                dve_routes(dve, m0)
                with dve.Fori(0, NG - 1) as g:
                    dve_moe(dve, m0 + g, merged(
                        moe_prepare(dve_next(n0 + g + 1, s0 + g + 1, g + 1), 1),
                        {8: [lambda e: dve_routes(e, m0 + g + 1)]}))
                    dve_sum(dve, n0 + g, g, 0.5 / (WS * US))
                dve_moe(dve, m0 + NG - 1, last)
                dve_sum(dve, n0 + NG - 1, NG - 1, 0.5 / (WS * US))

            dve_moe_layer(12, 0, merged(*[moe_prepare(dve_next(16 + k, SPLIT[16] + k, k), at)
                                          for k, at in enumerate(LAST_AT)]))
            nc.vector.memset(vst[:, :, :, DH:VW], 1.0)
            dve_normalise(dve, 19, 3)
            dve_low(dve, 19, SPLIT[16] + 3)
            dve_low_out(dve, SPLIT[16] + 3, 3)
            with dve.Fori(0, NG) as a:
                dve_qkv(dve, a)
            for v in range(MU):
                dve_max_block(dve, 0, v)
            dve_max_end(dve, 0)
            with dve.Fori(0, NQ // 2 - 1) as i:
                dve_unit(dve, 2 * i)
                dve_unit(dve, 2 * i + 1)
            dve_unit(dve, NQ - 2)
            dve_unit(dve, NQ - 1, nxt=False)
            with dve.Fori(0, B) as b:
                for j in range(2):
                    dve_att_project(dve, 16 + 2 * b + j, 2 * b + j, b, j)
            dve_normalise(dve, 20, 0)
            dve_low(dve, 20, SPLIT[20])
            dve_low_out(dve, SPLIT[20], 0)
            dve_moe_layer(20, NG, {})


def packed(i):
    def cols(w, chunks):
        return w.reshape(chunks, P, -1).transpose(1, 0, 2).reshape(P, -1)

    fc1 = np.concatenate([i["L1_ffn_expert_fc1"].reshape(NE * FE, D), i["L1_ffn_shared_fc1"]], 0).T
    fc2 = np.concatenate([i["L1_ffn_expert_fc2"].reshape(NE * FE, D), i["L1_ffn_shared_fc2"]], 0).T
    proj = np.zeros((MC * P, D), np.float32)
    proj[0:NE * FE] = i["L1_ffn_expert_proj"].transpose(0, 2, 1).reshape(NE * FE, D)
    proj[NE * FE:FM] = i["L1_ffn_shared_proj"].T
    w = np.zeros((P, WCOLS), np.float32)
    for at, part in ((O_W0, cols(i["L0_ffn_W0"].T, KD)), (O_W1, cols(i["L0_ffn_W1"].T, FC)),
                     (O_SH, cols(i["L0_attn_W_shift"].T, KD)), (O_WK, cols(i["L0_attn_W_key"].T, KD)),
                     (O_WV, cols(i["L0_attn_W_value"].T, KD)),
                     (O_RT, cols(np.concatenate([i["L1_ffn_gate_w"], i["L1_ffn_shared_gate_w"]], 0).T, KD)),
                     (O_F1, cols(fc1, KD)), (O_F2, cols(fc2, KD)), (O_PR, cols(proj, MC)),
                     (O_AQ, cols(i["L1_attn_Wq"].T, KD)), (O_AK, cols(i["L1_attn_Wk"].T, KD)),
                     (O_AV, cols(i["L1_attn_Wv"].T, KD)), (O_AO, cols(i["L1_attn_Wo"].T, KD))):
        w[:, at:at + part.shape[1]] = part
    w[0:NST, O_WO:O_WO + D] = i["L0_attn_W_output"].T
    small = np.zeros((P, SCOLS), np.float32)
    small[:, S_B0:S_B0 + FC] = i["L0_ffn_bias0"].reshape(FC, P).T
    small[0:NST, S_LW] = i["L0_attn_time_decay"]
    small[0:NST, S_U] = i["L0_attn_time_first"]
    small[:, S_BQ:S_BQ + KD] = i["L1_attn_bq"].reshape(KD, P).T
    small[:, S_BK:S_BK + KD] = i["L1_attn_bk"].reshape(KD, P).T
    rows = np.stack([i["L0_ffn_bias1"], i["L0_attn_gate"], i["L0_attn_ln_gamma"], i["L0_attn_ln_beta"],
                     i["L1_attn_bv"], i["L1_attn_bo"]])
    rows = np.broadcast_to(rows, (P,) + rows.shape)
    ident = np.eye(P, dtype=np.float16)
    sel = np.zeros((2 * NR, MC * P), np.float16)
    for j in range(FM):
        e = min(j // FE, NE)
        sel[e, j] = sel[NR + e, j] = SEL
    order = np.broadcast_to(np.arange(NE, 0, -1, dtype=np.float32), (P, NE))
    upper = np.triu(np.full((P, P), MASK, np.float16), 1)
    masks = np.stack([upper, upper.T], 1)
    slopes = np.array([2.0 ** (-0.5 * (h + 1)) for h in range(H)], np.float32)
    scaled = np.tile(slopes, B).astype(np.float64) * SS
    high = scaled.astype(np.float16)
    low = ((scaled - high) * T).astype(np.float16)
    pos = np.arange(T)
    alibi = np.zeros((2, 5, B * H, T), np.float16)
    alibi[0, 0], alibi[0, 2] = high[:, None], low[:, None]
    alibi[0, 1], alibi[0, 3] = -pos, -pos / T
    alibi[1, 0], alibi[1, 2] = pos, pos / T
    alibi[1, 1], alibi[1, 3] = high[:, None], low[:, None]
    alibi[1, 4] = 1.0
    return {"x": i["L0_attn_x"].reshape(B * T, D), "w": w, "small": small, "rows": rows, "ident": ident, "sel": sel,
            "order": order, "masks": masks, "alibi": alibi}


def kernel(**inputs):
    import concourse.bacc as bacc
    from concourse.bass_utils import run_bass_kernel_spmd

    nc = bacc.Bacc("TRN2", target_bir_lowering=False, num_devices=1)
    arrays = {f"in_{k}": np.ascontiguousarray(v) for k, v in packed(inputs).items()}
    args = [nc.dram_tensor(k, a.shape, mybir.dt.from_np(a.dtype), kind="ExternalInput").ap() for k, a in arrays.items()]
    out = nc.dram_tensor("out_x", (B * T, D), F32, kind="ExternalOutput").ap()
    block_kernel(nc, *args, out)
    r = run_bass_kernel_spmd(nc, [arrays], core_ids=[0])
    return r.results[0]["out_x"].reshape(B, T, D)
```

```python
from contextlib import ExitStack
import math

import numpy as np

import concourse.bass as bass
from concourse import mybir

F32, F16 = mybir.dt.float32, mybir.dt.float16
ALU, ACT, AX = mybir.AluOpType, mybir.ActivationFunctionType, mybir.AxisListType

P = 128
B, T, D = 2, 1024, 256
KD = D // P
GT = 4
GW = GT * P
NG = B * T // GW
FF = 1024
FC = FF // P
NST = 64
NE, FE, FS = 8, 176, 704
FM = NE * FE + FS
MC = -(-FM // P)
ML = FM - (MC - 1) * P
NR = NE + 1
H = 16
DH = D // H
TT = T // P
HH = H // 2
QH = 4
NQ = B * H // QH
VW = DH + 1
KR = 4 + 3 * DH
KM = 96
QC = T // 512
MU = QH * TT
SS = 16.0
MASK = -60000.0
EPS = 1e-5

WS = 2.0 ** 8
US = 2.0 ** 4
CS = 2.0 ** 8
SEL = US / (WS * CS)

O_W0 = 0
O_W1 = O_W0 + KD * FF
O_SH = O_W1 + FC * D
O_WK = O_SH + KD * D
O_WV = O_WK + KD * NST
O_WO = O_WV + KD * NST
O_RT = O_WO + D
O_F1 = O_RT + 32
O_F2 = O_F1 + KD * FM
O_PR = O_F2 + KD * FM
O_AQ = O_PR + MC * D
O_AK = O_AQ + KD * D
O_AV = O_AK + KD * D
O_AO = O_AV + KD * D
WCOLS = O_AO + KD * D
WCH = 1000
RING = 4
SHARED = 49 * 1024
NCHUNK = WCOLS // WCH
NWG = NCHUNK // RING
assert WCOLS % WCH == 0 and NCHUNK % RING == 0

S_B0, S_LW, S_U, S_BQ, S_BK = 0, FC, FC + 1, FC + 2, FC + 4
SCOLS = FC + 6
R_B1, R_G, R_GAM, R_BET, R_BV, R_BO = range(6)


def block_kernel(nc, x_in, w_in, small_in, rows_in, ident_in, sel_in, order_in, masks_in, alibi_in, out):
    ctx = ExitStack()
    with ctx:
        def sb(name, shape, dt):
            return ctx.enter_context(nc.sbuf_tensor(name, shape, dt))

        def sem(name):
            return ctx.enter_context(nc.semaphore(name))

        shared = sb("shared", [P, SHARED // 4], F32)

        def part_of_shared():
            at = [0]

            def part(name, shape, dt):
                size = math.prod(shape[1:]) * (4 if dt is F32 else 2)
                v = shared[0:shape[0], at[0] // 4:(at[0] + size) // 4]
                at[0] += size
                assert at[0] <= SHARED, (name, at[0])
                v = v if dt is F32 else v.bitcast(dt)
                if len(shape) == 3:
                    v = v.rearrange("p (a b) -> p a b", b=shape[2])
                elif len(shape) == 4:
                    v = v.rearrange("p (a b c) -> p a b c", b=shape[2], c=shape[3])
                return v
            return part

        wkv_part, moe_part, att_part = part_of_shared(), part_of_shared(), part_of_shared()

        x = sb("x", [P, NG * GT, D], F32)
        xTh = sb("xTh", [P, KD, NG * GW], F16)
        xTl = sb("xTl", [P, KD, NG * GW], F16)
        n32 = sb("n32", [P, GT, D], F32)
        nh = sb("nh", [P, GT, D], F16)
        nl = sb("nl", [P, GT, D], F16)
        stat = sb("stat", [P, GT, 6], F32)
        mv = sb("mv", [P, GT, 2], F32)
        ve = sb("ve", [P, GT], F32)
        rstd = sb("rstd", [P, GT], F32)
        mhalf = sb("mhalf", [P, GT], F32)
        wh = sb("wh", [P, WCOLS], F16)
        wl = sb("wl", [P, WCOLS], F16)
        stage_raw = sb("stage", [P, NG * GT * D], F32)
        stage = stage_raw[:, 0:RING * WCH].rearrange("p (r c) -> p r c", r=RING)
        small = sb("small", [P, SCOLS], F32)
        rows = sb("rows", [P, 6, D], F32)
        ident = sb("ident", [P, P], F16)
        ident32 = sb("ident32", [P, P], F32)
        sel = sb("sel", [2 * NR, MC * P], F16)
        order = sb("order", [P, NE], F32)
        hT = sb("hT", [P, FC, GW], F16)
        t16 = sb("t16", [P, 2, 2 * D], F16)
        sg = moe_part("sg", [P, 2, GW], F32)
        pr = moe_part("pr", [P, 2, GW], F32)
        u32 = moe_part("u32", [P, 2, GW], F32)
        uh = moe_part("uh", [P, 2, GW], F16)
        ul = moe_part("ul", [P, 2, GW], F16)
        lg = sb("lg", [P, GT, NR], F32)
        dl = sb("dl", [P, GT, NR], F32)
        er = sb("er", [P, GT, NR], F32)
        prob = sb("prob", [P, GT, NE], F32)
        pm = sb("pm", [P, GT, NE], F32)
        m8 = sb("m8", [P, GT, NE], F32)
        s1 = sb("s1", [P, GT, NE], F32)
        s2 = sb("s2", [P, GT, NE], F32)
        mx = sb("mx", [P, GT], F32)
        comb = sb("comb", [P, GT, NR], F32)
        ch = sb("ch", [P, GT, 2 * NR], F16)
        cT = sb("cT", [2 * NR, GW], F16)
        omg = wkv_part("omg", [P, D], F32)
        gsc = wkv_part("gsc", [P, D], F32)
        eg = wkv_part("eg", [P, D], F32)
        R = wkv_part("R", [P, 2, GT, D], F32)
        z = wkv_part("z", [P, GT, D], F32)
        zn = wkv_part("zn", [P, GT, D], F32)
        zh = wkv_part("zh", [P, GT, D], F16)
        zl = wkv_part("zl", [P, GT, D], F16)
        zTh = wkv_part("zTh", [P, KD, GW], F16)
        zTl = wkv_part("zTl", [P, KD, GW], F16)
        ka = wkv_part("ka", [NST, GW], F32)
        ev = wkv_part("ev", [NST, GW], F32)
        zve = sb("zve", [P, GT], F32)
        zrstd = sb("zrstd", [P, GT], F32)
        kb = wkv_part("kb", [NST, GW], F32)
        wkv = wkv_part("wkv", [NST, GW], F32)
        decay = sb("decay", [NST, 1], F32)
        decayw = wkv_part("decayw", [NST, GW], F32)
        nu = sb("nu", [NST, 1], F32)
        st32 = wkv_part("st32", [NST, 2, GW], F32)
        sth = wkv_part("sth", [NST, 2, GW], F16)
        stl = wkv_part("stl", [NST, 2, GW], F16)

        def by_chunk(v):
            return v.rearrange("p (q j c) -> p q j c", q=QC, j=QH)

        qop = [by_chunk(att_part("qop", [P, QC * QH * 512], F16)), by_chunk(xTh[:].rearrange("p k c -> p (k c)"))]
        kop = [by_chunk(att_part("kop", [P, QC * QH * 512], F16)), by_chunk(xTl[:].rearrange("p k c -> p (k c)"))]
        vals = att_part("vals", [P, B * 2 * TT * HH * VW], F32)
        vals_by = vals.rearrange("p (m t h c) -> p m t h c", m=B * 2, t=TT, h=HH)
        prob_t = att_part("prob_t", [P, 2, QH * 512], F32).rearrange("p a (j c) -> p a j c", j=QH)
        rest = prob_t.rearrange("p a j c -> p (a j c)")
        p32 = rest[:, 0:2 * GW].rearrange("p (a c) -> p a c", a=2)
        psplit = rest[:, 2 * GW:4 * GW].bitcast(F16).rearrange("p (a h c) -> p a h c", a=2, h=2)
        att = stage_raw[:].rearrange("p (t d) -> p t d", d=QH * DH)
        o32 = t16[:].rearrange("p a b -> p (a b)").bitcast(F32)
        mxs = sb("mxs", [P, MU], F32)
        mneg = sb("mneg", [P, QC, MU // QC], F16)
        vq = hT[:, 1:1 + 2 * TT * QH * VW * 2 // GW + 1, :].rearrange("p a b -> p (a b)").bitcast(F32)[
            :, 0:2 * TT * QH * VW].rearrange("p (a t r) -> p a t r", a=2, t=TT)
        mT = hT[0:MU // QC, 0, :].rearrange("p (a h c) -> p a h c", a=2, h=QC)
        masks = sb("masks", [P, 2, P], F16)
        rec = sb("rec", [P, GT, QH], F32)
        bq4 = sb("bq4", [P, KD], F32)

        low_banks = [ctx.enter_context(nc.psum_tensor(f"bank{i}", [P, 512], F32)) for i in range(2)]
        mid = ctx.enter_context(nc.psum_tensor("mid", [P, 4, 512], F32))
        bank = [low_banks[0][:], low_banks[1][:]] + [mid[:, i, :] for i in range(4)]
        ybank = ctx.enter_context(nc.psum_tensor("ybank", [P, 2, 512], F32))
        tp = bank[0].bitcast(F16).rearrange("p (k c) -> p k c", k=KD)
        order4 = order[:].unsqueeze(1).to_broadcast([P, GT, NE])
        tp2 = bank[1].bitcast(F16).rearrange("p (k c) -> p k c", k=KD)

        x_in_done = sem("x_in_done")
        x0_in_done = sem("x0_in_done")
        early_done = sem("early_done")
        const_done = sem("const_done")
        w_in_done = [sem(f"w_in_done{i}") for i in range(RING)]
        w_high = sem("w_high")
        w_low = sem("w_low")
        set_done = sem("set_done")
        pool_set = sem("pool_set")
        x_done = sem("x_done")
        stat_done = sem("stat_done")
        aggr_done = sem("aggr_done")
        wait_carrier = sem("wait_carrier")
        ve_done = sem("ve_done")
        rstd_done = sem("rstd_done")
        n32_done = sem("n32_done")
        nh_done = sem("nh_done")
        nl_done = sem("nl_done")
        th_ready = sem("th_ready")
        tl_ready = sem("tl_ready")
        xTh_done = sem("xTh_done")
        xTl_done = sem("xTl_done")
        h_ready = sem("h_ready")
        gelu_done = sem("gelu_done")
        y_ready = sem("y_ready")
        t16_done = sem("t16_done")
        h1_ready = sem("h1_ready")
        C_ready = sem("C_ready")
        silu_done = sem("silu_done")
        pr_done = sem("pr_done")
        u32_done = sem("u32_done")
        uh_done = sem("uh_done")
        ul_done = sem("ul_done")
        rt_ready = sem("rt_ready")
        rt_step = sem("rt_step")
        dl_done = sem("dl_done")
        er_done = sem("er_done")
        rt_sel = sem("rt_sel")
        comb_done = sem("comb_done")
        zg_done = sem("zg_done")
        wk2_step = sem("wk2_step")
        act_set = sem("act_set")
        ch_done = sem("ch_done")
        ct_ready = sem("ct_ready")
        cT_done = sem("cT_done")
        wk_set = sem("wk_set")
        R_done = sem("R_done")
        sh_ready = sem("sh_ready")
        z_read = sem("z_read")
        zn_done = sem("zn_done")
        wk_step = sem("wk_step")
        zve_done = sem("zve_done")
        zrstd_done = sem("zrstd_done")
        z_done = sem("z_done")
        zh_done = sem("zh_done")
        zl_done = sem("zl_done")
        zth_ready = sem("zth_ready")
        ztl_ready = sem("ztl_ready")
        zTh_done = sem("zTh_done")
        zTl_done = sem("zTl_done")
        kv_ready = sem("kv_ready")
        ek_done = sem("ek_done")
        sig_done = sem("sig_done")
        ev_done = sem("ev_done")
        st_done = sem("st_done")
        sth_done = sem("sth_done")
        stl_done = sem("stl_done")
        out_done = sem("out_done")
        bq_done = sem("bq_done")
        qk_ready = sem("qk_ready")
        p32_done = sem("p32_done")
        ph_done = sem("ph_done")
        pl_done = sem("pl_done")
        v_ready = sem("v_ready")
        v_done = sem("v_done")
        scratch_done = [sem(f"scratch_done{i}") for i in range(2)]
        pos_done = sem("pos_done")
        fill_done = sem("fill_done")
        vones_done = sem("vones_done")
        vq_done = sem("vq_done")
        op_in = [sem(f"op_in{i}") for i in range(2)]
        ql_in = [sem(f"ql_in{i}") for i in range(2)]
        m_in = [[sem(f"m_in{i}{h}") for h in range(QC)] for i in range(2)]
        s_ready = sem("s_ready")
        mx_done = sem("mx_done")
        mneg_done = sem("mneg_done")
        mt_ready = sem("mt_ready")
        mT_done = sem("mT_done")
        st_ready = sem("st_ready")
        exp_done = sem("exp_done")
        pv_done = sem("pv_done")
        o32_done = sem("o32_done")
        ot_ready = sem("ot_ready")
        rec_done = sem("rec_done")
        att_done = sem("att_done")
        ah_done = sem("ah_done")
        al_done = sem("al_done")
        ath_ready = sem("ath_ready")
        atl_ready = sem("atl_ready")
        aTh_done = sem("aTh_done")
        aTl_done = sem("aTl_done")
        ob_done = sem("ob_done")
        op_dram = nc.dram_tensor("scratch_operands", [2, B * 2, KR * HH, T], F16).ap()

        RT_STEPS = 16

        def tokens(g, t=0, n=GW):
            return bass.ds(g * GW + t * P, n)

        def tiles(g, t=0, n=GT):
            return bass.ds(g * GT + t, n)

        def W(parts, col, n, rows_=P):
            return parts[0:rows_, col:col + n]

        def row(i, n):
            return rows[:, i:i + 1, :].to_broadcast([P, n, D])

        def pe_transpose_high(pe, n):
            pe.wait_ge(nh_done, n + 1)
            for t in range(GT):
                for k in range(KD):
                    last = nc.tensor.transpose(tp[:, k, t * P:(t + 1) * P], nh[:, t, k * P:(k + 1) * P], ident[:])
            last.then_inc(th_ready, 1)

        def pe_transpose_low(pe, n, ns):
            pe.wait_ge(nl_done, ns + 1)
            pe.wait_ge(xTh_done, n + 1)
            for t in range(GT):
                for k in range(KD):
                    last = nc.tensor.transpose(tp[:, k, t * P:(t + 1) * P], nl[:, t, k * P:(k + 1) * P], ident[:])
            last.then_inc(tl_ready, 1)

        def pe_router(pe, ns, g):
            pe.wait_ge(xTl_done, ns + 1)
            for t in range(GT):
                for i, (xs, ws) in enumerate(((xTh, wh), (xTh, wl), (xTl, wh))):
                    for k in range(KD):
                        last = nc.tensor.matmul(bank[0][:, t * NR:(t + 1) * NR], xs[:, k, tokens(g, t, P)],
                                                W(ws, O_RT + k * NR, NR), start=(i == 0 and k == 0),
                                                stop=(i == 2 and k == KD - 1))
            last.then_inc(rt_ready, 1)

        def pe_transpose_routes(pe, m):
            pe.wait_ge(ch_done, m + 1)
            for t in range(GT):
                last = nc.tensor.transpose(tp[0:2 * NR, 0, t * P:(t + 1) * P], ch[:, t, :], ident[:])
            last.then_inc(ct_ready, 1)

        def pe_ffn(pe, n, f, g, steps):
            pe.wait_ge(xTh_done, n + 1)

            def hidden(c):
                for k in range(KD):
                    for i, ws in enumerate((wh, wl)):
                        last = nc.tensor.matmul(bank[2 + c % 4], W(ws, O_W0 + k * FF + c * P, P),
                                                xTh[:, k, tokens(g)], start=(k == 0 and i == 0),
                                                stop=(k == KD - 1 and i == 1))
                last.then_inc(h_ready, 1)

            def project(c):
                pe.wait_ge(gelu_done, FC * f + c + 1)
                if c == 0:
                    pe.wait_ge(x_done, n + 1)
                    pe.wait_ge(w_low, 5)
                for t in range(GT):
                    for i, ws in enumerate((wh, wl)):
                        last = nc.tensor.matmul(ybank[:, t // 2, (t % 2) * D:(t % 2 + 1) * D],
                                                hT[:, c, t * P:(t + 1) * P], W(ws, O_W1 + c * D, D),
                                                start=(c == 0 and i == 0 and t % 2 == 0),
                                                stop=(c == FC - 1 and i == 1), skip_group_check=True)
                if c == FC - 1:
                    last.then_inc(y_ready, 1)

            for c in range(FC):
                hidden(c)
                if c >= 2:
                    project(c - 2)
                for step in steps.get(c, ()):
                    step(pe)
            project(FC - 2)
            project(FC - 1)

        def pe_moe(pe, n, ns, m, g, steps):
            def hidden(c):
                rows_ = P if c < MC - 1 else ML
                for off, bk in ((O_F1, bank[2 + c % 2]), (O_F2, bank[4 + c % 2])):
                    for k in range(KD):
                        for i, (ws, xs) in enumerate(((wh, xTh), (wh, xTl), (wl, xTh))):
                            last = nc.tensor.matmul(bk[0:rows_, :], W(ws, off + k * FM + c * P, rows_),
                                                    xs[:, k, tokens(g)], start=(k == 0 and i == 0),
                                                    stop=(k == KD - 1 and i == 2))
                    if off == O_F1:
                        last.then_inc(h1_ready, 1)
                if c >= 1:
                    pe.wait_ge(u32_done, MC * m + c)
                nc.tensor.matmul(bank[1][0:rows_, :], sel[:, c * P:c * P + rows_], cT[:],
                                 start=True, stop=True).then_inc(C_ready, 1)

            def project(c):
                rows_ = P if c < MC - 1 else ML
                pe.wait_ge(ul_done, MC * m + c + 1)
                if c == 0:
                    pe.wait_ge(x_done, n + 1)
                for t in range(GT):
                    for i, (us, ws) in enumerate(((uh, wh), (uh, wl), (ul, wh))):
                        last = nc.tensor.matmul(ybank[:, t // 2, (t % 2) * D:(t % 2 + 1) * D],
                                                us[0:rows_, c % 2, t * P:(t + 1) * P],
                                                W(ws, O_PR + c * D, D, rows_),
                                                start=(c == 0 and i == 0 and t % 2 == 0),
                                                stop=(c == MC - 1 and i == 2), skip_group_check=True)
                if c == MC - 1:
                    last.then_inc(y_ready, 1)

            pe.wait_ge(xTh_done, n + 1)
            pe.wait_ge(xTl_done, ns + 1)
            pe.wait_ge(cT_done, m + 1)
            for c in range(MC):
                hidden(c)
                if c >= 1:
                    project(c - 1)
                for step in steps.get(c, ()):
                    step(pe)
            project(MC - 1)

        def pe_wkv(pe, n, ns, q, b):
            pe.wait_ge(xTh_done, n + 2)
            pe.wait_ge(xTl_done, ns + 2)
            for j in range(2):
                if j == 0:
                    pe.wait_ge(x_done, n + 1)
                else:
                    pe.wait_ge(z_read, q + 1)
                for t in range(GT):
                    for i, (xs, ws) in enumerate(((xTh, wh), (xTh, wl), (xTl, wh))):
                        for k in range(KD):
                            last = nc.tensor.matmul(ybank[:, t // 2, (t % 2) * D:(t % 2 + 1) * D],
                                                    xs[:, k, bass.ds((2 * b + 1 - j) * GW + t * P, P)],
                                                    W(ws, O_SH + k * D, D),
                                                    start=(i == 0 and k == 0), stop=(i == 2 and k == KD - 1))
                last.then_inc(sh_ready, 1)
            for j in range(2):
                pe.wait_ge(zh_done, q + j + 1)
                for t in range(GT):
                    for k in range(KD):
                        last = nc.tensor.transpose(tp2[:, k, t * P:(t + 1) * P], zh[:, t, k * P:(k + 1) * P], ident[:])
                last.then_inc(zth_ready, 1)
                pe.wait_ge(zl_done, q + j + 1)
                pe.wait_ge(zTh_done, q + j + 1)
                for t in range(GT):
                    for k in range(KD):
                        last = nc.tensor.transpose(tp2[:, k, t * P:(t + 1) * P], zl[:, t, k * P:(k + 1) * P], ident[:])
                last.then_inc(ztl_ready, 1)
                pe.wait_ge(zTl_done, q + j + 1)
                for off, bk in ((O_WK, bank[2 + j]), (O_WV, bank[4 + j])):
                    for k in range(KD):
                        for i, (ws, zs) in enumerate(((wh, zTh), (wh, zTl), (wl, zTh))):
                            last = nc.tensor.matmul(bk[0:NST, :], W(ws, off + k * NST, NST), zs[:, k, :],
                                                    start=(k == 0 and i == 0), stop=(k == KD - 1 and i == 2))
                last.then_inc(kv_ready, 1)
            for j in range(2):
                pe.wait_ge(stl_done, q + j + 1)
                if j == 1:
                    pe.wait_ge(x_done, n + 2)
                for t in range(GT):
                    for i, (ss, ws) in enumerate(((sth, wh), (sth, wl), (stl, wh))):
                        last = nc.tensor.matmul(ybank[:, t // 2, (t % 2) * D:(t % 2 + 1) * D],
                                                ss[:, j, t * P:(t + 1) * P], W(ws, O_WO, D, NST),
                                                start=(i == 0), stop=(i == 2))
                last.then_inc(y_ready, 1)

        def act_round(act, n):
            act.wait_ge(n32_done, n + 1)
            if not isinstance(n, int) or n:
                act.wait_ge(th_ready, n)
            nc.scalar.copy(nh[:], n32[:]).then_inc(nh_done, 1)

        def act_high_out(act, n, g):
            act.wait_ge(th_ready, n + 1)
            nc.scalar.copy(xTh[:, :, tokens(g)], tp).then_inc(xTh_done, 1)

        def act_exp_routes(act, m):
            act.wait_ge(dl_done, m + 1)
            nc.scalar.activation(er[:], dl[:], ACT.Exp).then_inc(er_done, 1)

        def act_routes_out(act, m):
            act.wait_ge(ct_ready, m + 1)
            nc.scalar.copy(cT[:], tp[0:2 * NR, 0, :]).then_inc(cT_done, 1)

        def act_weights(act, r, j):
            act.wait_ge(w_in_done[j], 16 * (r + 1))
            nc.scalar.activation(wh[:, bass.ds((RING * r + j) * WCH, WCH)], stage[:, j, :], ACT.Copy,
                                 scale=WS).then_inc(w_high, 1)

        def act_ffn(act, f, steps):
            for c in range(FC):
                act.wait_ge(h_ready, FC * f + c + 1)
                nc.scalar.activation(hT[:, c, :], bank[2 + c % 4], ACT.Gelu, bias=small[:, S_B0 + c:S_B0 + c + 1],
                                     scale=1 / WS).then_inc(gelu_done, 1)
                for step in steps.get(c, ()):
                    step(act)

        def act_moe(act, m, steps):
            for c in range(MC):
                rows_ = P if c < MC - 1 else ML
                act.wait_ge(h1_ready, MC * m + c + 1)
                nc.scalar.activation(sg[0:rows_, c % 2, :], bank[2 + c % 2][0:rows_, :], ACT.Silu,
                                     scale=1 / WS).then_inc(silu_done, 1)
                act.wait_ge(u32_done, MC * m + c + 1)
                nc.scalar.copy(uh[0:rows_, c % 2, :], u32[0:rows_, c % 2, :]).then_inc(uh_done, 1)
                for step in steps.get(c, ()):
                    step(act)

        def act_wkv(act, q):
            for j in range(2):
                act.wait_ge(zn_done, q + j + 1)
                if j == 1:
                    act.wait_ge(zth_ready, q + 1)
                nc.scalar.copy(zh[:], zn[:]).then_inc(zh_done, 1)
                act.wait_ge(zth_ready, q + j + 1)
                if j == 1:
                    act.wait_ge(kv_ready, q + 1)
                nc.scalar.copy(zTh[:], tp2).then_inc(zTh_done, 1)
            for j in range(2):
                act.wait_ge(kv_ready, q + j + 1)
                nc.scalar.activation(ka[:], bank[2 + j][0:NST, :], ACT.Exp, scale=-1 / WS).then_inc(ek_done, 1)
                act.wait_ge(sig_done, q + j + 1)
                nc.scalar.activation(ev[:], kb[:], ACT.Exp, scale=nu[:]).then_inc(ev_done, 1)
                act.wait_ge(st_done, q + j + 1)
                nc.scalar.copy(sth[:, j, :], st32[:, j, :]).then_inc(sth_done, 1)

        def dve_normalise(dve, n, g, first=False):
            dve_moments(dve, n, g, first)
            dve_scale(dve, n, g)

        def dve_moments(dve, n, g, first=False):
            dve.wait_ge(x_done, 1 if first else n - 2)
            for t in range(GT):
                last = nc.vector.bn_stats(stat[:, t, :], x[:, tiles(g, t, 1), :])
            last.then_inc(stat_done, 1)
            dve.wait_ge(stat_done, n + 1)
            dve.sem_inc(wait_carrier, 1)
            for t in range(GT):
                last = nc.vector.bn_aggr(mv[:, t, :], stat[:, t, :])
            last.then_inc(aggr_done, 1)
            dve.wait_ge(aggr_done, n + 1)
            nc.vector.tensor_scalar(ve[:], mv[:, :, 1], EPS, None, ALU.add).then_inc(ve_done, 1)

        def dve_scale(dve, n, g):
            dve.wait_ge(rstd_done, n + 1)
            if not isinstance(n, int) or n:
                dve.wait_ge(nh_done, n)
            for t in range(GT):
                last = nc.vector.tensor_scalar(n32[:, t, :], x[:, tiles(g, t, 1), :], mv[:, t, 0:1], rstd[:, t:t + 1],
                                               ALU.subtract, ALU.mult)
            last.then_inc(n32_done, 1)

        def dve_low(dve, n, ns):
            dve.wait_ge(nh_done, n + 1)
            if not isinstance(ns, int) or ns:
                dve.wait_ge(tl_ready, ns)
            nc.vector.tensor_tensor(nl[:], n32[:], nh[:], ALU.subtract).then_inc(nl_done, 1)

        def dve_low_out(dve, ns, g):
            dve.wait_ge(tl_ready, ns + 1)
            nc.vector.tensor_copy(xTl[:, :, tokens(g)], tp).then_inc(xTl_done, 1)

        def dve_skip(dve, n, j):
            dve.wait_ge(n32_done, n + 1)
            nc.vector.tensor_tensor(R[:, j, :, :], n32[:], omg[:].unsqueeze(1).to_broadcast([P, GT, D]),
                                    ALU.mult).then_inc(R_done, 1)

        def dve_routes(dve, m):
            at = [0]

            def step(ins):
                at[0] += 1
                ins.then_inc(rt_step, 1)
                dve.wait_ge(rt_step, RT_STEPS * m + at[0])

            def wide(v, n=NE):
                return v.unsqueeze(2).to_broadcast([P, GT, n])

            dve.wait_ge(rt_ready, m + 1)
            step(nc.vector.tensor_scalar(lg[:], bank[0][:, 0:GT * NR].rearrange("p (t r) -> p t r", r=NR), 1 / WS,
                                         None, ALU.mult))
            step(nc.vector.tensor_reduce(mx[:], lg[:, :, 0:NE], AX.X, ALU.max))
            step(nc.vector.tensor_scalar(dl[:, :, NE:NR], lg[:, :, NE:NR], -1.0, None, ALU.mult))
            nc.vector.tensor_tensor(dl[:, :, 0:NE], lg[:, :, 0:NE], wide(mx[:]), ALU.subtract).then_inc(dl_done, 1)
            dve.wait_ge(er_done, m + 1)
            step(nc.vector.tensor_reduce(mx[:], er[:, :, 0:NE], AX.X, ALU.add))
            step(nc.vector.reciprocal(mx[:], mx[:]))
            step(nc.vector.tensor_tensor(prob[:], er[:, :, 0:NE], wide(mx[:]), ALU.mult))
            step(nc.vector.tensor_reduce(mx[:], prob[:], AX.X, ALU.max))
            step(nc.vector.tensor_tensor(s1[:], prob[:], wide(mx[:]), ALU.is_equal))
            step(nc.vector.tensor_tensor(pm[:], s1[:], order4, ALU.mult))
            step(nc.vector.tensor_reduce(mx[:], pm[:], AX.X, ALU.max))
            step(nc.vector.tensor_tensor(s1[:], pm[:], wide(mx[:]), ALU.is_equal))
            step(nc.vector.scalar_tensor_tensor(pm[:], s1[:], -2.0, prob[:], ALU.mult, ALU.add))
            step(nc.vector.tensor_reduce(mx[:], pm[:], AX.X, ALU.max))
            step(nc.vector.tensor_tensor(s2[:], pm[:], wide(mx[:]), ALU.is_equal))
            step(nc.vector.tensor_tensor(s2[:], s2[:], order4, ALU.mult))
            step(nc.vector.tensor_reduce(mx[:], s2[:], AX.X, ALU.max))
            assert at[0] == RT_STEPS
            nc.vector.tensor_tensor(s2[:], s2[:], wide(mx[:]), ALU.is_equal).then_inc(rt_sel, 1)
            dve.wait_ge(rt_sel, 4 * m + 1)
            nc.vector.tensor_tensor(s1[:], s1[:], s2[:], ALU.add).then_inc(rt_sel, 1)
            nc.vector.tensor_scalar(comb[:, :, NE:NR], er[:, :, NE:NR], 1.0, None, ALU.add).then_inc(rt_sel, 1)
            dve.wait_ge(rt_sel, 4 * m + 3)
            nc.vector.scalar_tensor_tensor(comb[:, :, 0:NE], s1[:], CS, prob[:], ALU.mult, ALU.mult)
            nc.vector.reciprocal(er[:, :, NE:NR], comb[:, :, NE:NR]).then_inc(rt_sel, 1)
            dve.wait_ge(rt_sel, 4 * m + 4)
            nc.vector.tensor_scalar(comb[:, :, NE:NR], er[:, :, NE:NR], CS, None, ALU.mult).then_inc(comb_done, 1)
            dve.wait_ge(comb_done, 2 * m + 1)
            if not isinstance(m, int) or m:
                dve.wait_ge(ct_ready, m)
            nc.vector.tensor_copy(ch[:, :, 0:NR], comb[:]).then_inc(comb_done, 1)
            dve.wait_ge(comb_done, 2 * m + 2)
            nc.vector.tensor_tensor(ch[:, :, NR:2 * NR], comb[:], ch[:, :, 0:NR], ALU.subtract).then_inc(ch_done, 1)

        def dve_weights(dve, r, j):
            dve.wait_ge(w_high, RING * r + j + 1)
            c = bass.ds((RING * r + j) * WCH, WCH)
            nc.vector.scalar_tensor_tensor(wl[:, c], stage[:, j, :], WS, wh[:, c], ALU.mult,
                                           ALU.subtract).then_inc(w_low, 1)

        def dve_ffn_sum(dve, n, f, g):
            dve.wait_ge(y_ready, n + 1)
            for h in range(2):
                nc.vector.scalar_tensor_tensor(t16[:, h, :].rearrange("p (t d) -> p t d", t=2),
                                               ybank[:, h, :].rearrange("p (t d) -> p t d", t=2), 1 / WS,
                                               row(R_B1, 2), ALU.mult, ALU.add).then_inc(t16_done, 1)
            for h in range(2):
                dve.wait_ge(t16_done, 2 * f + h + 1)
                xs = x[:, tiles(g, 2 * h, 2), :]
                last = nc.vector.scalar_tensor_tensor(xs, t16[:, h, :].rearrange("p (t d) -> p t d", t=2), 0.5, xs,
                                                      ALU.mult, ALU.add)
            last.then_inc(x_done, 1)

        def dve_sum(dve, n, g, factor):
            dve.wait_ge(y_ready, n + 1)
            for h in range(2):
                xs = x[:, tiles(g, 2 * h, 2), :]
                last = nc.vector.scalar_tensor_tensor(xs, ybank[:, h, :].rearrange("p (t d) -> p t d", t=2), factor, xs,
                                                      ALU.mult, ALU.add)
            last.then_inc(x_done, 1)

        def dve_moe(dve, m, steps):
            for c in range(MC):
                rows_ = P if c < MC - 1 else ML
                dve.wait_ge(silu_done, MC * m + c + 1)
                dve.wait_ge(C_ready, MC * m + c + 1)
                nc.vector.tensor_tensor(pr[0:rows_, c % 2, :], bank[4 + c % 2][0:rows_, :], sg[0:rows_, c % 2, :],
                                        ALU.mult).then_inc(pr_done, 1)
                dve.wait_ge(pr_done, MC * m + c + 1)
                nc.vector.tensor_tensor(u32[0:rows_, c % 2, :], bank[1][0:rows_, :], pr[0:rows_, c % 2, :],
                                        ALU.mult).then_inc(u32_done, 1)
                for step in steps.get(c, ()):
                    step(dve)

        def dve_wkv(dve, n, q, b):
            for j in range(2):
                dve.wait_ge(sh_ready, q + j + 1)
                for h in range(2):
                    last = nc.vector.tensor_tensor(z[:, 2 * h:2 * h + 2, :],
                                                   ybank[:, h, :].rearrange("p (t d) -> p t d", t=2),
                                                   gsc[:].unsqueeze(1).to_broadcast([P, 2, D]), ALU.mult)
                last.then_inc(z_read, 1)
                dve.wait_ge(z_read, q + j + 1)
                nc.vector.tensor_tensor(z[:], z[:], R[:, j, :, :], ALU.add).then_inc(wk_step, 1)
                dve.wait_ge(wk_step, 3 * (q + j) + 1)
                for t in range(GT):
                    last = nc.vector.bn_stats(stat[:, t, :], z[:, t, :])
                last.then_inc(wk_step, 1)
                dve.wait_ge(wk_step, 3 * (q + j) + 2)
                dve.sem_inc(wait_carrier, 1)
                for t in range(GT):
                    last = nc.vector.bn_aggr(mv[:, t, :], stat[:, t, :])
                last.then_inc(wk_step, 1)
                dve.wait_ge(wk_step, 3 * (q + j) + 3)
                nc.vector.tensor_scalar(zve[:], mv[:, :, 1], EPS, None, ALU.add).then_inc(zve_done, 1)
                for t in range(GT):
                    last = nc.vector.scalar_tensor_tensor(z[:, t, :], z[:, t, :], mv[:, t, 0:1], rows[:, R_GAM, :],
                                                          ALU.subtract, ALU.mult)
                last.then_inc(zg_done, 1)
                dve.wait_ge(zg_done, q + j + 1)
                dve.wait_ge(zrstd_done, q + j + 1)
                if j == 1:
                    dve.wait_ge(zh_done, q + 1)
                for t in range(GT):
                    last = nc.vector.scalar_tensor_tensor(zn[:, t, :], z[:, t, :], zrstd[:, t:t + 1], rows[:, R_BET, :],
                                                          ALU.mult, ALU.add)
                last.then_inc(zn_done, 1)
                dve.wait_ge(zh_done, q + j + 1)
                if j == 1:
                    dve.wait_ge(ztl_ready, q + 1)
                nc.vector.tensor_tensor(zl[:], zn[:], zh[:], ALU.subtract).then_inc(zl_done, 1)
                dve.wait_ge(ztl_ready, q + j + 1)
                if j == 1:
                    dve.wait_ge(kv_ready, q + 1)
                nc.vector.tensor_copy(zTl[:], tp2).then_inc(zTl_done, 1)
            for j in range(2):
                dve.wait_ge(ek_done, q + j + 1)
                nc.vector.tensor_scalar(kb[:], ka[:], 1.0, None, ALU.add).then_inc(wk2_step, 1)
                dve.wait_ge(wk2_step, 2 * (q + j) + 1)
                nc.vector.reciprocal(kb[:], kb[:]).then_inc(sig_done, 1)
                dve.wait_ge(ev_done, q + j + 1)
                nc.vector.scalar_tensor_tensor(wkv[:], bank[4 + j][0:NST, :], 1 / WS, ev[:], ALU.mult,
                                               ALU.mult).then_inc(wk2_step, 1)
                dve.wait_ge(wk2_step, 2 * (q + j) + 2)
                nc.vector.tensor_tensor_scan(st32[:, j, :], decayw[:], wkv[:],
                                             0.0 if j == 0 else st32[:, 0, GW - 1:GW], ALU.mult,
                                             ALU.add).then_inc(st_done, 1)
                dve.wait_ge(sth_done, q + j + 1)
                nc.vector.tensor_tensor(stl[:, j, :], st32[:, j, :], sth[:, j, :], ALU.subtract).then_inc(stl_done, 1)
            for j in range(2):
                dve_sum(dve, n + j, 2 * b + j, 1 / WS)

        def pool_root(pool, n, src, dst, src_done, dst_done):
            pool.wait_ge(src_done, n + 1)
            nc.gpsimd.tensor_tensor(dst[:], src[:], mhalf[:], ALU.pow).then_inc(dst_done, 1)

        def pool_moe(pool, m, steps):
            for c in range(MC):
                rows_ = P if c < MC - 1 else ML
                pool.wait_ge(uh_done, MC * m + c + 1)
                nc.gpsimd.tensor_tensor(ul[0:rows_, c % 2, :], u32[0:rows_, c % 2, :], uh[0:rows_, c % 2, :],
                                        ALU.subtract).then_inc(ul_done, 1)
                for step in steps.get(c, ()):
                    step(pool)


        STEPS = [(qc, kt) for qc in reversed(range(QC)) for kt in range(4 * (qc + 1))]
        NS = len(STEPS)
        HEAVY = MU // QC
        M_SLOTS = {}
        for v in range(MU):
            slot = 2 + 28 * v // HEAVY if v < HEAVY else 31 + 17 * (v - HEAVY) // HEAVY
            M_SLOTS.setdefault(slot, []).append(v)
        M_OUT = sum(len(vs) for slot, vs in M_SLOTS.items() if slot < QH * (4 * QC + 2))
        HALF = 4 * QC

        def span(s):
            qc, kt = STEPS[s]
            return max(0, kt * P - qc * 512)

        def pe_qkv(pe, n, ns, a, g):
            pe.wait_ge(xTh_done, n + 1)
            pe.wait_ge(xTl_done, ns + 1)
            for i, off in enumerate((O_AQ, O_AK)):
                for m in range(KD):
                    o = 2 * i + m
                    if o >= 2:
                        pe.wait_ge(p32_done, 4 * a + o - 1)
                    for k in range(KD):
                        for j, (ws, xs) in enumerate(((wh, xTh), (wh, xTl), (wl, xTh))):
                            last = nc.tensor.matmul(bank[2 + o % 2], W(ws, off + k * D + m * P, P),
                                                    xs[:, k, tokens(g)], start=(k == 0 and j == 0),
                                                    stop=(k == KD - 1 and j == 2))
                    last.then_inc(qk_ready, 1)
            pe.wait_ge(p32_done, 4 * a + 4)
            pe.wait_ge(v_done, a + 1)
            for t in range(GT):
                for j, (xs, ws) in enumerate(((xTh, wh), (xTh, wl), (xTl, wh))):
                    for k in range(KD):
                        last = nc.tensor.matmul(ybank[:, t // 2, (t % 2) * D:(t % 2 + 1) * D], xs[:, k, tokens(g, t, P)],
                                                W(ws, O_AV + k * D, D), start=(j == 0 and k == 0),
                                                stop=(j == 2 and k == KD - 1))
            last.then_inc(v_ready, 1)

        def act_qkv(act, a):
            for o in range(4):
                act.wait_ge(qk_ready, 4 * a + o + 1)
                act.wait_ge(pl_done, 4 * a + o + 1)
                q = o < 2
                m = o % 2
                nc.scalar.activation(p32[:, o % 2, :], bank[2 + o % 2], ACT.Identity,
                                     bias=bq4[:, m:m + 1] if q else small[:, S_BK + m:S_BK + m + 1],
                                     scale=SS / math.sqrt(DH) / WS if q else 1 / WS).then_inc(p32_done, 1)
                act.wait_ge(p32_done, 4 * a + o + 1)
                act.wait_ge(scratch_done[o % 2], 48 * (2 * a + o // 2 + 1))
                nc.scalar.copy(psplit[:, o % 2, 0, :], p32[:, o % 2, :]).then_inc(ph_done, 1)

        def dve_qkv(dve, a, b, j):
            for o in range(4):
                dve.wait_ge(ph_done, 4 * a + o + 1)
                nc.vector.tensor_tensor(psplit[:, o % 2, 1, :], p32[:, o % 2, :], psplit[:, o % 2, 0, :],
                                        ALU.subtract).then_inc(pl_done, 1)
            dve.wait_ge(v_ready, a + 1)
            for t in range(GT):
                for m in range(2):
                    last = nc.vector.scalar_tensor_tensor(
                        vals_by[:, bass.ds(2 * b + m, 1), j * GT + t, :, 0:DH].rearrange("p m h c -> p (m h) c"),
                        ybank[:, t // 2, (t % 2) * D + m * P:(t % 2) * D + (m + 1) * P].rearrange(
                            "p (h c) -> p h c", h=HH), 1 / WS,
                        rows[:, R_BV, m * P:(m + 1) * P].rearrange("p (h c) -> p h c", h=HH), ALU.mult, ALU.add)
            last.then_inc(v_done, 1)

        PLACES = (((0, 2), (1,)), ((0, 1), (2,)))

        def sp_qkv(sp, a, b, j):
            for o in range(4):
                for part, done in ((0, ph_done), (1, pl_done)):
                    sp.wait_ge(done, 4 * a + o + 1 + 2 * part)
                    for place in PLACES[o // 2][part]:
                        row0 = (4 + place * DH) * HH
                        dst = op_dram[o // 2, bass.ds(2 * b + o % 2, 1), row0:row0 + P, j * GW:(j + 1) * GW]
                        sp.dma_start(dst.rearrange("m r n -> r (m n)"),
                                     psplit[:, o % 2, part, :]).then_inc(scratch_done[o % 2], 16)

        def sp_load(sp, i, par, c, q, done):
            op = (qop, kop)[c]
            src = op_dram[c, bass.ds(i, 1), :, q * 512:(q + 1) * 512].rearrange("m (r h) n -> r (m h) n", h=HH)
            sp.dma_start(op[par][0:KR, q, :, :], src[:, par * QH:(par + 1) * QH, :]).then_inc(done, 16)

        def sp_load_upper(sp, i, par):
            sp_load(sp, i, par, 1, 1, op_in[par])
            sp_load(sp, i, par, 0, 1, op_in[par])

        def sp_load_lower(sp, i, par):
            sp_load(sp, i, par, 1, 0, op_in[par])
            sp_load(sp, i, par, 0, 0, ql_in[par])

        def block_of(v):
            return v % HEAVY // GT, GT * (QC - 1 - v // HEAVY) + v % GT

        def pe_max_block(pe, u, par, v):
            j, qt = block_of(v)
            pe.wait_ge(mx_done, MU * u + v + 1)
            dst = mid[:, 2 * (v % 2):2 * (v % 2) + 2, :]
            n = (qt + 1) * P
            for q in range(-(-n // 512)):
                w = min(512, n - q * 512)
                nc.tensor.matmul(dst[:, q, 0:w], qop[par][0:KM, qt // GT, j, (qt % GT) * P:(qt % GT + 1) * P],
                                 kop[par][0:KM, q, j, 0:w], start=True, stop=False, skip_group_check=True)
            nc.tensor.matmul(dst[:, qt // 4, (qt % 4) * P:(qt % 4 + 1) * P], ident[:], masks[:, 0, :],
                             start=False, stop=True, skip_group_check=True).then_inc(s_ready, 1)

        def dve_max_block(dve, u, v):
            qt = block_of(v)[1]
            dve.wait_ge(s_ready, MU * u + v + 1)
            flat = mid[:, 2 * (v % 2):2 * (v % 2) + 2, :].rearrange("p a b -> p (a b)")
            nc.vector.tensor_reduce(mxs[:, v:v + 1], flat[:, 0:(qt + 1) * P], AX.X, ALU.max).then_inc(mx_done, 1)

        def dve_max_end(dve, u, h):
            dve.wait_ge(mx_done, MU * u + (h + 1) * HEAVY + 2)
            if not isinstance(u, int) or u:
                dve.wait_ge(mt_ready, 2 * u - 1 + h)
            nc.vector.tensor_scalar(mneg[:, h, :], mxs[:, h * HEAVY:(h + 1) * HEAVY], -1.0, None,
                                    ALU.mult).then_inc(mneg_done, 1)

        def pe_max_end(pe, u, h):
            pe.wait_ge(mneg_done, 2 * u + h + 1)
            if h:
                pe.wait_ge(att_done, 2 * u + 1)
                pe.wait_ge(mT_done, 2 * u + 1)
            elif not isinstance(u, int) or u:
                pe.wait_ge(mT_done, 2 * u)
            nc.tensor.transpose(ybank[0:HEAVY, 1, 0:P // 2].bitcast(F16), mneg[:, h, :], ident[:]).then_inc(mt_ready, 1)

        def act_max_end(act, u, par, h):
            act.wait_ge(mt_ready, 2 * u + h + 1)
            nc.scalar.copy(mT[:, par, h, :], ybank[0:HEAVY, 1, 0:P // 2].bitcast(F16)).then_inc(mT_done, 1)

        def sp_max_row(sp, u, par, h):
            sp.wait_ge(mT_done, 2 * u + h + 1)
            sp.dma_start(qop[par][KM:KM + 1, QC - 1 - h, :, :].rearrange("p j c -> p (j c)"),
                         mT[:, par, h, :]).then_inc(m_in[par][h], 16)

        def pe_scores(pe, u, par, s, j):
            qc, kt = STEPS[s]
            c0 = span(s)
            e = QH * s + j
            pe.wait_ge(exp_done, QH * NS * u + e + 1)
            diag = kt >= 4 * qc
            last = nc.tensor.matmul(bank[e % 2][:, c0:512],
                                    kop[par][0:KM + 1, kt // GT, j, (kt % GT) * P:(kt % GT + 1) * P],
                                    qop[par][0:KM + 1, qc, j, c0:512], start=True, stop=not diag,
                                    skip_group_check=True)
            if diag:
                last = nc.tensor.matmul(bank[e % 2][:, c0:c0 + P], ident[:], masks[:, 1, :], start=False, stop=True,
                                        skip_group_check=True)
            last.then_inc(st_ready, 1)

        def act_exp(act, u, s):
            c0 = span(s)
            act.wait_ge(pv_done, NS * u + s + 1)
            for j in range(QH):
                e = QH * s + j
                act.wait_ge(st_ready, QH * NS * u + e + 1)
                nc.scalar.activation(prob_t[:, s % 2, j, c0:512], bank[e % 2][:, c0:512], ACT.Exp,
                                     scale=1 / SS).then_inc(exp_done, 1)

        def pe_values(pe, u, par, s):
            qc, kt = STEPS[s]
            c0 = span(s)
            pe.wait_ge(exp_done, QH * NS * u + QH * (s + 1) + 2)
            for j in range(QH):
                last = nc.tensor.matmul(ybank[32 * j:32 * j + VW, 0, c0:512],
                                        vq[:, par, kt, j * VW:(j + 1) * VW],
                                        prob_t[:, s % 2, j, c0:512], start=(kt == 0), stop=(kt == 4 * qc + 3),
                                        skip_group_check=True)
            last.then_inc(pv_done, 1)

        def act_out(act, u, i):
            act.wait_ge(pv_done, NS * u + (HALF, NS)[i] + 2)
            nc.scalar.copy(o32, ybank[:, 0, :]).then_inc(o32_done, 1)

        def pe_out(pe, u, i):
            pe.wait_ge(o32_done, 2 * u + i + 1)
            for t in range(GT):
                last = nc.tensor.transpose(ybank[:, 1, t * P:(t + 1) * P], o32[:, t * P:(t + 1) * P], ident32[:])
            last.then_inc(ot_ready, 1)

        def dve_out(dve, u, i):
            dve.wait_ge(ot_ready, 2 * u + i + 1)
            ot = ybank[:, 1, :].rearrange("p (t j c) -> p t j c", t=GT, j=QH)
            nc.vector.reciprocal(rec[:], ot[:, :, :, DH]).then_inc(rec_done, 1)
            dve.wait_ge(rec_done, 2 * u + i + 1)
            dst = att[:, bass.ds(u * TT + (QC - 1 - i) * GT, GT), :].rearrange("p t (j c) -> p t j c", j=QH)
            nc.vector.tensor_tensor(dst, ot[:, :, :, 0:DH], rec[:].unsqueeze(3).to_broadcast([P, GT, QH, DH]),
                                    ALU.mult).then_inc(att_done, 1)

        def pe_unit(pe, u, par, i, nxt=True):
            pe.wait_ge(vq_done, u + 1)
            pe.wait_ge(m_in[par][0], 16 * (i + 1))
            for s in range(NS):
                if s == HALF:
                    pe.wait_ge(m_in[par][1], 16 * (i + 1))
                for j in range(QH):
                    pe_scores(pe, u, par, s, j)
                    for v in M_SLOTS.get(QH * s + j, ()) if nxt else ():
                        if v == 0:
                            pe.wait_ge(op_in[1 - par], 48 * (i + par + 1))
                        if v == HEAVY:
                            pe.wait_ge(ql_in[1 - par], 16 * (i + par + 1))
                        pe_max_block(pe, u + 1, 1 - par, v)
                if s == 1:
                    pe_max_end(pe, u, 1)
                if s == HALF and nxt:
                    pe_max_end(pe, u + 1, 0)
                if s == HALF + 1:
                    pe.wait_ge(mT_done, 2 * u + (3 if nxt else 2))
                    pe_out(pe, u, 0)
                if s >= 1:
                    pe_values(pe, u, par, s - 1)
            pe_values(pe, u, par, NS - 1)
            pe.wait_ge(att_done, 2 * u + 2)
            pe_out(pe, u, 1)

        def act_unit(act, u, par, nxt=True):
            for s in range(NS):
                act_exp(act, u, s)
                if s == 1:
                    act_max_end(act, u, par, 1)
                if s == HALF:
                    if nxt:
                        act_max_end(act, u + 1, 1 - par, 0)
                    act_out(act, u, 0)
            act_out(act, u, 1)

        def dve_unit(dve, u, nxt=True):
            if nxt:
                for v in range(HEAVY):
                    dve_max_block(dve, u + 1, v)
                dve_max_end(dve, u + 1, 0)
                for v in range(HEAVY, M_OUT):
                    dve_max_block(dve, u + 1, v)
            dve_out(dve, u, 0)
            if nxt:
                for v in range(M_OUT, MU):
                    dve_max_block(dve, u + 1, v)
                dve_max_end(dve, u + 1, 1)
            dve_out(dve, u, 1)

        def pe_att_project(pe, n, a, g):
            pe.wait_ge(ah_done, a + 1)
            for t in range(GT):
                for k in range(KD):
                    last = nc.tensor.transpose(tp[:, k, t * P:(t + 1) * P], nh[:, t, k * P:(k + 1) * P], ident[:])
            last.then_inc(ath_ready, 1)
            pe.wait_ge(al_done, a + 2)
            pe.wait_ge(aTh_done, a + 1)
            for t in range(GT):
                for k in range(KD):
                    last = nc.tensor.transpose(tp[:, k, t * P:(t + 1) * P], nl[:, t, k * P:(k + 1) * P], ident[:])
            last.then_inc(atl_ready, 1)
            pe.wait_ge(aTl_done, a + 1)
            pe.wait_ge(x_done, n + 1)
            for t in range(GT):
                for j, (xs, ws) in enumerate(((xTh, wh), (xTh, wl), (xTl, wh))):
                    for k in range(KD):
                        last = nc.tensor.matmul(ybank[:, t // 2, (t % 2) * D:(t % 2 + 1) * D], xs[:, k, tokens(g, t, P)],
                                                W(ws, O_AO + k * D, D), start=(j == 0 and k == 0),
                                                stop=(j == 2 and k == KD - 1))
            last.then_inc(y_ready, 1)

        def att_rows(b, j):
            return att[:, bass.ds(b * (H // QH) * TT, H // QH * TT), :].rearrange(
                "p (q t) c -> p t q c", t=TT)[:, j * GT:(j + 1) * GT, :, :]

        def quads(v):
            return v[:].rearrange("p t (q c) -> p t q c", c=QH * DH)

        def act_att_project(act, a, b, j):
            act.wait_ge(al_done, a + 1)
            act.wait_ge(att_done, 2 * NQ + 1)
            for t in range(GT):
                last = nc.scalar.copy(quads(nh)[:, t], att_rows(b, j)[:, t])
            last.then_inc(ah_done, 1)
            act.wait_ge(ath_ready, a + 1)
            nc.scalar.copy(xTh[:, :, tokens(2 * b + j)], tp).then_inc(aTh_done, 1)

        def dve_att_project(dve, n, a, b, j):
            dve.wait_ge(ah_done, a + 1)
            nc.vector.tensor_tensor(quads(nl), att_rows(b, j), quads(nh), ALU.subtract).then_inc(al_done, 1)
            dve.wait_ge(atl_ready, a + 1)
            nc.vector.tensor_copy(xTl[:, :, tokens(2 * b + j)], tp).then_inc(aTl_done, 1)
            dve.wait_ge(y_ready, n + 1)
            for h in range(2):
                last = nc.vector.scalar_tensor_tensor(n32[:, 2 * h:2 * h + 2, :],
                                                      ybank[:, h, :].rearrange("p (t d) -> p t d", t=2), 1 / WS,
                                                      row(R_BO, 2), ALU.mult, ALU.add)
            last.then_inc(ob_done, 1)
            dve.wait_ge(ob_done, a + 1)
            xs = x[:, tiles(2 * b + j), :]
            nc.vector.tensor_tensor(xs, xs, n32[:], ALU.add).then_inc(x_done, 1)

        SPLIT = {4: 0, 8: 4, 12: 5, 16: 9, 20: 13}

        def moe_prepare(parts, at):
            return {at + c: [step] for c, step in parts.items()}

        def merged(*lists):
            out = {}
            for steps in lists:
                for c, todo in steps.items():
                    out.setdefault(c, []).extend(todo)
            return out

        def pe_next(n, ns):
            return {3: lambda e: pe_transpose_high(e, n), 5: lambda e: pe_transpose_low(e, n, ns)}

        def act_next(n, g):
            return {1: lambda e: act_round(e, n), 3: lambda e: act_high_out(e, n, g)}

        def dve_next(n, ns, g):
            return {0: lambda e: dve_moments(e, n, g), 1: lambda e: dve_scale(e, n, g),
                    2: lambda e: dve_low(e, n, ns), 5: lambda e: dve_low_out(e, ns, g)}

        def pool_next(n):
            return {0: lambda e: pool_root(e, n, ve, rstd, ve_done, rstd_done)}

        LAST_AT = [1 + 5 * k for k in range(NG - 1)]

        block = ctx.enter_context(nc.Block())

        @block.sync
        def _(sp):
            for j in range(RING):
                sp.dma_start(stage[:, j, :], w_in[:, j * WCH:(j + 1) * WCH]).then_inc(w_in_done[j], 16)
            sp.dma_start(rows[:], rows_in).then_inc(const_done, 16)
            sp.dma_start(sel[:], sel_in).then_inc(const_done, 16)
            sp.dma_start(order[:], order_in).then_inc(const_done, 16)
            sp.dma_start(masks[:], masks_in).then_inc(const_done, 16)
            with sp.Fori(1, NWG) as r:
                for j in range(RING):
                    sp.wait_ge(w_low, RING * r + j - (RING - 1))
                    sp.dma_start(stage[:, j, :], w_in[:, bass.ds((RING * r + j) * WCH, WCH)]).then_inc(w_in_done[j], 16)
            sp.wait_ge(x_done, 17)
            for c in range(2):
                sp.dma_start(op_dram[c, :, 0:4 * HH, :], alibi_in[c]).then_inc(pos_done, 16)
                sp.sem_inc(scratch_done[c], 48)
            with sp.Fori(0, B) as b:
                for j in range(2):
                    sp_qkv(sp, 2 * b + j, b, j)
            sp.wait_ge(pos_done, 32)
            for par in range(2):
                sp.wait_ge(scratch_done[par], 48 * (2 * NG + 1))
            for par in range(2):
                sp.wait_ge(fill_done, 2 * par + 2)
                sp_load_upper(sp, 0, par)
                sp_load_lower(sp, 0, par)
            sp_max_row(sp, 0, 0, 0)
            sp_max_row(sp, 0, 0, 1)
            with sp.Fori(0, NQ // 2 - 1) as i:
                for par in range(2):
                    u = 2 * i + par
                    sp.wait_ge(st_ready, QH * (NS * u + HALF))
                    sp_load_upper(sp, i + 1, par)
                    sp_max_row(sp, u + 1, 1 - par, 0)
                    sp.wait_ge(st_ready, QH * NS * (u + 1))
                    sp_load_lower(sp, i + 1, par)
                    sp_max_row(sp, u + 1, 1 - par, 1)
            sp_max_row(sp, NQ - 1, 1, 0)
            sp_max_row(sp, NQ - 1, 1, 1)
            for g in range(NG):
                sp.wait_ge(x_done, 22 + g)
                sp.dma_start(out[g * GW:(g + 1) * GW, :].rearrange("(t p) d -> p t d", p=P),
                             x[:, g * GT:(g + 1) * GT, :]).then_inc(out_done, 16)
            sp.wait_ge(out_done, 16 * NG)

        @block.gpsimd
        def _(pool):
            nc.gpsimd.memset(mhalf[:], -0.5).then_inc(pool_set, 1)
            pool.wait_ge(pool_set, 1)
            with pool.Fori(0, 5) as n:
                pool_root(pool, n, ve, rstd, ve_done, rstd_done)
            with pool.Fori(0, B) as b:
                pool_root(pool, 5 + 2 * b, ve, rstd, ve_done, rstd_done)
                for j in range(2):
                    pool_root(pool, 2 * b + j, zve, zrstd, zve_done, zrstd_done)
                pool_root(pool, 6 + 2 * b, ve, rstd, ve_done, rstd_done)
            with pool.Fori(9, 13) as n:
                pool_root(pool, n, ve, rstd, ve_done, rstd_done)
            with pool.Fori(0, NG - 1) as g:
                pool_moe(pool, g, moe_prepare(pool_next(13 + g), 1))
            pool_moe(pool, NG - 1, merged(*[moe_prepare(pool_next(16 + k), at) for k, at in enumerate(LAST_AT)]))
            pool.wait_ge(x_done, 17)
            nc.gpsimd.memset(kop[0], 1.0).then_inc(fill_done, 1)
            nc.gpsimd.memset(qop[0], 0.0).then_inc(fill_done, 1)
            pool_root(pool, 19, ve, rstd, ve_done, rstd_done)

            def pool_values(i, par):
                nc.gpsimd.tensor_copy(vq[:, par, :, :],
                                      vals_by[:, bass.ds(i, 1), :, par * QH:(par + 1) * QH, :].rearrange(
                                          "p m t h c -> p (m t) (h c)")).then_inc(vq_done, 1)

            pool.wait_ge(v_done, NG + 1)
            nc.gpsimd.memset(kop[1], 1.0).then_inc(fill_done, 1)
            nc.gpsimd.memset(qop[1], 0.0).then_inc(fill_done, 1)
            pool.wait_ge(vones_done, 1)
            for par in range(2):
                pool_values(0, par)
            with pool.Fori(0, NQ // 2 - 1) as i:
                for par in range(2):
                    pool.wait_ge(pv_done, NS * (2 * i + par + 1) + 2)
                    pool_values(i + 1, par)
            pool_root(pool, 20, ve, rstd, ve_done, rstd_done)
            with pool.Fori(0, NG - 1) as g:
                pool_moe(pool, NG + g, moe_prepare(pool_next(21 + g), 1))
            pool_moe(pool, 2 * NG - 1, {})

        @block.tensor
        def _(pe):
            pe.sem_inc(pv_done, 2)
            pe.wait_ge(early_done, 2 * 16)
            pe_transpose_high(pe, 0)
            pe.wait_ge(w_low, 3)
            with pe.Fori(0, NG - 1) as g:
                pe_ffn(pe, g, g, g, {5: [lambda e: pe_transpose_high(e, g + 1)]})
            pe_ffn(pe, 3, 3, 3, {5: [lambda e: pe_transpose_high(e, 4)], 7: [lambda e: pe_transpose_low(e, 4, 0)]})
            with pe.Fori(0, B) as b:
                pe.wait_ge(xTl_done, 2 * b + 1)
                pe_transpose_high(pe, 5 + 2 * b)
                pe_transpose_low(pe, 5 + 2 * b, 1 + 2 * b)
                pe_wkv(pe, 4 + 2 * b, 2 * b, 2 * b, b)
                pe_transpose_high(pe, 6 + 2 * b)
                pe_transpose_low(pe, 6 + 2 * b, 2 + 2 * b)
            pe.wait_ge(xTl_done, SPLIT[8] + 1)
            with pe.Fori(0, NG - 1) as g:
                pe_ffn(pe, 8 + g, 4 + g, g, {5: [lambda e: pe_transpose_high(e, 9 + g)]})
            pe_ffn(pe, 11, 7, 3, {5: [lambda e: pe_transpose_high(e, 12)],
                                  7: [lambda e: pe_transpose_low(e, 12, SPLIT[12])]})
            pe.wait_ge(const_done, 4 * 16)

            def pe_moe_layer(n0, m0, last):
                s0 = SPLIT[n0]
                pe_router(pe, s0, 0)
                pe_transpose_routes(pe, m0)
                with pe.Fori(0, NG - 1) as g:
                    pe_moe(pe, n0 + g, s0 + g, m0 + g, g, merged(
                        moe_prepare(pe_next(n0 + g + 1, s0 + g + 1), 1),
                        {8: [lambda e: pe_router(e, s0 + g + 1, g + 1)],
                         14: [lambda e: pe_transpose_routes(e, m0 + g + 1)]}))
                pe_moe(pe, n0 + NG - 1, s0 + NG - 1, m0 + NG - 1, NG - 1, last)

            pe_moe_layer(12, 0, merged(*[moe_prepare(pe_next(16 + k, SPLIT[16] + k), at)
                                         for k, at in enumerate(LAST_AT)]))
            pe.wait_ge(xTl_done, SPLIT[16] + 3)
            pe_transpose_high(pe, 19)
            pe_transpose_low(pe, 19, SPLIT[16] + 3)
            pe.wait_ge(x_done, 17)
            with pe.Fori(0, NG) as g:
                pe_qkv(pe, 16 + g, SPLIT[16] + g, g, g)
            pe.wait_ge(v_done, NG + 1)
            pe.wait_ge(op_in[0], 48)
            pe.wait_ge(ql_in[0], 16)
            for v in range(MU):
                pe_max_block(pe, 0, 0, v)
            pe_max_end(pe, 0, 0)
            pe.wait_ge(vones_done, 1)
            with pe.Fori(0, NQ // 2 - 1) as i:
                pe_unit(pe, 2 * i, 0, i)
                pe_unit(pe, 2 * i + 1, 1, i)
            pe_unit(pe, NQ - 2, 0, NQ // 2 - 1)
            pe_unit(pe, NQ - 1, 1, NQ // 2 - 1, nxt=False)
            with pe.Fori(0, NG) as g:
                pe_att_project(pe, 16 + g, g, g)
            pe_transpose_high(pe, 20)
            pe_transpose_low(pe, 20, SPLIT[20])
            pe_moe_layer(20, NG, {})

        @block.scalar
        def _(act):
            def load_rows(g, done):
                act.dma_start(x[:, g * GT:(g + 1) * GT, :],
                              x_in[g * GW:(g + 1) * GW, :].rearrange("(t p) d -> p t d", p=P)).then_inc(done, 16)

            load_rows(0, x0_in_done)
            act.dma_start(ident[:], ident_in).then_inc(early_done, 16)
            act.dma_start(small[:], small_in).then_inc(early_done, 16)
            for g in range(1, NG):
                load_rows(g, x_in_done)
            act.sem_inc(exp_done, 2)
            act_weights(act, 0, 0)
            act_weights(act, 0, 1)
            act_round(act, 0)
            act_high_out(act, 0, 0)
            act_weights(act, 0, 2)
            act_weights(act, 0, 3)
            act.wait_ge(early_done, 2 * 16)

            def act_next_weights(r):
                return {c: [lambda e, j=j: act_weights(e, r, j)] for j, c in enumerate((0, 2, 4, 6))}

            with act.Fori(0, NG - 1) as g:
                act_ffn(act, g, merged(act_next_weights(g + 1), {
                    3: [lambda e: act_round(e, g + 1)], 6: [lambda e: act_high_out(e, g + 1, g + 1)]}))
            act.wait_ge(const_done, 4 * 16)
            nc.scalar.activation(eg[:], rows[:, R_G, :], ACT.Exp, scale=-1.0).then_inc(act_set, 1)
            nc.scalar.activation(decay[:], small[0:NST, S_LW:S_LW + 1], ACT.Exp).then_inc(act_set, 1)
            nc.scalar.activation(nu[:], small[0:NST, S_U:S_U + 1], ACT.Exp).then_inc(act_set, 1)
            nc.scalar.activation(bq4[:], small[:, S_BQ:S_BQ + KD], ACT.Copy, scale=SS / math.sqrt(DH)).then_inc(act_set, 1)
            nc.scalar.copy(ident32[:], ident[:]).then_inc(act_set, 1)
            act_ffn(act, 3, merged(act_next_weights(4), {
                3: [lambda e: act_round(e, 4)], 6: [lambda e: act_high_out(e, 4, 0)]}))
            act.wait_ge(set_done, 4)
            with act.Fori(0, B) as b:
                act_round(act, 5 + 2 * b)
                act_high_out(act, 5 + 2 * b, 2 * b + 1)
                act_wkv(act, 2 * b)
                act_round(act, 6 + 2 * b)
                act_high_out(act, 6 + 2 * b, (2 * b + 2) % NG)
            with act.Fori(0, NG - 1) as g:
                act_ffn(act, g + 4, {3: [lambda e: act_round(e, g + 9)], 6: [lambda e: act_high_out(e, g + 9, g + 1)]})
            act_ffn(act, 7, {3: [lambda e: act_round(e, 12)], 6: [lambda e: act_high_out(e, 12, 0)]})

            def act_moe_layer(n0, m0, last):
                act_exp_routes(act, m0)
                act_routes_out(act, m0)
                with act.Fori(0, NG - 1) as g:
                    act_moe(act, m0 + g, merged(
                        moe_prepare(act_next(n0 + g + 1, g + 1), 1),
                        {8: [lambda e: act_exp_routes(e, m0 + g + 1)],
                         MC - 1: [lambda e: act_routes_out(e, m0 + g + 1)]}))
                act_moe(act, m0 + NG - 1, last)

            act_moe_layer(12, 0, merged(*[moe_prepare(act_next(16 + k, k), at) for k, at in enumerate(LAST_AT)]))
            act_round(act, 19)
            act_high_out(act, 19, 3)
            with act.Fori(0, NG) as a:
                act_qkv(act, a)
            act_max_end(act, 0, 0, 0)
            with act.Fori(0, NQ // 2 - 1) as i:
                act_unit(act, 2 * i, 0)
                act_unit(act, 2 * i + 1, 1)
            act_unit(act, NQ - 2, 0)
            act_unit(act, NQ - 1, 1, nxt=False)
            with act.Fori(0, B) as b:
                for j in range(2):
                    act_att_project(act, 2 * b + j, b, j)
            act_round(act, 20)
            act_high_out(act, 20, 0)
            act_moe_layer(20, NG, {})

        @block.vector
        def _(dve):
            nc.vector.memset(decayw[:], 1.0).then_inc(set_done, 1)
            dve.sem_inc(x_done, 1)
            dve.sem_inc(mx_done, 2)
            dve.sem_inc(pl_done, 2)
            dve.sem_inc(v_done, 1)
            dve.sem_inc(al_done, 1)
            dve.sem_inc(att_done, 1)
            dve.wait_ge(x0_in_done, 16)
            dve_normalise(dve, 0, 0, first=True)
            for j in range(RING):
                dve_weights(dve, 0, j)
            dve.wait_ge(x_in_done, 16 * (NG - 1))
            dve.wait_ge(const_done, 4 * 16)
            with dve.Fori(0, NG - 1) as g:
                dve_moments(dve, g + 1, g + 1, first=True)
                dve_weights(dve, g + 1, 0)
                dve_scale(dve, g + 1, g + 1)
                for j in range(1, RING):
                    dve_weights(dve, g + 1, j)
                dve_ffn_sum(dve, g, g, g)
            dve.wait_ge(act_set, 5)
            nc.vector.tensor_scalar(gsc[:], eg[:], 1.0, None, ALU.add).then_inc(set_done, 1)
            dve.wait_ge(set_done, 2)
            nc.vector.tensor_scalar(decayw[:], decayw[:], decay[:], None, ALU.mult).then_inc(set_done, 1)
            nc.vector.tensor_scalar(nu[:], nu[:], -1.0, None, ALU.mult).then_inc(set_done, 1)
            nc.vector.reciprocal(gsc[:], gsc[:]).then_inc(set_done, 1)
            dve.wait_ge(set_done, 5)
            nc.vector.tensor_scalar(omg[:], gsc[:], -1.0, 1.0, ALU.mult, ALU.add).then_inc(set_done, 1)
            dve.wait_ge(set_done, 6)
            nc.vector.tensor_scalar(gsc[:], gsc[:], 1 / WS, None, ALU.mult).then_inc(set_done, 1)
            dve.wait_ge(set_done, 7)
            dve_moments(dve, 4, 0)
            dve_weights(dve, 4, 0)
            dve_scale(dve, 4, 0)
            for j in range(1, RING):
                dve_weights(dve, 4, j)
            dve_low(dve, 4, 0)
            dve_skip(dve, 4, 0)
            dve_low_out(dve, 0, 0)
            dve_ffn_sum(dve, 3, 3, 3)
            with dve.Fori(0, B) as b:
                dve_normalise(dve, 5 + 2 * b, 2 * b + 1)
                dve_low(dve, 5 + 2 * b, 1 + 2 * b)
                dve_skip(dve, 5 + 2 * b, 1)
                dve_low_out(dve, 1 + 2 * b, 2 * b + 1)
                dve_wkv(dve, 4 + 2 * b, 2 * b, b)
                dve_normalise(dve, 6 + 2 * b, (2 * b + 2) % NG)
                dve_low(dve, 6 + 2 * b, 2 + 2 * b)
                dve_skip(dve, 6 + 2 * b, 0)
                dve_low_out(dve, 2 + 2 * b, (2 * b + 2) % NG)
            with dve.Fori(0, NG - 1) as g:
                dve_normalise(dve, g + 9, g + 1)
                dve_ffn_sum(dve, 8 + g, 4 + g, g)
            dve_normalise(dve, 12, 0)
            dve_low(dve, 12, SPLIT[12])
            dve_low_out(dve, SPLIT[12], 0)
            dve_ffn_sum(dve, 11, 7, 3)

            def dve_moe_layer(n0, m0, last):
                s0 = SPLIT[n0]
                dve_routes(dve, m0)
                with dve.Fori(0, NG - 1) as g:
                    dve_moe(dve, m0 + g, merged(
                        moe_prepare(dve_next(n0 + g + 1, s0 + g + 1, g + 1), 1),
                        {8: [lambda e: dve_routes(e, m0 + g + 1)]}))
                    dve_sum(dve, n0 + g, g, 0.5 / (WS * US))
                dve_moe(dve, m0 + NG - 1, last)
                dve_sum(dve, n0 + NG - 1, NG - 1, 0.5 / (WS * US))

            dve_moe_layer(12, 0, merged(*[moe_prepare(dve_next(16 + k, SPLIT[16] + k, k), at)
                                          for k, at in enumerate(LAST_AT)]))
            dve_normalise(dve, 19, 3)
            dve_low(dve, 19, SPLIT[16] + 3)
            dve_low_out(dve, SPLIT[16] + 3, 3)
            nc.vector.memset(vals.rearrange("p (r c) -> p r c", c=VW)[:, :, DH:VW], 1.0).then_inc(vones_done, 1)
            with dve.Fori(0, B) as b:
                for j in range(2):
                    dve_qkv(dve, 2 * b + j, b, j)
            for h in range(2):
                for v in range(h * HEAVY, (h + 1) * HEAVY):
                    dve_max_block(dve, 0, v)
                dve_max_end(dve, 0, h)
            with dve.Fori(0, NQ // 2 - 1) as i:
                dve_unit(dve, 2 * i)
                dve_unit(dve, 2 * i + 1)
            dve_unit(dve, NQ - 2)
            dve_unit(dve, NQ - 1, nxt=False)
            with dve.Fori(0, B) as b:
                for j in range(2):
                    dve_att_project(dve, 16 + 2 * b + j, 2 * b + j, b, j)
            dve_normalise(dve, 20, 0)
            dve_low(dve, 20, SPLIT[20])
            dve_low_out(dve, SPLIT[20], 0)
            dve_moe_layer(20, NG, {})


def packed(i):
    def cols(w, chunks):
        return w.reshape(chunks, P, -1).transpose(1, 0, 2).reshape(P, -1)

    by_dim = np.arange(D).reshape(2, HH, DH).transpose(0, 2, 1).reshape(D)
    fc1 = np.concatenate([i["L1_ffn_expert_fc1"].reshape(NE * FE, D), i["L1_ffn_shared_fc1"]], 0).T
    fc2 = np.concatenate([i["L1_ffn_expert_fc2"].reshape(NE * FE, D), i["L1_ffn_shared_fc2"]], 0).T
    proj = np.zeros((MC * P, D), np.float32)
    proj[0:NE * FE] = i["L1_ffn_expert_proj"].transpose(0, 2, 1).reshape(NE * FE, D)
    proj[NE * FE:FM] = i["L1_ffn_shared_proj"].T
    w = np.zeros((P, WCOLS), np.float32)
    for at, part in ((O_W0, cols(i["L0_ffn_W0"].T, KD)), (O_W1, cols(i["L0_ffn_W1"].T, FC)),
                     (O_SH, cols(i["L0_attn_W_shift"].T, KD)), (O_WK, cols(i["L0_attn_W_key"].T, KD)),
                     (O_WV, cols(i["L0_attn_W_value"].T, KD)),
                     (O_RT, cols(np.concatenate([i["L1_ffn_gate_w"], i["L1_ffn_shared_gate_w"]], 0).T, KD)),
                     (O_F1, cols(fc1, KD)), (O_F2, cols(fc2, KD)), (O_PR, cols(proj, MC)),
                     (O_AQ, cols(i["L1_attn_Wq"][by_dim].T, KD)),
                     (O_AK, cols(i["L1_attn_Wk"][by_dim].T, KD)),
                     (O_AV, cols(i["L1_attn_Wv"].T, KD)), (O_AO, cols(i["L1_attn_Wo"].T, KD))):
        w[:, at:at + part.shape[1]] = part
    w[0:NST, O_WO:O_WO + D] = i["L0_attn_W_output"].T
    small = np.zeros((P, SCOLS), np.float32)
    small[:, S_B0:S_B0 + FC] = i["L0_ffn_bias0"].reshape(FC, P).T
    small[0:NST, S_LW] = i["L0_attn_time_decay"]
    small[0:NST, S_U] = i["L0_attn_time_first"]
    small[:, S_BQ:S_BQ + KD] = i["L1_attn_bq"][by_dim].reshape(KD, P).T
    small[:, S_BK:S_BK + KD] = i["L1_attn_bk"][by_dim].reshape(KD, P).T
    rows = np.stack([i["L0_ffn_bias1"], i["L0_attn_gate"], i["L0_attn_ln_gamma"], i["L0_attn_ln_beta"],
                     i["L1_attn_bv"], i["L1_attn_bo"]])
    rows = np.broadcast_to(rows, (P,) + rows.shape)
    ident = np.eye(P, dtype=np.float16)
    sel = np.zeros((2 * NR, MC * P), np.float16)
    for j in range(FM):
        e = min(j // FE, NE)
        sel[e, j] = sel[NR + e, j] = SEL
    order = np.broadcast_to(np.arange(NE, 0, -1, dtype=np.float32), (P, NE))
    upper = np.triu(np.full((P, P), MASK, np.float16), 1)
    masks = np.stack([upper, upper.T], 1)
    slopes = np.array([2.0 ** (-0.5 * (h + 1)) for h in range(H)], np.float32)
    scaled = np.tile(slopes, B).astype(np.float64) * SS
    high = scaled.astype(np.float16)
    low = ((scaled - high) * T).astype(np.float16)
    pos = np.arange(T)
    alibi = np.zeros((2, 4, B * H, T), np.float16)
    alibi[0, 0], alibi[0, 2] = high[:, None], low[:, None]
    alibi[0, 1], alibi[0, 3] = -pos, -pos / T
    alibi[1, 0], alibi[1, 2] = pos, pos / T
    alibi[1, 1], alibi[1, 3] = high[:, None], low[:, None]
    alibi = alibi.reshape(2, 4, 2 * B, HH, T).transpose(0, 2, 1, 3, 4).reshape(2, 2 * B, 4 * HH, T)
    return {"x": i["L0_attn_x"].reshape(B * T, D), "w": w, "small": small, "rows": rows, "ident": ident, "sel": sel,
            "order": order, "masks": masks, "alibi": alibi}


def kernel(**inputs):
    import concourse.bacc as bacc
    from concourse.bass_utils import run_bass_kernel_spmd

    nc = bacc.Bacc("TRN2", target_bir_lowering=False, num_devices=1)
    arrays = {f"in_{k}": np.ascontiguousarray(v) for k, v in packed(inputs).items()}
    args = [nc.dram_tensor(k, a.shape, mybir.dt.from_np(a.dtype), kind="ExternalInput").ap() for k, a in arrays.items()]
    out = nc.dram_tensor("out_x", (B * T, D), F32, kind="ExternalOutput").ap()
    block_kernel(nc, *args, out)
    r = run_bass_kernel_spmd(nc, [arrays], core_ids=[0])
    return r.results[0]["out_x"].reshape(B, T, D)
```

```python
from contextlib import ExitStack
import math

import numpy as np

import concourse.bass as bass
from concourse import mybir

F32, F16 = mybir.dt.float32, mybir.dt.float16
ALU, ACT, AX = mybir.AluOpType, mybir.ActivationFunctionType, mybir.AxisListType

P = 128
B, T, D = 2, 1024, 256
KD = D // P
GT = 4
GW = GT * P
NG = B * T // GW
FF = 1024
FC = FF // P
NST = 64
NE, FE, FS = 8, 176, 704
FM = NE * FE + FS
MC = -(-FM // P)
EC = NE * FE // P
assert EC * P == NE * FE
FB = (MC - 1) * P
ML = FM - FB
NR = NE + 1
H = 16
DH = D // H
TT = T // P
HH = H // 2
QH = 4
NQ = B * H // QH
VW = DH + 1
KR = 4 + 3 * DH
KM = 96
QC = T // 512
MU = QH * TT
SS = 16.0
MASK = -60000.0
EPS = 1e-5

WS = 2.0 ** 8
US = 2.0 ** 4
CS = 2.0 ** 8
SEL = US / (WS * CS)

O_W0 = 0
O_W1 = O_W0 + KD * FF
O_SH = O_W1 + FC * D
O_WK = O_SH + KD * D
O_WV = O_WK + KD * NST
O_WO = O_WV + KD * NST
O_RT = O_WO + D
O_F1 = O_RT + 32
O_F2 = O_F1 + KD * FB
O_FL = O_F2 + KD * FB
O_PR = O_FL + KD * 2 * ML
O_AQ = O_PR + MC * D
O_AK = O_AQ + KD * D
O_AV = O_AK + KD * D
O_AO = O_AV + KD * D
WCOLS = O_AO + KD * D
WCH = 1000
RING = 4
SHARED = 49 * 1024
NCHUNK = WCOLS // WCH
NWG = NCHUNK // RING
assert WCOLS % WCH == 0 and NCHUNK % RING == 0

S_B0, S_LW, S_U, S_BQ, S_BK = 0, FC, FC + 1, FC + 2, FC + 4
SCOLS = FC + 6
R_B1, R_G, R_GAM, R_BET, R_BV, R_BO = range(6)


def block_kernel(nc, x_in, w_in, small_in, rows_in, ident_in, sel_in, order_in, masks_in, alibi_in, out):
    ctx = ExitStack()
    with ctx:
        def sb(name, shape, dt):
            return ctx.enter_context(nc.sbuf_tensor(name, shape, dt))

        def sem(name):
            return ctx.enter_context(nc.semaphore(name))

        shared = sb("shared", [P, SHARED // 4], F32)

        def part_of_shared():
            at = [0]

            def part(name, shape, dt):
                size = math.prod(shape[1:]) * (4 if dt is F32 else 2)
                v = shared[0:shape[0], at[0] // 4:(at[0] + size) // 4]
                at[0] += size
                assert at[0] <= SHARED, (name, at[0])
                v = v if dt is F32 else v.bitcast(dt)
                if len(shape) == 3:
                    v = v.rearrange("p (a b) -> p a b", b=shape[2])
                elif len(shape) == 4:
                    v = v.rearrange("p (a b c) -> p a b c", b=shape[2], c=shape[3])
                return v
            return part

        wkv_part, moe_part, att_part = part_of_shared(), part_of_shared(), part_of_shared()

        x = sb("x", [P, NG * GT, D], F32)
        xTh = sb("xTh", [P, KD, NG * GW], F16)
        xTl = sb("xTl", [P, KD, NG * GW], F16)
        n32 = sb("n32", [P, GT, D], F32)
        nh = sb("nh", [P, GT, D], F16)
        nl = sb("nl", [P, GT, D], F16)
        stat = sb("stat", [P, GT, 6], F32)
        mv = sb("mv", [P, GT, 2], F32)
        ve = sb("ve", [P, GT], F32)
        rstd = sb("rstd", [P, GT], F32)
        mhalf = sb("mhalf", [P, GT], F32)
        wh = sb("wh", [P, WCOLS], F16)
        wl = sb("wl", [P, WCOLS], F16)
        stage_raw = sb("stage", [P, NG * GT * D], F32)
        stage = stage_raw[:, 0:RING * WCH].rearrange("p (r c) -> p r c", r=RING)
        small = sb("small", [P, SCOLS], F32)
        rows = sb("rows", [P, 6, D], F32)
        ident = sb("ident", [P, P], F16)
        ident32 = sb("ident32", [P, P], F32)
        sel = sb("sel", [2 * NR, 2, P], F16)
        order = sb("order", [P, NE], F32)
        hT = sb("hT", [P, FC, GW], F16)
        t16 = sb("t16", [P, 2, 2 * D], F16)
        sg = moe_part("sg", [P, 3, GW], F32)
        pr = moe_part("pr", [P, 3, GW], F32)
        u32 = moe_part("u32", [P, 3, GW], F32)
        uh = moe_part("uh", [P, 3, GW], F16)
        ul = moe_part("ul", [P, 3, GW], F16)
        lg = sb("lg", [P, GT, NR], F32)
        dl = sb("dl", [P, GT, NR], F32)
        er = sb("er", [P, GT, NR], F32)
        prob = sb("prob", [P, GT, NE], F32)
        pm = sb("pm", [P, GT, NE], F32)
        s1 = sb("s1", [P, GT, NE], F32)
        s2 = sb("s2", [P, GT, NE], F32)
        mx = sb("mx", [P, GT], F32)
        comb = sb("comb", [P, GT, NR], F32)
        ch = sb("ch", [P, GT, 2 * NR], F16)
        cT = moe_part("cT", [2 * NR, NG * GW], F16)
        omg = wkv_part("omg", [P, D], F32)
        gsc = wkv_part("gsc", [P, D], F32)
        R = wkv_part("R", [P, 2, GT, D], F32)
        z = wkv_part("z", [P, 2, GT, D], F32)
        zh = wkv_part("zh", [P, 2, GT, D], F16)
        zl = wkv_part("zl", [P, 2, GT, D], F16)
        zTh = wkv_part("zTh", [P, 2, KD, GW], F16)
        zTl = wkv_part("zTl", [P, 2, KD, GW], F16)
        zstat = wkv_part("zstat", [P, 2, GT, 6], F32)
        zmv = wkv_part("zmv", [P, 2, GT, 2], F32)
        zve = wkv_part("zve", [P, 2, GT], F32)
        zrstd = wkv_part("zrstd", [P, 2, GT], F32)
        ka = wkv_part("ka", [P, GW], F32)
        eg = ka[:, 0:D]
        ev = wkv_part("ev", [P, GW], F32)
        kb = wkv_part("kb", [P, GW], F32)
        wkv = wkv_part("wkv", [P, GW], F32)
        decayw = wkv_part("decayw", [P, GW], F32)
        st32 = wkv_part("st32", [P, GW], F32)
        sth = wkv_part("sth", [P, GW], F16)
        stl = wkv_part("stl", [P, GW], F16)
        decay = sb("decay", [P, 1], F32)
        nu = sb("nu", [P, 1], F32)

        def by_chunk(v):
            return v.rearrange("p (q j c) -> p q j c", q=QC, j=QH)

        qop = [by_chunk(att_part("qop", [P, QC * QH * 512], F16)), by_chunk(xTh[:].rearrange("p k c -> p (k c)"))]
        kop = [by_chunk(att_part("kop", [P, QC * QH * 512], F16)), by_chunk(xTl[:].rearrange("p k c -> p (k c)"))]
        vals = att_part("vals", [P, B * 2 * TT * HH * VW], F32)
        vals_by = vals.rearrange("p (m t h c) -> p m t h c", m=B * 2, t=TT, h=HH)
        prob_t = att_part("prob_t", [P, 2, QH * 512], F32).rearrange("p a (j c) -> p a j c", j=QH)
        rest = prob_t.rearrange("p a j c -> p (a j c)")
        p32 = rest[:, 0:2 * GW].rearrange("p (a c) -> p a c", a=2)
        psplit = rest[:, 2 * GW:4 * GW].bitcast(F16).rearrange("p (a h c) -> p a h c", a=2, h=2)
        att = stage_raw[:].rearrange("p (t d) -> p t d", d=QH * DH)
        aTh, aTl = [wh[:, i * KD * GW:(i + 1) * KD * GW].rearrange("p (k c) -> p k c", k=KD) for i in range(2)]
        o32 = t16[:].rearrange("p a b -> p (a b)").bitcast(F32)
        mxs = sb("mxs", [P, MU], F32)
        mneg = sb("mneg", [P, QC, MU // QC], F16)
        vq = hT[:, 1:1 + 2 * TT * QH * VW * 2 // GW + 1, :].rearrange("p a b -> p (a b)").bitcast(F32)[
            :, 0:2 * TT * QH * VW].rearrange("p (a t r) -> p a t r", a=2, t=TT)
        mT = hT[0:MU // QC, 0, :].rearrange("p (a h c) -> p a h c", a=2, h=QC)
        masks = sb("masks", [P, 2, P], F16)
        rec = sb("rec", [P, GT, QH], F32)
        bqs = sb("bqs", [P, KD], F32)

        low_banks = [ctx.enter_context(nc.psum_tensor(f"bank{i}", [P, 512], F32)) for i in range(2)]
        mid = ctx.enter_context(nc.psum_tensor("mid", [P, 4, 512], F32))
        bank = [low_banks[0][:], low_banks[1][:]] + [mid[:, i, :] for i in range(4)]
        ybank = ctx.enter_context(nc.psum_tensor("ybank", [P, 2, 512], F32))
        tp = bank[0].bitcast(F16).rearrange("p (k c) -> p k c", k=KD)
        order4 = order[:].unsqueeze(1).to_broadcast([P, GT, NE])
        zth_bank, ztl_bank = [[bank[i].bitcast(F16).rearrange("p (k c) -> p k c", k=KD) for i in pair]
                              for pair in ((1, 2), (3, 1))]
        y_of = [ybank, mid[:, 0:2, :]]
        ath_bank, atl_bank = [bank[i].bitcast(F16).rearrange("p (k c) -> p k c", k=KD) for i in (2, 3)]
        ya = [mid[:, 2:4, :]] * 2 + [ybank] * 2

        x_in_done = sem("x_in_done")
        x0_in_done = sem("x0_in_done")
        early_done = sem("early_done")
        const_done = sem("const_done")
        w_in_done = [sem(f"w_in_done{i}") for i in range(RING)]
        w_high = sem("w_high")
        w_low = sem("w_low")
        set_done = sem("set_done")
        pool_set = sem("pool_set")
        x_done = sem("x_done")
        stat_done = sem("stat_done")
        aggr_done = sem("aggr_done")
        wait_carrier = sem("wait_carrier")
        pe_carrier = sem("pe_carrier")
        ve_done = sem("ve_done")
        rstd_done = sem("rstd_done")
        n32_done = sem("n32_done")
        nh_done = sem("nh_done")
        nl_done = sem("nl_done")
        th_ready = sem("th_ready")
        tl_ready = sem("tl_ready")
        xTh_done = sem("xTh_done")
        xTl_done = sem("xTl_done")
        h_ready = sem("h_ready")
        gelu_done = sem("gelu_done")
        y_ready = sem("y_ready")
        t16_done = sem("t16_done")
        h1_ready = sem("h1_ready")
        h2_ready = sem("h2_ready")
        C_ready = sem("C_ready")
        silu_done = sem("silu_done")
        pr_done = sem("pr_done")
        u32_done = sem("u32_done")
        uh_done = sem("uh_done")
        ul_done = sem("ul_done")
        rt_ready = sem("rt_ready")
        rt_step = sem("rt_step")
        dl_done = sem("dl_done")
        er_done = sem("er_done")
        rt_sel = sem("rt_sel")
        comb_done = sem("comb_done")
        zg_done = sem("zg_done")
        kb_done = sem("kb_done")
        wkv_done = sem("wkv_done")
        carry_ready = sem("carry_ready")
        act_set = sem("act_set")
        ch_done = sem("ch_done")
        ct_ready = sem("ct_ready")
        cT_done = sem("cT_done")
        R_done = sem("R_done")
        sh_ready = sem("sh_ready")
        z_read = sem("z_read")
        zn_done = sem("zn_done")
        zsum_done = sem("zsum_done")
        zstat_done = sem("zstat_done")
        zaggr_done = sem("zaggr_done")
        zve_done = sem("zve_done")
        zrstd_done = sem("zrstd_done")
        zh_done = sem("zh_done")
        zl_done = sem("zl_done")
        zth_ready = sem("zth_ready")
        ztl_ready = sem("ztl_ready")
        zTh_done = sem("zTh_done")
        zTl_done = sem("zTl_done")
        kv_ready = sem("kv_ready")
        ek_done = sem("ek_done")
        sig_done = sem("sig_done")
        ev_done = sem("ev_done")
        st_done = sem("st_done")
        sth_done = sem("sth_done")
        stl_done = sem("stl_done")
        out_done = sem("out_done")
        qk_ready = sem("qk_ready")
        p32_done = sem("p32_done")
        ph_done = sem("ph_done")
        pl_done = sem("pl_done")
        v_ready = sem("v_ready")
        v_done = sem("v_done")
        scratch_done = [sem(f"scratch_done{i}") for i in range(2)]
        pos_done = sem("pos_done")
        fill_done = sem("fill_done")
        vones_done = sem("vones_done")
        vq_done = sem("vq_done")
        op_in = [sem(f"op_in{i}") for i in range(2)]
        ql_in = [sem(f"ql_in{i}") for i in range(2)]
        m_in = [[sem(f"m_in{i}{h}") for h in range(QC)] for i in range(2)]
        s_ready = sem("s_ready")
        mx_done = sem("mx_done")
        mneg_done = sem("mneg_done")
        mt_ready = sem("mt_ready")
        mT_done = sem("mT_done")
        st_ready = sem("st_ready")
        exp_done = sem("exp_done")
        pv_done = sem("pv_done")
        o32_done = sem("o32_done")
        ot_ready = sem("ot_ready")
        rec_done = sem("rec_done")
        att_done = sem("att_done")
        ah_done = sem("ah_done")
        al_done = sem("al_done")
        ath_ready = sem("ath_ready")
        atl_ready = sem("atl_ready")
        aTh_done = sem("aTh_done")
        aTl_done = sem("aTl_done")
        ob_done = sem("ob_done")
        op_dram = nc.dram_tensor("scratch_operands", [2, B * 2, KR * HH, T], F16).ap()

        RT_STEPS = 16

        def tokens(g, t=0, n=GW):
            return bass.ds(g * GW + t * P, n)

        def tiles(g, t=0, n=GT):
            return bass.ds(g * GT + t, n)

        def W(parts, col, n, rows_=P):
            return parts[0:rows_, col:col + n]

        def row(i, n):
            return rows[:, i:i + 1, :].to_broadcast([P, n, D])

        def pe_transpose_high(pe, n):
            pe.wait_ge(nh_done, n + 1)
            for t in range(GT):
                for k in range(KD):
                    last = nc.tensor.transpose(tp[:, k, t * P:(t + 1) * P], nh[:, t, k * P:(k + 1) * P], ident[:])
            last.then_inc(th_ready, 1)

        def pe_transpose_low(pe, n, ns):
            pe.wait_ge(nl_done, ns + 1)
            pe.wait_ge(xTh_done, n + 1)
            for t in range(GT):
                for k in range(KD):
                    last = nc.tensor.transpose(tp[:, k, t * P:(t + 1) * P], nl[:, t, k * P:(k + 1) * P], ident[:])
            last.then_inc(tl_ready, 1)

        def pe_router(pe, ns, g):
            pe.wait_ge(xTl_done, ns + 1)
            for t in range(GT):
                for i, (xs, ws) in enumerate(((xTh, wh), (xTh, wl), (xTl, wh))):
                    for k in range(KD):
                        last = nc.tensor.matmul(bank[0][:, t * NR:(t + 1) * NR], xs[:, k, tokens(g, t, P)],
                                                W(ws, O_RT + k * NR, NR), start=(i == 0 and k == 0),
                                                stop=(i == 2 and k == KD - 1))
            last.then_inc(rt_ready, 1)

        def pe_transpose_routes(pe, m):
            pe.wait_ge(ch_done, m + 1)
            for t in range(GT):
                last = nc.tensor.transpose(tp[0:2 * NR, 0, t * P:(t + 1) * P], ch[:, t, :], ident[:])
            last.then_inc(ct_ready, 1)

        def pe_ffn(pe, n, f, g, steps):
            pe.wait_ge(xTh_done, n + 1)

            def hidden(c):
                for k in range(KD):
                    for i, ws in enumerate((wh, wl)):
                        last = nc.tensor.matmul(bank[2 + c % 4], W(ws, O_W0 + k * FF + c * P, P),
                                                xTh[:, k, tokens(g)], start=(k == 0 and i == 0),
                                                stop=(k == KD - 1 and i == 1))
                last.then_inc(h_ready, 1)

            def project(c):
                pe.wait_ge(gelu_done, FC * f + c + 1)
                if c == 0:
                    pe.wait_ge(x_done, n + 1)
                    pe.wait_ge(w_low, 5)
                for t in range(GT):
                    for i, ws in enumerate((wh, wl)):
                        last = nc.tensor.matmul(ybank[:, t // 2, (t % 2) * D:(t % 2 + 1) * D],
                                                hT[:, c, t * P:(t + 1) * P], W(ws, O_W1 + c * D, D),
                                                start=(c == 0 and i == 0 and t % 2 == 0),
                                                stop=(c == FC - 1 and i == 1), skip_group_check=True)
                if c == FC - 1:
                    last.then_inc(y_ready, 1)

            for c in range(FC):
                hidden(c)
                if c >= 2:
                    project(c - 2)
                for step in steps.get(c, ()):
                    step(pe)
            project(FC - 2)
            project(FC - 1)

        def slot(c):
            return c % 2 if c < MC - 1 else 2

        def h_banks(c):
            return (bank[2 + c % 2], bank[4 + c % 2]) if c < MC - 1 else (bank[0][0:ML], bank[0][P - ML:P])

        def rows_of(c):
            return slice(0, P) if c < MC - 1 else slice(P - ML, P)

        def pe_moe_hidden(pe, n, ns, m, g, c, free=None):
            if c == 0:
                pe.wait_ge(xTh_done, n + 1)
                pe.wait_ge(xTl_done, ns + 1)
                pe.wait_ge(cT_done, m + 1)
            if c < MC - 1:
                products = [(O_F1 + c * P, FB, h_banks(c)[0]), (O_F2 + c * P, FB, h_banks(c)[1])]
            else:
                products = [(O_FL, 2 * ML, bank[0])]
                if free is not None:
                    free(pe)
                    pe.sem_inc(pe_carrier, 1)
            for off, width, bk in products:
                for k in range(KD):
                    for i, (ws, xs) in enumerate(((wh, xTh), (wh, xTl), (wl, xTh))):
                        last = nc.tensor.matmul(bk, W(ws, off + k * width, P), xs[:, k, tokens(g)],
                                                start=(k == 0 and i == 0), stop=(k == KD - 1 and i == 2))
                last.then_inc(h1_ready if off == products[0][0] else h2_ready, 1)
            if c in (0, EC):
                if c or not isinstance(m, int) or m:
                    pe.wait_ge(u32_done, MC * m + c)
                    pe.sem_inc(pe_carrier, 1)
                nc.tensor.matmul(bank[1], sel[:, c // EC, :], cT[:, tokens(g)],
                                 start=True, stop=True).then_inc(C_ready, 1)

        def pe_moe_project(pe, n, m, c):
            r_ = rows_of(c)
            pe.wait_ge(ul_done, MC * m + c + 1)
            if c == 0:
                pe.wait_ge(x_done, n + 1)
            for t in range(GT):
                for i, (us, ws) in enumerate(((uh, wh), (uh, wl), (ul, wh))):
                    last = nc.tensor.matmul(ybank[:, t // 2, (t % 2) * D:(t % 2 + 1) * D],
                                            us[r_, slot(c), t * P:(t + 1) * P],
                                            ws[r_, O_PR + c * D:O_PR + (c + 1) * D],
                                            start=(c == 0 and i == 0 and t % 2 == 0),
                                            stop=(c == MC - 1 and i == 2), skip_group_check=True)
            if c == MC - 1:
                last.then_inc(y_ready, 1)

        def pe_moe(pe, n, ns, m, g, steps, free, nxt=True):
            for c in range(1, MC):
                pe_moe_hidden(pe, n, ns, m, g, c, free)
                pe_moe_project(pe, n, m, c - 1)
                for step in steps.get(c, ()):
                    step(pe)
            if nxt:
                pe_moe_hidden(pe, n + 1, ns + 1, m + 1, g + 1, 0)
            pe_moe_project(pe, n, m, MC - 1)

        def pe_wkv(pe, b):
            n, q = 4 + 2 * b, 2 * b
            na, nb = n + 2, n + 3
            pe.wait_ge(xTh_done, n + 2)
            pe.wait_ge(xTl_done, q + 2)
            pe.wait_ge(x_done, n + 1)
            for j in range(2):
                for t in range(GT):
                    for i, (xs, ws) in enumerate(((xTh, wh), (xTh, wl), (xTl, wh))):
                        for k in range(KD):
                            last = nc.tensor.matmul(y_of[j][:, t // 2, (t % 2) * D:(t % 2 + 1) * D],
                                                    xs[:, k, bass.ds((2 * b + 1 - j) * GW + t * P, P)],
                                                    W(ws, O_SH + k * D, D),
                                                    start=(i == 0 and k == 0), stop=(i == 2 and k == KD - 1))
                last.then_inc(sh_ready, 1)
            for parts, banks, done, ready in ((zh, zth_bank, zh_done, zth_ready), (zl, ztl_bank, zl_done, ztl_ready)):
                for j in range(2):
                    pe.wait_ge(done, q + j + 1)
                    if parts is zl:
                        pe.wait_ge(zTh_done, q + j + 1)
                    for t in range(GT):
                        for k in range(KD):
                            last = nc.tensor.transpose(banks[j][:, k, t * P:(t + 1) * P],
                                                       parts[:, j, t, k * P:(k + 1) * P], ident[:])
                    last.then_inc(ready, 1)
            for j in range(2):
                pe.wait_ge(zTh_done, q + j + 1)
                pe.wait_ge(zTl_done, q + j + 1)
                for off, bk in ((O_WK, bank[4]), (O_WV, bank[5])):
                    for k in range(KD):
                        for i, (ws, zs) in enumerate(((wh, zTh), (wh, zTl), (wl, zTh))):
                            last = nc.tensor.matmul(bk[j * NST:(j + 1) * NST, :], W(ws, off + k * NST, NST),
                                                    zs[:, j, k, :], start=(k == 0 and i == 0),
                                                    stop=(k == KD - 1 and i == 2), skip_group_check=True)
            last.then_inc(kv_ready, 1)
            pe.wait_ge(xTl_done, q + 2)
            pe_transpose_high(pe, na)
            pe_transpose_low(pe, na, q + 2)
            pe.wait_ge(st_done, q + 1)
            pe.sem_inc(pe_carrier, 1)
            nc.tensor.matmul(bank[1][NST:2 * NST, 0:1], ident32[0:NST, 0:NST], st32[0:NST, GW - 1:GW],
                             start=True, stop=True).then_inc(carry_ready, 1)
            for j in range(2):
                pe.wait_ge(sth_done, q + j + 1)
                pe.wait_ge(stl_done, q + j + 1)
                rows_ = slice(j * NST, (j + 1) * NST)
                for t in range(GT):
                    for i, (ss, ws) in enumerate(((sth, wh), (sth, wl), (stl, wh))):
                        last = nc.tensor.matmul(y_of[j][:, t // 2, (t % 2) * D:(t % 2 + 1) * D],
                                                ss[rows_, t * P:(t + 1) * P], ws[rows_, O_WO:O_WO + D],
                                                start=(i == 0), stop=(i == 2))
                last.then_inc(y_ready, 1)
                if j == 0:
                    pe.wait_ge(xTl_done, q + 3)
                    pe_transpose_high(pe, nb)
            pe_transpose_low(pe, nb, q + 3)

        def act_round(act, n):
            act.wait_ge(n32_done, n + 1)
            if not isinstance(n, int) or n:
                act.wait_ge(th_ready, n)
            nc.scalar.copy(nh[:], n32[:]).then_inc(nh_done, 1)

        def act_high_out(act, n, g):
            act.wait_ge(th_ready, n + 1)
            nc.scalar.copy(xTh[:, :, tokens(g)], tp).then_inc(xTh_done, 1)

        def act_exp_routes(act, m):
            act.wait_ge(dl_done, m + 1)
            nc.scalar.activation(er[:], dl[:], ACT.Exp).then_inc(er_done, 1)

        def act_routes_out(act, m, g):
            act.wait_ge(ct_ready, m + 1)
            nc.scalar.copy(cT[:, tokens(g)], tp[0:2 * NR, 0, :]).then_inc(cT_done, 1)

        def act_weights(act, r, j):
            act.wait_ge(w_in_done[j], 16 * (r + 1))
            nc.scalar.activation(wh[:, bass.ds((RING * r + j) * WCH, WCH)], stage[:, j, :], ACT.Copy,
                                 scale=WS).then_inc(w_high, 1)

        def act_ffn(act, f, steps):
            for c in range(FC):
                act.wait_ge(h_ready, FC * f + c + 1)
                nc.scalar.activation(hT[:, c, :], bank[2 + c % 4], ACT.Gelu, bias=small[:, S_B0 + c:S_B0 + c + 1],
                                     scale=1 / WS).then_inc(gelu_done, 1)
                for step in steps.get(c, ()):
                    step(act)

        def act_moe(act, m, steps):
            for c in range(MC):
                r_ = rows_of(c)
                act.wait_ge(h1_ready, MC * m + c + 1)
                nc.scalar.activation(sg[r_, slot(c), :], h_banks(c)[0], ACT.Silu,
                                     scale=1 / WS).then_inc(silu_done, 1)
                act.wait_ge(u32_done, MC * m + c + 1)
                nc.scalar.copy(uh[r_, slot(c), :], u32[r_, slot(c), :]).then_inc(uh_done, 1)
                for step in steps.get(c, ()):
                    step(act)

        def act_wkv(act, b):
            n, q = 4 + 2 * b, 2 * b
            for j in range(2):
                act.wait_ge(zn_done, q + j + 1)
                nc.scalar.copy(zh[:, j, :, :], z[:, j, :, :]).then_inc(zh_done, 1)
            for j in range(2):
                act.wait_ge(zth_ready, q + j + 1)
                nc.scalar.copy(zTh[:, j, :, :], zth_bank[j]).then_inc(zTh_done, 1)
            act_round(act, n + 2)
            act.wait_ge(kv_ready, b + 1)
            nc.scalar.activation(ka[:], bank[4], ACT.Exp, scale=-1 / WS).then_inc(ek_done, 1)
            act_high_out(act, n + 2, (q + 2) % NG)
            act.wait_ge(sig_done, b + 1)
            nc.scalar.activation(ev[:], kb[:], ACT.Exp, scale=nu[:]).then_inc(ev_done, 1)
            for j in range(2):
                rows_ = slice(j * NST, (j + 1) * NST)
                act.wait_ge(st_done, q + j + 1)
                nc.scalar.copy(sth[rows_, :], st32[rows_, :]).then_inc(sth_done, 1)
                if j == 0:
                    act_round(act, n + 3)
            act_high_out(act, n + 3, (q + 3) % NG)

        def dve_normalise(dve, n, g, first=False):
            dve_moments(dve, n, g, first)
            dve_scale(dve, n, g)

        def dve_moments(dve, n, g, first=False):
            dve.wait_ge(x_done, 1 if first else n - 2)
            for t in range(GT):
                last = nc.vector.bn_stats(stat[:, t, :], x[:, tiles(g, t, 1), :])
            last.then_inc(stat_done, 1)
            dve.wait_ge(stat_done, n + 1)
            dve.sem_inc(wait_carrier, 1)
            for t in range(GT):
                last = nc.vector.bn_aggr(mv[:, t, :], stat[:, t, :])
            last.then_inc(aggr_done, 1)
            dve.wait_ge(aggr_done, n + 1)
            nc.vector.tensor_scalar(ve[:], mv[:, :, 1], EPS, None, ALU.add).then_inc(ve_done, 1)

        def dve_scale(dve, n, g, skipped=None):
            if skipped is not None:
                dve.wait_ge(R_done, skipped)
            dve.wait_ge(rstd_done, n + 1)
            if not isinstance(n, int) or n:
                dve.wait_ge(nh_done, n)
            for t in range(GT):
                last = nc.vector.tensor_scalar(n32[:, t, :], x[:, tiles(g, t, 1), :], mv[:, t, 0:1], rstd[:, t:t + 1],
                                               ALU.subtract, ALU.mult)
            last.then_inc(n32_done, 1)

        def dve_low(dve, n, ns):
            dve.wait_ge(nh_done, n + 1)
            if not isinstance(ns, int) or ns:
                dve.wait_ge(tl_ready, ns)
            nc.vector.tensor_tensor(nl[:], n32[:], nh[:], ALU.subtract).then_inc(nl_done, 1)

        def dve_low_out(dve, ns, g):
            dve.wait_ge(tl_ready, ns + 1)
            nc.vector.tensor_copy(xTl[:, :, tokens(g)], tp).then_inc(xTl_done, 1)

        def dve_skip(dve, n, j):
            dve.wait_ge(n32_done, n + 1)
            nc.vector.tensor_tensor(R[:, j, :, :], n32[:], omg[:].unsqueeze(1).to_broadcast([P, GT, D]),
                                    ALU.mult).then_inc(R_done, 1)

        def stepper(dve, m, at):
            count = [at]

            def step(ins):
                count[0] += 1
                ins.then_inc(rt_step, 1)
                dve.wait_ge(rt_step, RT_STEPS * m + count[0])
            return step

        def wide(v, n=NE):
            return v.unsqueeze(2).to_broadcast([P, GT, n])

        def dve_routes_logits(dve, m):
            step = stepper(dve, m, 0)
            dve.wait_ge(rt_ready, m + 1)
            step(nc.vector.tensor_scalar(lg[:], bank[0][:, 0:GT * NR].rearrange("p (t r) -> p t r", r=NR), 1 / WS,
                                         None, ALU.mult))
            step(nc.vector.tensor_reduce(mx[:], lg[:, :, 0:NE], AX.X, ALU.max))
            step(nc.vector.tensor_scalar(dl[:, :, NE:NR], lg[:, :, NE:NR], -1.0, None, ALU.mult))
            nc.vector.tensor_tensor(dl[:, :, 0:NE], lg[:, :, 0:NE], wide(mx[:]), ALU.subtract).then_inc(dl_done, 1)

        def dve_routes_first(dve, m):
            step = stepper(dve, m, 3)
            dve.wait_ge(er_done, m + 1)
            step(nc.vector.tensor_reduce(mx[:], er[:, :, 0:NE], AX.X, ALU.add))
            step(nc.vector.reciprocal(mx[:], mx[:]))
            step(nc.vector.tensor_tensor(prob[:], er[:, :, 0:NE], wide(mx[:]), ALU.mult))
            step(nc.vector.tensor_reduce(mx[:], prob[:], AX.X, ALU.max))
            step(nc.vector.tensor_tensor(s1[:], prob[:], wide(mx[:]), ALU.is_equal))
            step(nc.vector.tensor_tensor(pm[:], s1[:], order4, ALU.mult))

        def dve_routes_second(dve, m):
            step = stepper(dve, m, 9)
            step(nc.vector.tensor_reduce(mx[:], pm[:], AX.X, ALU.max))
            step(nc.vector.tensor_tensor(s1[:], pm[:], wide(mx[:]), ALU.is_equal))
            step(nc.vector.scalar_tensor_tensor(pm[:], s1[:], -2.0, prob[:], ALU.mult, ALU.add))
            step(nc.vector.tensor_reduce(mx[:], pm[:], AX.X, ALU.max))
            step(nc.vector.tensor_tensor(s2[:], pm[:], wide(mx[:]), ALU.is_equal))
            step(nc.vector.tensor_tensor(s2[:], s2[:], order4, ALU.mult))
            step(nc.vector.tensor_reduce(mx[:], s2[:], AX.X, ALU.max))

        def dve_routes_split(dve, m):
            nc.vector.tensor_tensor(s2[:], s2[:], wide(mx[:]), ALU.is_equal).then_inc(rt_sel, 1)
            dve.wait_ge(rt_sel, 4 * m + 1)
            nc.vector.tensor_tensor(s1[:], s1[:], s2[:], ALU.add).then_inc(rt_sel, 1)
            nc.vector.tensor_scalar(comb[:, :, NE:NR], er[:, :, NE:NR], 1.0, None, ALU.add).then_inc(rt_sel, 1)
            dve.wait_ge(rt_sel, 4 * m + 3)
            nc.vector.scalar_tensor_tensor(comb[:, :, 0:NE], s1[:], CS, prob[:], ALU.mult, ALU.mult)
            nc.vector.reciprocal(er[:, :, NE:NR], comb[:, :, NE:NR]).then_inc(rt_sel, 1)
            dve.wait_ge(rt_sel, 4 * m + 4)
            nc.vector.tensor_scalar(comb[:, :, NE:NR], er[:, :, NE:NR], CS, None, ALU.mult).then_inc(comb_done, 1)
            dve.wait_ge(comb_done, 2 * m + 1)
            if not isinstance(m, int) or m:
                dve.wait_ge(ct_ready, m)
            nc.vector.tensor_copy(ch[:, :, 0:NR], comb[:]).then_inc(comb_done, 1)
            dve.wait_ge(comb_done, 2 * m + 2)
            nc.vector.tensor_tensor(ch[:, :, NR:2 * NR], comb[:], ch[:, :, 0:NR], ALU.subtract).then_inc(ch_done, 1)

        def dve_routes(dve, m):
            for part in (dve_routes_logits, dve_routes_first, dve_routes_second, dve_routes_split):
                part(dve, m)

        def dve_weights(dve, r, j):
            dve.wait_ge(w_high, RING * r + j + 1)
            c = bass.ds((RING * r + j) * WCH, WCH)
            nc.vector.scalar_tensor_tensor(wl[:, c], stage[:, j, :], WS, wh[:, c], ALU.mult,
                                           ALU.subtract).then_inc(w_low, 1)

        def dve_ffn_sum(dve, n, f, g):
            dve.wait_ge(y_ready, n + 1)
            for h in range(2):
                nc.vector.scalar_tensor_tensor(t16[:, h, :].rearrange("p (t d) -> p t d", t=2),
                                               ybank[:, h, :].rearrange("p (t d) -> p t d", t=2), 1 / WS,
                                               row(R_B1, 2), ALU.mult, ALU.add).then_inc(t16_done, 1)
            for h in range(2):
                dve.wait_ge(t16_done, 2 * f + h + 1)
                xs = x[:, tiles(g, 2 * h, 2), :]
                last = nc.vector.scalar_tensor_tensor(xs, t16[:, h, :].rearrange("p (t d) -> p t d", t=2), 0.5, xs,
                                                      ALU.mult, ALU.add)
            last.then_inc(x_done, 1)

        def dve_sum(dve, n, g, factor, y=ybank):
            dve.wait_ge(y_ready, n + 1)
            for h in range(2):
                xs = x[:, tiles(g, 2 * h, 2), :]
                last = nc.vector.scalar_tensor_tensor(xs, y[:, h, :].rearrange("p (t d) -> p t d", t=2), factor, xs,
                                                      ALU.mult, ALU.add)
            last.then_inc(x_done, 1)

        def dve_moe(dve, m, steps):
            for c in range(MC):
                r_ = rows_of(c)
                dve.wait_ge(silu_done, MC * m + c + 1)
                if c < MC - 1:
                    dve.wait_ge(h2_ready, (MC - 1) * m + c + 1)
                dve.wait_ge(C_ready, 2 * m + 1 + c // EC)
                nc.vector.tensor_tensor(pr[r_, slot(c), :], h_banks(c)[1], sg[r_, slot(c), :],
                                        ALU.mult).then_inc(pr_done, 1)
                dve.wait_ge(pr_done, MC * m + c + 1)
                nc.vector.tensor_tensor(u32[r_, slot(c), :], bank[1][r_], pr[r_, slot(c), :],
                                        ALU.mult).then_inc(u32_done, 1)
                for step in steps.get(c, ()):
                    step(dve)

        def dve_wkv(dve, b):
            n, q = 4 + 2 * b, 2 * b
            na, nb, ga, gb = n + 2, n + 3, (q + 2) % NG, (q + 3) % NG
            for j in range(2):
                dve.wait_ge(sh_ready, q + j + 1)
                for h in range(2):
                    last = nc.vector.tensor_tensor(z[:, j, 2 * h:2 * h + 2, :],
                                                   y_of[j][:, h, :].rearrange("p (t d) -> p t d", t=2),
                                                   gsc[:].unsqueeze(1).to_broadcast([P, 2, D]), ALU.mult)
                last.then_inc(z_read, 1)
                dve.wait_ge(z_read, q + j + 1)
                nc.vector.tensor_tensor(z[:, j, :, :], z[:, j, :, :], R[:, j, :, :], ALU.add).then_inc(zsum_done, 1)
                dve.wait_ge(zsum_done, q + j + 1)
                for t in range(GT):
                    last = nc.vector.bn_stats(zstat[:, j, t, :], z[:, j, t, :])
                last.then_inc(zstat_done, 1)
                dve.wait_ge(zstat_done, q + j + 1)
                dve.sem_inc(wait_carrier, 1)
                for t in range(GT):
                    last = nc.vector.bn_aggr(zmv[:, j, t, :], zstat[:, j, t, :])
                last.then_inc(zaggr_done, 1)
                dve.wait_ge(zaggr_done, q + j + 1)
                nc.vector.tensor_scalar(zve[:, j, :], zmv[:, j, :, 1], EPS, None, ALU.add).then_inc(zve_done, 1)
            for j in range(2):
                for t in range(GT):
                    last = nc.vector.scalar_tensor_tensor(z[:, j, t, :], z[:, j, t, :], zmv[:, j, t, 0:1],
                                                          rows[:, R_GAM, :], ALU.subtract, ALU.mult)
                last.then_inc(zg_done, 1)
                dve.wait_ge(zg_done, q + j + 1)
                dve.wait_ge(zrstd_done, q + j + 1)
                for t in range(GT):
                    last = nc.vector.scalar_tensor_tensor(z[:, j, t, :], z[:, j, t, :], zrstd[:, j, t:t + 1],
                                                          rows[:, R_BET, :], ALU.mult, ALU.add)
                last.then_inc(zn_done, 1)
            for j in range(2):
                dve.wait_ge(zh_done, q + j + 1)
                nc.vector.tensor_tensor(zl[:, j, :, :], z[:, j, :, :], zh[:, j, :, :],
                                        ALU.subtract).then_inc(zl_done, 1)
            dve_moments(dve, na, ga)
            for j in range(2):
                dve.wait_ge(ztl_ready, q + j + 1)
                nc.vector.tensor_copy(zTl[:, j, :, :], ztl_bank[j]).then_inc(zTl_done, 1)
            dve_scale(dve, na, ga, skipped=q + 2)
            dve_moments(dve, nb, gb)
            dve_low(dve, na, q + 2)
            dve_skip(dve, na, 0)
            dve.wait_ge(ek_done, b + 1)
            nc.vector.tensor_scalar(kb[:], ka[:], 1.0, None, ALU.add).then_inc(kb_done, 1)
            dve.wait_ge(kb_done, b + 1)
            nc.vector.reciprocal(kb[:], kb[:]).then_inc(sig_done, 1)
            dve_scale(dve, nb, gb, skipped=q + 3)
            dve.wait_ge(ev_done, b + 1)
            nc.vector.scalar_tensor_tensor(wkv[:], bank[5], 1 / WS, ev[:], ALU.mult, ALU.mult).then_inc(wkv_done, 1)
            dve.wait_ge(wkv_done, b + 1)
            nc.vector.tensor_tensor_scan(st32[0:NST, :], decayw[0:NST, :], wkv[0:NST, :], 0.0, ALU.mult,
                                         ALU.add).then_inc(st_done, 1)
            dve_low_out(dve, q + 2, ga)
            dve.wait_ge(carry_ready, b + 1)
            nc.vector.tensor_tensor_scan(st32[NST:2 * NST, :], decayw[NST:2 * NST, :], wkv[NST:2 * NST, :],
                                         bank[1][NST:2 * NST, 0:1], ALU.mult, ALU.add).then_inc(st_done, 1)
            for j in range(2):
                rows_ = slice(j * NST, (j + 1) * NST)
                dve.wait_ge(sth_done, q + j + 1)
                nc.vector.tensor_tensor(stl[rows_, :], st32[rows_, :], sth[rows_, :],
                                        ALU.subtract).then_inc(stl_done, 1)
                if j == 0:
                    dve_skip(dve, nb, 1)
            dve_low(dve, nb, q + 3)
            for j in range(2):
                dve_sum(dve, n + j, 2 * b + j, 1 / WS, y_of[j])
            dve_low_out(dve, q + 3, gb)

        def pool_root(pool, n, src, dst, src_done, dst_done):
            pool.wait_ge(src_done, n + 1)
            nc.gpsimd.tensor_tensor(dst[:], src[:], mhalf[:], ALU.pow).then_inc(dst_done, 1)

        def pool_moe(pool, m, steps):
            for c in range(MC):
                r_ = rows_of(c)
                if c == MC - 1:
                    pool.wait_ge(ul_done, MC * m + c)
                pool.wait_ge(uh_done, MC * m + c + 1)
                nc.gpsimd.tensor_tensor(ul[r_, slot(c), :], u32[r_, slot(c), :], uh[r_, slot(c), :],
                                        ALU.subtract).then_inc(ul_done, 1)
                if c == MC - 1:
                    pool.wait_ge(ul_done, MC * m + MC)
                for step in steps.get(c, ()):
                    step(pool)


        STEPS = [(qc, kt) for qc in reversed(range(QC)) for kt in range(4 * (qc + 1))]
        NS = len(STEPS)
        HEAVY = MU // QC
        M_SLOTS = {}
        for v in range(MU):
            at = 1 + 30 * v // HEAVY if v < HEAVY else 32 + 16 * (v - HEAVY) // HEAVY
            M_SLOTS.setdefault(at, []).append(v)
        M_OUT = sum(len(vs) for at, vs in M_SLOTS.items() if at < QH * (4 * QC + 2))
        HALF = 4 * QC

        def span(s):
            qc, kt = STEPS[s]
            return max(0, kt * P - qc * 512)

        QKV_M = {}
        for v in range(MU):
            QKV_M.setdefault(2 + 8 * v // MU, []).append(v)

        def blocks_after(a, o):
            return QKV_M.get(5 * (a - NG // B) + o, ())

        def pe_qkv_blocks(pe, a, o):
            for v in blocks_after(a, o):
                if v == 0:
                    pe.wait_ge(op_in[0], 48)
                if v == HEAVY:
                    pe.wait_ge(ql_in[0], 16)
                pe_max_block(pe, 0, 0, v)

        def pe_qkv(pe, a):
            n, ns = 16 + a, SPLIT[16] + a
            banks = [bank[2], bank[3]] if a < NG // B else [bank[0], bank[1]]
            pe.wait_ge(xTh_done, n + 1)
            pe.wait_ge(xTl_done, ns + 1)
            for i, off in enumerate((O_AQ, O_AK)):
                for m in range(KD):
                    o = 2 * i + m
                    if o >= 2:
                        pe.wait_ge(p32_done, 4 * a + o - 1)
                    for k in range(KD):
                        for j, (ws, xs) in enumerate(((wh, xTh), (wh, xTl), (wl, xTh))):
                            last = nc.tensor.matmul(banks[o % 2], W(ws, off + k * D + m * P, P),
                                                    xs[:, k, tokens(a)], start=(k == 0 and j == 0),
                                                    stop=(k == KD - 1 and j == 2))
                    last.then_inc(qk_ready, 1)
                    pe_qkv_blocks(pe, a, o)
            pe.wait_ge(p32_done, 4 * a + 4)
            pe.wait_ge(v_done, a + 1)
            for t in range(GT):
                for j, (xs, ws) in enumerate(((xTh, wh), (xTh, wl), (xTl, wh))):
                    for k in range(KD):
                        last = nc.tensor.matmul(ybank[:, t // 2, (t % 2) * D:(t % 2 + 1) * D], xs[:, k, tokens(a, t, P)],
                                                W(ws, O_AV + k * D, D), start=(j == 0 and k == 0),
                                                stop=(j == 2 and k == KD - 1))
            last.then_inc(v_ready, 1)
            pe_qkv_blocks(pe, a, 4)

        def act_qkv(act, a):
            for o in range(4):
                act.wait_ge(qk_ready, 4 * a + o + 1)
                act.wait_ge(pl_done, 4 * a + o + 1)
                q = o < 2
                m = o % 2
                nc.scalar.activation(p32[:, o % 2, :], bank[(2 if a < NG // B else 0) + o % 2], ACT.Identity,
                                     bias=bqs[:, m:m + 1] if q else small[:, S_BK + m:S_BK + m + 1],
                                     scale=SS / math.sqrt(DH) / WS if q else 1 / WS).then_inc(p32_done, 1)
                act.wait_ge(p32_done, 4 * a + o + 1)
                act.wait_ge(scratch_done[o % 2], 48 * (2 * a + o // 2 + 1))
                nc.scalar.copy(psplit[:, o % 2, 0, :], p32[:, o % 2, :]).then_inc(ph_done, 1)

        def dve_qkv(dve, a):
            b, j = a // 2, a % 2
            for o in range(4):
                for v in blocks_after(a, o):
                    dve_max_block(dve, 0, v)
                dve.wait_ge(ph_done, 4 * a + o + 1)
                nc.vector.tensor_tensor(psplit[:, o % 2, 1, :], p32[:, o % 2, :], psplit[:, o % 2, 0, :],
                                        ALU.subtract).then_inc(pl_done, 1)
            for v in blocks_after(a, 4):
                dve_max_block(dve, 0, v)
            dve.wait_ge(v_ready, a + 1)
            for t in range(GT):
                for m in range(2):
                    last = nc.vector.scalar_tensor_tensor(
                        vals_by[:, 2 * b + m:2 * b + m + 1, j * GT + t, :, 0:DH].rearrange("p m h c -> p (m h) c"),
                        ybank[:, t // 2, (t % 2) * D + m * P:(t % 2) * D + (m + 1) * P].rearrange(
                            "p (h c) -> p h c", h=HH), 1 / WS,
                        rows[:, R_BV, m * P:(m + 1) * P].rearrange("p (h c) -> p h c", h=HH), ALU.mult, ALU.add)
            last.then_inc(v_done, 1)

        PLACES = (((0, 2), (1,)), ((0, 1), (2,)))

        def sp_qkv(sp, a, b, j):
            for o in range(4):
                for part, done in ((0, ph_done), (1, pl_done)):
                    sp.wait_ge(done, 4 * a + o + 1 + 2 * part)
                    for place in PLACES[o // 2][part]:
                        row0 = (4 + place * DH) * HH
                        dst = op_dram[o // 2, 2 * b + o % 2:2 * b + o % 2 + 1, row0:row0 + P, j * GW:(j + 1) * GW]
                        sp.dma_start(dst.rearrange("m r n -> r (m n)"),
                                     psplit[:, o % 2, part, :]).then_inc(scratch_done[o % 2], 16)

        def sp_load(sp, i, par, c, q, done):
            op = (qop, kop)[c]
            src = op_dram[c, bass.ds(i, 1), :, q * 512:(q + 1) * 512].rearrange("m (r h) n -> r (m h) n", h=HH)
            sp.dma_start(op[par][0:KR, q, :, :], src[:, par * QH:(par + 1) * QH, :]).then_inc(done, 16)

        def sp_load_upper(sp, i, par):
            sp_load(sp, i, par, 1, 1, op_in[par])
            sp_load(sp, i, par, 0, 1, op_in[par])

        def sp_load_lower(sp, i, par):
            sp_load(sp, i, par, 1, 0, op_in[par])
            sp_load(sp, i, par, 0, 0, ql_in[par])

        def block_of(v):
            return v % HEAVY // GT, GT * (QC - 1 - v // HEAVY) + v % GT

        def pe_max_block(pe, u, par, v):
            j, qt = block_of(v)
            pe.wait_ge(mx_done, MU * u + v + 1)
            dst = mid[:, 2 * (v % 2):2 * (v % 2) + 2, :]
            n = (qt + 1) * P
            for q in range(-(-n // 512)):
                w = min(512, n - q * 512)
                nc.tensor.matmul(dst[:, q, 0:w], qop[par][0:KM, qt // GT, j, (qt % GT) * P:(qt % GT + 1) * P],
                                 kop[par][0:KM, q, j, 0:w], start=True, stop=False, skip_group_check=True)
            nc.tensor.matmul(dst[:, qt // 4, (qt % 4) * P:(qt % 4 + 1) * P], ident[:], masks[:, 0, :],
                             start=False, stop=True, skip_group_check=True).then_inc(s_ready, 1)

        def dve_max_block(dve, u, v):
            qt = block_of(v)[1]
            dve.wait_ge(s_ready, MU * u + v + 1)
            flat = mid[:, 2 * (v % 2):2 * (v % 2) + 2, :].rearrange("p a b -> p (a b)")
            nc.vector.tensor_reduce(mxs[:, v:v + 1], flat[:, 0:(qt + 1) * P], AX.X, ALU.max).then_inc(mx_done, 1)

        def dve_max_end(dve, u, h):
            dve.wait_ge(mx_done, MU * u + (h + 1) * HEAVY + 2)
            if not isinstance(u, int) or u:
                dve.wait_ge(mt_ready, 2 * u - 1 + h)
            nc.vector.tensor_scalar(mneg[:, h, :], mxs[:, h * HEAVY:(h + 1) * HEAVY], -1.0, None,
                                    ALU.mult).then_inc(mneg_done, 1)

        def pe_max_end(pe, u, h):
            pe.wait_ge(mneg_done, 2 * u + h + 1)
            if h:
                pe.wait_ge(att_done, 2 * u + 1)
                pe.wait_ge(mT_done, 2 * u + 1)
            elif not isinstance(u, int) or u:
                pe.wait_ge(mT_done, 2 * u)
            nc.tensor.transpose(ybank[0:HEAVY, 1, 0:P // 2].bitcast(F16), mneg[:, h, :], ident[:]).then_inc(mt_ready, 1)

        def act_max_end(act, u, par, h):
            act.wait_ge(mt_ready, 2 * u + h + 1)
            nc.scalar.copy(mT[:, par, h, :], ybank[0:HEAVY, 1, 0:P // 2].bitcast(F16)).then_inc(mT_done, 1)

        def sp_max_row(sp, u, par, h):
            sp.wait_ge(mT_done, 2 * u + h + 1)
            sp.dma_start(qop[par][KM:KM + 1, QC - 1 - h, :, :].rearrange("p j c -> p (j c)"),
                         mT[:, par, h, :]).then_inc(m_in[par][h], 16)

        def pe_scores(pe, u, par, s, j):
            qc, kt = STEPS[s]
            c0 = span(s)
            e = QH * s + j
            pe.wait_ge(exp_done, QH * NS * u + e + 1)
            diag = kt >= 4 * qc
            last = nc.tensor.matmul(bank[e % 2][:, c0:512],
                                    kop[par][0:KM + 1, kt // GT, j, (kt % GT) * P:(kt % GT + 1) * P],
                                    qop[par][0:KM + 1, qc, j, c0:512], start=True, stop=not diag,
                                    skip_group_check=True)
            if diag:
                last = nc.tensor.matmul(bank[e % 2][:, c0:c0 + P], ident[:], masks[:, 1, :], start=False, stop=True,
                                        skip_group_check=True)
            last.then_inc(st_ready, 1)

        def act_exp(act, u, s):
            c0 = span(s)
            act.wait_ge(pv_done, NS * u + s + 1)
            for j in range(QH):
                e = QH * s + j
                act.wait_ge(st_ready, QH * NS * u + e + 1)
                nc.scalar.activation(prob_t[:, s % 2, j, c0:512], bank[e % 2][:, c0:512], ACT.Exp,
                                     scale=1 / SS).then_inc(exp_done, 1)

        def pe_values(pe, u, par, s):
            qc, kt = STEPS[s]
            c0 = span(s)
            pe.wait_ge(exp_done, QH * NS * u + QH * (s + 1) + 2)
            for j in range(QH):
                last = nc.tensor.matmul(ybank[32 * j:32 * j + VW, 0, c0:512],
                                        vq[:, par, kt, j * VW:(j + 1) * VW],
                                        prob_t[:, s % 2, j, c0:512], start=(kt == 0), stop=(kt == 4 * qc + 3),
                                        skip_group_check=True)
            last.then_inc(pv_done, 1)

        def act_out(act, u, i):
            act.wait_ge(pv_done, NS * u + (HALF, NS)[i] + 2)
            nc.scalar.copy(o32, ybank[:, 0, :]).then_inc(o32_done, 1)

        def pe_out(pe, u, i):
            pe.wait_ge(o32_done, 2 * u + i + 1)
            for t in range(GT):
                last = nc.tensor.transpose(ybank[:, 1, t * P:(t + 1) * P], o32[:, t * P:(t + 1) * P], ident32[:])
            last.then_inc(ot_ready, 1)

        def dve_out(dve, u, i):
            dve.wait_ge(ot_ready, 2 * u + i + 1)
            ot = ybank[:, 1, :].rearrange("p (t j c) -> p t j c", t=GT, j=QH)
            nc.vector.reciprocal(rec[:], ot[:, :, :, DH]).then_inc(rec_done, 1)
            dve.wait_ge(rec_done, 2 * u + i + 1)
            dst = att[:, bass.ds(u * TT + (QC - 1 - i) * GT, GT), :].rearrange("p t (j c) -> p t j c", j=QH)
            nc.vector.tensor_tensor(dst, ot[:, :, :, 0:DH], rec[:].unsqueeze(3).to_broadcast([P, GT, QH, DH]),
                                    ALU.mult).then_inc(att_done, 1)

        def pe_unit(pe, u, par, i, nxt=True, steps={}):
            pe.wait_ge(m_in[par][0], 16 * (i + 1))
            for s in range(NS):
                if s == HALF:
                    pe.wait_ge(m_in[par][1], 16 * (i + 1))
                for j in range(QH):
                    pe_scores(pe, u, par, s, j)
                    for v in M_SLOTS.get(QH * s + j, ()) if nxt else ():
                        if v == 0:
                            pe.wait_ge(op_in[1 - par], 48 * (i + par + 1))
                        if v == HEAVY:
                            pe.wait_ge(ql_in[1 - par], 16 * (i + par + 1))
                        pe_max_block(pe, u + 1, 1 - par, v)
                if s == 1:
                    pe_max_end(pe, u, 1)
                if s == HALF and nxt:
                    pe_max_end(pe, u + 1, 0)
                if s == HALF + 1:
                    pe.wait_ge(mT_done, 2 * u + (3 if nxt else 2))
                    pe_out(pe, u, 0)
                if s == 1:
                    pe.wait_ge(vq_done, u + 1)
                if s >= 1:
                    pe_values(pe, u, par, s - 1)
                for step in steps.get(s, ()):
                    step(pe)
            pe_values(pe, u, par, NS - 1)
            pe.wait_ge(att_done, 2 * u + 2)
            pe_out(pe, u, 1)

        def act_unit(act, u, par, nxt=True, steps={}):
            for s in range(NS):
                act_exp(act, u, s)
                for step in steps.get(s, ()):
                    step(act)
                if s == 1:
                    act_max_end(act, u, par, 1)
                if s == HALF:
                    if nxt:
                        act_max_end(act, u + 1, 1 - par, 0)
                    act_out(act, u, 0)
            act_out(act, u, 1)

        def dve_unit(dve, u):
            for v in range(HEAVY):
                dve_max_block(dve, u + 1, v)
            dve_max_end(dve, u + 1, 0)
            for v in range(HEAVY, M_OUT):
                dve_max_block(dve, u + 1, v)
            dve_out(dve, u, 0)
            for v in range(M_OUT, MU):
                dve_max_block(dve, u + 1, v)
            dve_max_end(dve, u + 1, 1)
            dve_out(dve, u, 1)

        def pe_att_high(pe, a):
            pe.wait_ge(ah_done, a + 1)
            if a:
                pe.wait_ge(aTh_done, a)
            for t in range(GT):
                for k in range(KD):
                    last = nc.tensor.transpose(ath_bank[:, k, t * P:(t + 1) * P], nh[:, t, k * P:(k + 1) * P], ident[:])
            last.then_inc(ath_ready, 1)

        def pe_att_low(pe, a):
            pe.wait_ge(al_done, a + 1)
            if a:
                pe.wait_ge(aTl_done, a)
            for t in range(GT):
                for k in range(KD):
                    last = nc.tensor.transpose(atl_bank[:, k, t * P:(t + 1) * P], nl[:, t, k * P:(k + 1) * P], ident[:])
            last.then_inc(atl_ready, 1)

        def pe_att_project(pe, a):
            pe.wait_ge(aTh_done, a + 1)
            pe.wait_ge(aTl_done, a + 1)
            pe.wait_ge(x_done, 17 + a)
            for t in range(GT):
                for j, (xs, ws) in enumerate(((aTh, wh), (aTh, wl), (aTl, wh))):
                    for k in range(KD):
                        last = nc.tensor.matmul(ya[a][:, t // 2, (t % 2) * D:(t % 2 + 1) * D], xs[:, k, t * P:(t + 1) * P],
                                                W(ws, O_AO + k * D, D), start=(j == 0 and k == 0),
                                                stop=(j == 2 and k == KD - 1))
            last.then_inc(y_ready, 1)

        def att_rows(b, j):
            return att[:, bass.ds(b * (H // QH) * TT, H // QH * TT), :].rearrange(
                "p (q t) c -> p t q c", t=TT)[:, j * GT:(j + 1) * GT, :, :]

        def quads(v):
            return v[:].rearrange("p t (q c) -> p t q c", c=QH * DH)

        def act_att_high(act, a):
            act.wait_ge(att_done, 2 * NQ // B * (a // 2 + 1) + 1)
            if a:
                act.wait_ge(al_done, a)
                act.wait_ge(ath_ready, a)
            for t in range(GT):
                last = nc.scalar.copy(quads(nh)[:, t], att_rows(a // 2, a % 2)[:, t])
            last.then_inc(ah_done, 1)

        def act_att_out(act, a):
            act.wait_ge(ath_ready, a + 1)
            if a:
                act.wait_ge(y_ready, 16 + a)
            nc.scalar.copy(aTh, ath_bank).then_inc(aTh_done, 1)

        def dve_att_low(dve, a):
            dve.wait_ge(ah_done, a + 1)
            if a:
                dve.wait_ge(atl_ready, a)
            nc.vector.tensor_tensor(quads(nl), att_rows(a // 2, a % 2), quads(nh), ALU.subtract).then_inc(al_done, 1)

        def dve_att_out(dve, a):
            dve.wait_ge(atl_ready, a + 1)
            if a:
                dve.wait_ge(y_ready, 16 + a)
            nc.vector.tensor_copy(aTl, atl_bank).then_inc(aTl_done, 1)

        def dve_att_sum(dve, a):
            dve.wait_ge(y_ready, 17 + a)
            if a:
                dve.wait_ge(x_done, 17 + a)
            for h in range(2):
                last = nc.vector.scalar_tensor_tensor(n32[:, 2 * h:2 * h + 2, :],
                                                      ya[a][:, h, :].rearrange("p (t d) -> p t d", t=2), 1 / WS,
                                                      row(R_BO, 2), ALU.mult, ALU.add)
            last.then_inc(ob_done, 1)
            dve.wait_ge(ob_done, a + 1)
            xs = x[:, tiles(a), :]
            nc.vector.tensor_tensor(xs, xs, n32[:], ALU.add).then_inc(x_done, 1)

        SPLIT = {4: 0, 8: 4, 12: 6, 16: 10, 20: 14}

        def moe_prepare(parts, at):
            return {at + c: [step] for c, step in parts.items()}

        def merged(*lists):
            out = {}
            for steps in lists:
                for c, todo in steps.items():
                    out.setdefault(c, []).extend(todo)
            return out

        def pe_next(n, ns):
            return {3: lambda e: pe_transpose_high(e, n), 5: lambda e: pe_transpose_low(e, n, ns)}

        def act_next(n, g):
            return {1: lambda e: act_round(e, n), 3: lambda e: act_high_out(e, n, g)}

        def dve_next(n, ns, g):
            return {0: lambda e: dve_moments(e, n, g), 1: lambda e: dve_scale(e, n, g),
                    2: lambda e: dve_low(e, n, ns), 5: lambda e: dve_low_out(e, ns, g)}

        def pool_next(n):
            return {0: lambda e: pool_root(e, n, ve, rstd, ve_done, rstd_done)}

        LAST_AT = [0, 4, 9]

        block = ctx.enter_context(nc.Block())

        @block.sync
        def _(sp):
            for j in range(RING):
                sp.dma_start(stage[:, j, :], w_in[:, j * WCH:(j + 1) * WCH]).then_inc(w_in_done[j], 16)
            sp.dma_start(rows[:], rows_in).then_inc(const_done, 16)
            sp.dma_start(sel[:], sel_in).then_inc(const_done, 16)
            sp.dma_start(order[:], order_in).then_inc(const_done, 16)
            sp.dma_start(masks[:], masks_in).then_inc(const_done, 16)
            with sp.Fori(1, NWG) as r:
                for j in range(RING):
                    sp.wait_ge(w_low, RING * r + j - (RING - 1))
                    sp.dma_start(stage[:, j, :], w_in[:, bass.ds((RING * r + j) * WCH, WCH)]).then_inc(w_in_done[j], 16)
            for c in range(2):
                sp.dma_start(op_dram[c, :, 0:4 * HH, :], alibi_in[c]).then_inc(pos_done, 16)
                sp.sem_inc(scratch_done[c], 48)
            sp.wait_ge(pos_done, 32)
            for b in range(B):
                for j in range(2):
                    sp_qkv(sp, 2 * b + j, b, j)
                if b == 0:
                    for par in range(2):
                        sp.wait_ge(scratch_done[par], 48 * (2 * NG // B + 1))
                    sp.wait_ge(fill_done, 2)
                    sp_load_upper(sp, 0, 0)
                    sp_load_lower(sp, 0, 0)
            for par in range(2):
                sp.wait_ge(scratch_done[par], 48 * (2 * NG + 1))
            sp_max_row(sp, 0, 0, 0)
            sp.wait_ge(fill_done, 4)
            sp_load_upper(sp, 0, 1)
            sp_load_lower(sp, 0, 1)
            sp_max_row(sp, 0, 0, 1)
            with sp.Fori(0, NQ // 2 - 1) as i:
                for par in range(2):
                    u = 2 * i + par
                    sp.wait_ge(st_ready, QH * (NS * u + HALF))
                    sp_load_upper(sp, i + 1, par)
                    sp_max_row(sp, u + 1, 1 - par, 0)
                    sp.wait_ge(st_ready, QH * NS * (u + 1))
                    sp_load_lower(sp, i + 1, par)
                    sp_max_row(sp, u + 1, 1 - par, 1)
            sp_max_row(sp, NQ - 1, 1, 0)
            sp_max_row(sp, NQ - 1, 1, 1)
            for g in range(NG):
                sp.wait_ge(x_done, 22 + g)
                sp.dma_start(out[g * GW:(g + 1) * GW, :].rearrange("(t p) d -> p t d", p=P),
                             x[:, g * GT:(g + 1) * GT, :]).then_inc(out_done, 16)
            sp.wait_ge(out_done, 16 * NG)

        @block.gpsimd
        def _(pool):
            nc.gpsimd.memset(mhalf[:], -0.5).then_inc(pool_set, 1)
            pool.wait_ge(pool_set, 1)
            with pool.Fori(0, 6) as n:
                pool_root(pool, n, ve, rstd, ve_done, rstd_done)
            with pool.Fori(0, B) as b:
                for j in range(2):
                    pool.wait_ge(zve_done, 2 * b + j + 1)
                    nc.gpsimd.tensor_tensor(zrstd[:, j, :], zve[:, j, :], mhalf[:], ALU.pow).then_inc(zrstd_done, 1)
                for j in range(2):
                    pool_root(pool, 6 + 2 * b + j, ve, rstd, ve_done, rstd_done)
            with pool.Fori(10, 13) as n:
                pool_root(pool, n, ve, rstd, ve_done, rstd_done)
            with pool.Fori(0, NG - 1) as g:
                pool_moe(pool, g, moe_prepare(pool_next(13 + g), 1))
            pool_moe(pool, NG - 1, merged(*[moe_prepare(pool_next(16 + k), at) for k, at in enumerate(LAST_AT)]))
            pool.wait_ge(x_done, 17)
            pool_root(pool, 19, ve, rstd, ve_done, rstd_done)
            nc.gpsimd.memset(kop[0], 1.0).then_inc(fill_done, 1)
            nc.gpsimd.memset(qop[0], 0.0).then_inc(fill_done, 1)

            def pool_values(i, par):
                nc.gpsimd.tensor_copy(vq[:, par, :, :],
                                      vals_by[:, bass.ds(i, 1), :, par * QH:(par + 1) * QH, :].rearrange(
                                          "p m t h c -> p (m t) (h c)")).then_inc(vq_done, 1)

            pool.wait_ge(v_ready, NG)
            nc.gpsimd.memset(kop[1], 1.0).then_inc(fill_done, 1)
            pool.wait_ge(v_done, NG + 1)
            pool.wait_ge(vones_done, 1)
            for par in range(2):
                pool_values(0, par)
            with pool.Fori(0, NQ // 2 - 1) as i:
                for par in range(2):
                    pool.wait_ge(pv_done, NS * (2 * i + par + 1) + 2)
                    pool_values(i + 1, par)
            pool_root(pool, 20, ve, rstd, ve_done, rstd_done)
            with pool.Fori(0, NG - 1) as g:
                pool_moe(pool, NG + g, moe_prepare(pool_next(21 + g), 1))
            pool_moe(pool, 2 * NG - 1, {})

        @block.tensor
        def _(pe):
            pe.sem_inc(pv_done, 2)
            pe.wait_ge(early_done, 2 * 16)
            pe_transpose_high(pe, 0)
            pe.wait_ge(w_low, 2)
            with pe.Fori(0, NG - 1) as g:
                pe_ffn(pe, g, g, g, {5: [lambda e: pe_transpose_high(e, g + 1)]})
            def pe_second_high(pe):
                pe.wait_ge(xTl_done, 1)
                pe_transpose_high(pe, 5)

            pe_ffn(pe, 3, 3, 3, {4: [lambda e: pe_transpose_high(e, 4)], 5: [lambda e: pe_transpose_low(e, 4, 0)],
                                 7: [pe_second_high]})
            pe_transpose_low(pe, 5, 1)
            with pe.Fori(0, B) as b:
                pe_wkv(pe, b)
            pe.wait_ge(xTl_done, SPLIT[12])
            with pe.Fori(0, 2) as g:
                pe_ffn(pe, 8 + g, 4 + g, g, {5: [lambda e: pe_transpose_high(e, 10 + g)]})
            pe_ffn(pe, 10, 6, 2, {5: [lambda e: pe_transpose_high(e, 12)],
                                  7: [lambda e: pe_transpose_low(e, 12, SPLIT[12])]})
            pe_ffn(pe, 11, 7, 3, {0: [lambda e: pe_router(e, SPLIT[12], 0)], 7: [lambda e: pe_transpose_routes(e, 0)]})
            pe.wait_ge(const_done, 4 * 16)

            def pe_moe_layer(n0, m0, last):
                s0 = SPLIT[n0]
                pe_moe_hidden(pe, n0, s0, m0, 0, 0)
                with pe.Fori(0, NG - 1) as g:
                    pe_moe(pe, n0 + g, s0 + g, m0 + g, g, merged(
                        moe_prepare(pe_next(n0 + g + 1, s0 + g + 1), 1),
                        {8: [lambda e: pe_router(e, s0 + g + 1, g + 1)],
                         13: [lambda e: pe_transpose_routes(e, m0 + g + 1)]}),
                        lambda e: e.wait_ge(cT_done, m0 + g + 2))
                pe_moe(pe, n0 + NG - 1, s0 + NG - 1, m0 + NG - 1, NG - 1, last,
                       (lambda e: e.wait_ge(xTl_done, SPLIT[16] + 3)) if last else None, nxt=False)

            pe_moe_layer(12, 0, merged(*[moe_prepare(pe_next(16 + k, SPLIT[16] + k), at)
                                         for k, at in enumerate(LAST_AT)]))
            pe.wait_ge(x_done, 17)
            pe_qkv(pe, 0)
            pe_transpose_high(pe, 19)
            pe_qkv(pe, 1)
            pe_transpose_low(pe, 19, SPLIT[16] + 3)
            pe.wait_ge(xTl_done, SPLIT[16] + 4)
            pe_qkv(pe, 2)
            pe_qkv(pe, 3)
            pe.wait_ge(v_done, NG + 1)
            pe_max_end(pe, 0, 0)
            pe.wait_ge(vones_done, 1)
            with pe.Fori(0, NQ // 2 - 1) as i:
                pe_unit(pe, 2 * i, 0, i)
                pe_unit(pe, 2 * i + 1, 1, i)
            pe_unit(pe, NQ - 2, 0, NQ // 2 - 1)
            pe_unit(pe, NQ - 1, 1, NQ // 2 - 1, nxt=False, steps={
                1: [lambda e: pe_att_high(e, 0)], 2: [lambda e: pe_att_low(e, 0)], 3: [lambda e: pe_att_project(e, 0)],
                5: [lambda e: pe_att_high(e, 1)], 6: [lambda e: pe_att_low(e, 1)], 7: [lambda e: pe_att_project(e, 1)]})
            pe_transpose_high(pe, 20)
            pe_transpose_low(pe, 20, SPLIT[20])
            pe_router(pe, SPLIT[20], 0)
            pe_att_high(pe, 2)
            pe_att_low(pe, 2)
            pe_att_project(pe, 2)
            pe_att_high(pe, 3)
            pe_att_low(pe, 3)
            pe_transpose_routes(pe, NG)
            pe_att_project(pe, 3)
            pe_moe_layer(20, NG, {})

        @block.scalar
        def _(act):
            def load_rows(g, done):
                act.dma_start(x[:, g * GT:(g + 1) * GT, :],
                              x_in[g * GW:(g + 1) * GW, :].rearrange("(t p) d -> p t d", p=P)).then_inc(done, 16)

            load_rows(0, x0_in_done)
            act.dma_start(ident[:], ident_in).then_inc(early_done, 16)
            act.dma_start(small[:], small_in).then_inc(early_done, 16)
            for g in range(1, NG):
                load_rows(g, x_in_done)
            act.sem_inc(exp_done, 2)
            act_weights(act, 0, 0)
            act_weights(act, 0, 1)
            act_round(act, 0)
            act_high_out(act, 0, 0)
            act_weights(act, 0, 2)
            act_weights(act, 0, 3)
            act.wait_ge(early_done, 2 * 16)

            def act_next_weights(r):
                return {c: [lambda e, j=j: act_weights(e, r, j)] for j, c in enumerate((0, 2, 4, 6))}

            with act.Fori(0, NG - 1) as g:
                act_ffn(act, g, merged(act_next_weights(g + 1), {
                    3: [lambda e: act_round(e, g + 1)], 6: [lambda e: act_high_out(e, g + 1, g + 1)]}))
            act.wait_ge(const_done, 4 * 16)
            nc.scalar.activation(eg, rows[:, R_G, :], ACT.Exp, scale=-1.0).then_inc(act_set, 1)
            nc.scalar.activation(decay[:], small[:, S_LW:S_LW + 1], ACT.Exp).then_inc(act_set, 1)
            nc.scalar.activation(nu[:], small[:, S_U:S_U + 1], ACT.Exp).then_inc(act_set, 1)
            nc.scalar.activation(bqs[:], small[:, S_BQ:S_BQ + KD], ACT.Copy,
                                 scale=SS / math.sqrt(DH)).then_inc(act_set, 1)
            nc.scalar.copy(ident32[:], ident[:]).then_inc(act_set, 1)
            act_ffn(act, 3, merged(act_next_weights(4), {
                2: [lambda e: act_round(e, 4)], 4: [lambda e: act_high_out(e, 4, 0)],
                5: [lambda e: act_round(e, 5)], 7: [lambda e: act_high_out(e, 5, 1)]}))
            act.wait_ge(set_done, 4)
            with act.Fori(0, B) as b:
                act_wkv(act, b)
            with act.Fori(0, 2) as g:
                act_ffn(act, g + 4, {3: [lambda e: act_round(e, g + 10)], 6: [lambda e: act_high_out(e, g + 10, g + 2)]})
            act_ffn(act, 6, {3: [lambda e: act_round(e, 12)], 6: [lambda e: act_high_out(e, 12, 0)]})
            act_ffn(act, 7, {3: [lambda e: act_exp_routes(e, 0)], 7: [lambda e: act_routes_out(e, 0, 0)]})

            def act_moe_layer(n0, m0, last):
                with act.Fori(0, NG - 1) as g:
                    act_moe(act, m0 + g, merged(
                        moe_prepare(act_next(n0 + g + 1, g + 1), 1),
                        {8: [lambda e: act_exp_routes(e, m0 + g + 1)],
                         14: [lambda e: act_routes_out(e, m0 + g + 1, g + 1)]}))
                act_moe(act, m0 + NG - 1, last)

            act_moe_layer(12, 0, merged(*[moe_prepare(act_next(16 + k, k), at) for k, at in enumerate(LAST_AT)]))
            act_qkv(act, 0)
            act_round(act, 19)
            act_high_out(act, 19, 3)
            for a in range(1, NG):
                act_qkv(act, a)
            act_max_end(act, 0, 0, 0)
            with act.Fori(0, NQ // 2 - 1) as i:
                act_unit(act, 2 * i, 0)
                act_unit(act, 2 * i + 1, 1)
            act_unit(act, NQ - 2, 0)
            act_att_high(act, 0)
            act_unit(act, NQ - 1, 1, nxt=False, steps={
                1: [lambda e: act_att_out(e, 0)], 3: [lambda e: act_att_high(e, 1)], 5: [lambda e: act_att_out(e, 1)],
                10: [lambda e: act_round(e, 20)]})
            act_high_out(act, 20, 0)
            act.wait_ge(nl_done, SPLIT[20] + 1)
            act_att_high(act, 2)
            act_att_out(act, 2)
            act_exp_routes(act, NG)
            act_att_high(act, 3)
            act_att_out(act, 3)
            act_routes_out(act, NG, 0)
            act_moe_layer(20, NG, {})

        @block.vector
        def _(dve):
            nc.vector.memset(decayw[:], 1.0).then_inc(set_done, 1)
            dve.sem_inc(x_done, 1)
            dve.sem_inc(mx_done, 2)
            dve.sem_inc(pl_done, 2)
            dve.sem_inc(v_done, 1)
            dve.sem_inc(att_done, 1)
            dve.wait_ge(x0_in_done, 16)
            dve_normalise(dve, 0, 0, first=True)
            for j in range(RING):
                dve_weights(dve, 0, j)
            dve.wait_ge(x_in_done, 16 * (NG - 1))
            dve.wait_ge(const_done, 4 * 16)
            with dve.Fori(0, NG - 1) as g:
                dve_moments(dve, g + 1, g + 1, first=True)
                dve_weights(dve, g + 1, 0)
                dve_scale(dve, g + 1, g + 1)
                for j in range(1, RING):
                    dve_weights(dve, g + 1, j)
                dve_ffn_sum(dve, g, g, g)
            dve.wait_ge(act_set, 5)
            nc.vector.tensor_scalar(gsc[:], eg, 1.0, None, ALU.add).then_inc(set_done, 1)
            dve.wait_ge(set_done, 2)
            nc.vector.tensor_scalar(decayw[:], decayw[:], decay[:], None, ALU.mult).then_inc(set_done, 1)
            nc.vector.tensor_scalar(nu[:], nu[:], -1.0, None, ALU.mult).then_inc(set_done, 1)
            nc.vector.reciprocal(gsc[:], gsc[:]).then_inc(set_done, 1)
            dve.wait_ge(set_done, 5)
            nc.vector.tensor_scalar(omg[:], gsc[:], -1.0, 1.0, ALU.mult, ALU.add).then_inc(set_done, 1)
            dve.wait_ge(set_done, 6)
            nc.vector.tensor_scalar(gsc[:], gsc[:], 1 / WS, None, ALU.mult).then_inc(set_done, 1)
            dve.wait_ge(set_done, 7)
            dve_moments(dve, 4, 0)
            dve_weights(dve, 4, 0)
            dve_scale(dve, 4, 0)
            dve_weights(dve, 4, 1)
            dve_moments(dve, 5, 1)
            dve_low(dve, 4, 0)
            dve_skip(dve, 4, 0)
            dve_scale(dve, 5, 1, skipped=1)
            dve_weights(dve, 4, 2)
            dve_low_out(dve, 0, 0)
            dve_weights(dve, 4, 3)
            dve_skip(dve, 5, 1)
            dve_low(dve, 5, 1)
            dve_ffn_sum(dve, 3, 3, 3)
            dve_low_out(dve, 1, 1)
            with dve.Fori(0, B) as b:
                dve_wkv(dve, b)
            dve.wait_ge(R_done, 6)
            with dve.Fori(0, 2) as g:
                dve_normalise(dve, g + 10, g + 2)
                dve_ffn_sum(dve, 8 + g, 4 + g, g)
            dve_normalise(dve, 12, 0)
            dve_low(dve, 12, SPLIT[12])
            dve_low_out(dve, SPLIT[12], 0)
            dve_ffn_sum(dve, 10, 6, 2)
            dve_routes(dve, 0)
            dve_ffn_sum(dve, 11, 7, 3)

            def dve_moe_layer(n0, m0, last):
                s0 = SPLIT[n0]
                with dve.Fori(0, NG - 1) as g:
                    dve_moe(dve, m0 + g, merged(
                        moe_prepare(dve_next(n0 + g + 1, s0 + g + 1, g + 1), 1),
                        {8: [lambda e: dve_routes_logits(e, m0 + g + 1)], 9: [lambda e: dve_routes_first(e, m0 + g + 1)],
                         10: [lambda e: dve_routes_second(e, m0 + g + 1)],
                         11: [lambda e: dve_routes_split(e, m0 + g + 1)]}))
                    dve_sum(dve, n0 + g, g, 0.5 / (WS * US))
                dve_moe(dve, m0 + NG - 1, last)
                dve_sum(dve, n0 + NG - 1, NG - 1, 0.5 / (WS * US))

            dve_moe_layer(12, 0, merged(*[moe_prepare(dve_next(16 + k, SPLIT[16] + k, k), at)
                                          for k, at in enumerate(LAST_AT)]))
            dve_normalise(dve, 19, 3)
            nc.vector.memset(vals.rearrange("p (r c) -> p r c", c=VW)[:, :, DH:VW], 1.0).then_inc(vones_done, 1)
            dve_qkv(dve, 0)
            dve_low(dve, 19, SPLIT[16] + 3)
            dve_qkv(dve, 1)
            dve_low_out(dve, SPLIT[16] + 3, 3)
            dve_qkv(dve, 2)
            dve_qkv(dve, 3)
            dve_max_end(dve, 0, 0)
            nc.vector.memset(qop[1], 0.0).then_inc(fill_done, 1)
            dve_max_end(dve, 0, 1)
            with dve.Fori(0, NQ // 2 - 1) as i:
                dve_unit(dve, 2 * i)
                dve_unit(dve, 2 * i + 1)
            dve_unit(dve, NQ - 2)
            for a in range(2):
                dve_att_low(dve, a)
                dve_att_out(dve, a)
                dve_att_sum(dve, a)
            dve.wait_ge(x_done, 19)
            dve_normalise(dve, 20, 0)
            dve_out(dve, NQ - 1, 0)
            dve.wait_ge(atl_ready, 2)
            dve_low(dve, 20, SPLIT[20])
            dve_out(dve, NQ - 1, 1)
            dve_low_out(dve, SPLIT[20], 0)
            dve_att_low(dve, 2)
            dve_att_out(dve, 2)
            dve_routes(dve, NG)
            dve_att_sum(dve, 2)
            dve_att_low(dve, 3)
            dve_att_out(dve, 3)
            dve_att_sum(dve, 3)
            dve_moe_layer(20, NG, {})


def packed(i):
    def cols(w, chunks):
        return w.reshape(chunks, P, -1).transpose(1, 0, 2).reshape(P, -1)

    by_dim = np.arange(D).reshape(2, HH, DH).transpose(0, 2, 1).reshape(D)
    def hidden(experts, shared):
        by_chunk = experts.reshape(NE, EC, P // NE, D).transpose(1, 0, 2, 3).reshape(NE * FE, D)
        return np.concatenate([by_chunk, shared], 0)

    fc1 = hidden(i["L1_ffn_expert_fc1"], i["L1_ffn_shared_fc1"]).T
    fc2 = hidden(i["L1_ffn_expert_fc2"], i["L1_ffn_shared_fc2"]).T
    both = np.concatenate([fc1[:, FB:], fc2[:, FB:]], 1)
    proj = np.zeros((MC * P, D), np.float32)
    proj[0:FM] = hidden(i["L1_ffn_expert_proj"].transpose(0, 2, 1), i["L1_ffn_shared_proj"].T)
    proj[MC * P - ML:] = proj[FB:FM].copy()
    w = np.zeros((P, WCOLS), np.float32)
    for at, part in ((O_W0, cols(i["L0_ffn_W0"].T, KD)), (O_W1, cols(i["L0_ffn_W1"].T, FC)),
                     (O_SH, cols(i["L0_attn_W_shift"].T, KD)), (O_WK, cols(i["L0_attn_W_key"].T, KD)),
                     (O_WV, cols(i["L0_attn_W_value"].T, KD)),
                     (O_RT, cols(np.concatenate([i["L1_ffn_gate_w"], i["L1_ffn_shared_gate_w"]], 0).T, KD)),
                     (O_F1, cols(fc1[:, :FB], KD)), (O_F2, cols(fc2[:, :FB], KD)), (O_FL, cols(both, KD)), (O_PR, cols(proj, MC)),
                     (O_AQ, cols(i["L1_attn_Wq"][by_dim].T, KD)),
                     (O_AK, cols(i["L1_attn_Wk"][by_dim].T, KD)),
                     (O_AV, cols(i["L1_attn_Wv"].T, KD)), (O_AO, cols(i["L1_attn_Wo"].T, KD))):
        w[:, at:at + part.shape[1]] = part
    w[:, O_WO:O_WO + D] = np.tile(i["L0_attn_W_output"].T, (2, 1))
    small = np.zeros((P, SCOLS), np.float32)
    small[:, S_B0:S_B0 + FC] = i["L0_ffn_bias0"].reshape(FC, P).T
    small[:, S_LW] = np.tile(i["L0_attn_time_decay"], 2)
    small[:, S_U] = np.tile(i["L0_attn_time_first"], 2)
    small[:, S_BQ:S_BQ + KD] = i["L1_attn_bq"][by_dim].reshape(KD, P).T
    small[:, S_BK:S_BK + KD] = i["L1_attn_bk"][by_dim].reshape(KD, P).T
    rows = np.stack([i["L0_ffn_bias1"], i["L0_attn_gate"], i["L0_attn_ln_gamma"], i["L0_attn_ln_beta"],
                     i["L1_attn_bv"], i["L1_attn_bo"]])
    rows = np.broadcast_to(rows, (P,) + rows.shape)
    ident = np.eye(P, dtype=np.float16)
    sel = np.zeros((2 * NR, 2, P), np.float16)
    for e in range(NE):
        sel[[e, NR + e], 0, e * P // NE:(e + 1) * P // NE] = SEL
    sel[[NE, NR + NE], 1, :] = SEL
    order = np.broadcast_to(np.arange(NE, 0, -1, dtype=np.float32), (P, NE))
    upper = np.triu(np.full((P, P), MASK, np.float16), 1)
    masks = np.stack([upper, upper.T], 1)
    slopes = np.array([2.0 ** (-0.5 * (h + 1)) for h in range(H)], np.float32)
    scaled = np.tile(slopes, B).astype(np.float64) * SS
    high = scaled.astype(np.float16)
    low = ((scaled - high) * T).astype(np.float16)
    pos = np.arange(T)
    alibi = np.zeros((2, 4, B * H, T), np.float16)
    alibi[0, 0], alibi[0, 2] = high[:, None], low[:, None]
    alibi[0, 1], alibi[0, 3] = -pos, -pos / T
    alibi[1, 0], alibi[1, 2] = pos, pos / T
    alibi[1, 1], alibi[1, 3] = high[:, None], low[:, None]
    alibi = alibi.reshape(2, 4, 2 * B, HH, T).transpose(0, 2, 1, 3, 4).reshape(2, 2 * B, 4 * HH, T)
    return {"x": i["L0_attn_x"].reshape(B * T, D), "w": w, "small": small, "rows": rows, "ident": ident, "sel": sel,
            "order": order, "masks": masks, "alibi": alibi}


def kernel(**inputs):
    import concourse.bacc as bacc
    from concourse.bass_utils import run_bass_kernel_spmd

    nc = bacc.Bacc("TRN2", target_bir_lowering=False, num_devices=1)
    arrays = {f"in_{k}": np.ascontiguousarray(v) for k, v in packed(inputs).items()}
    args = [nc.dram_tensor(k, a.shape, mybir.dt.from_np(a.dtype), kind="ExternalInput").ap() for k, a in arrays.items()]
    out = nc.dram_tensor("out_x", (B * T, D), F32, kind="ExternalOutput").ap()
    block_kernel(nc, *args, out)
    r = run_bass_kernel_spmd(nc, [arrays], core_ids=[0])
    return r.results[0]["out_x"].reshape(B, T, D)
```
